# Optimizing a Trainium2 kernel written in Bass

```python
import numpy as np
import jax
import jax.numpy as jnp

def _softmax(x, axis=-1):
    return jax.nn.softmax(x, axis=axis)

def _gelu(x):
    return jax.nn.gelu(x, approximate=True)

def _silu(x):
    return jax.nn.silu(x)

def _sigmoid(x):
    return jax.nn.sigmoid(x)

def _layernorm(x, axis=-1, eps=1e-05):
    m = jnp.mean(x, axis=axis, keepdims=True)
    v = jnp.var(x, axis=axis, keepdims=True)
    return (x - m) / jnp.sqrt(v + eps)

def _scatter_add(tgt, idx, src, axis=0):
    return tgt.at[idx].add(src)

def _segment_sum(src, seg, n):
    return jax.ops.segment_sum(src, seg, n)
kernel_name = 'mk_early_fusion_d2_tok_img512_r4_ce42ab'

def setup_inputs(seed: int=0):
    np.random.seed(seed)
    _w = jnp.asarray

    def _rec_inputs():
        import jax
        import jax.numpy as jnp
        _rk = jax.random.key(seed)
        x = -0.000392918 + 0.999932 * jax.random.normal(jax.random.fold_in(_rk, 1), (8, 1, 128, 128), jnp.float32)
        txt = 0.229487 + 0.681011 * jax.random.normal(jax.random.fold_in(_rk, 2), (8, 128, 128), jnp.float32)
        return (x, txt)
    x, txt = _rec_inputs()

    def _L0_tok_setup():
        import math
        import jax, jax.numpy as jnp
        import numpy as np
        PW = PH = 16
        EMB = 128
        HID = 128
        B, H, W = (64, 128, 128)
        L = H // PW * (W // PH)
        SIGMA_ZERO = 0.1

        def _f_noise(x):
            return jnp.sign(x) * jnp.sqrt(jnp.abs(x))

        def _noisy_linear(x, w, b, sw, sb, eps_in, eps_out):
            ei = _f_noise(eps_in)
            eo = _f_noise(eps_out)
            w_n = w + sw * (eo[:, None] * ei[None, :])
            b_n = b + sb * eo
            return x @ w_n.T + b_n

        def _unfold_patches(x):
            b = x.shape[0]
            p = x.reshape(b, H // PW, PW, W // PH, PH)
            p = p.transpose(0, 1, 3, 2, 4)
            return p.reshape(b, L, PW * PH)

        def _pos_encoding(x):
            pos = jnp.arange(L, dtype=jnp.float32)[:, None]
            div = jnp.exp(jnp.arange(0, EMB, 2, dtype=jnp.float32) * (-math.log(10000.0) / EMB))
            ang = pos * div
            pe = jnp.stack([jnp.sin(ang), jnp.cos(ang)], axis=-1).reshape(L, EMB)
            return x + pe[None, :, :]
        key = jax.random.key(seed)
        ks = jax.random.split(key, 12)
        in_f = PW * PH
        sig = SIGMA_ZERO / math.sqrt(in_f)
        bnd1 = 1.0 / math.sqrt(in_f)
        bnd3 = 1.0 / math.sqrt(HID)
        u = lambda k, shape, bnd: jax.random.uniform(k, shape, jnp.float32, -bnd, bnd)
        return {'inputs': jax.random.normal(ks[0], (B, 1, H, W), jnp.float32), 'W1_w': u(ks[1], (HID, in_f), bnd1), 'W1_b': u(ks[2], (HID,), bnd1), 'W1_sw': jnp.full((HID, in_f), sig, jnp.float32), 'W1_sb': jnp.full((HID,), sig, jnp.float32), 'W2_w': u(ks[3], (HID, in_f), bnd1), 'W2_b': u(ks[4], (HID,), bnd1), 'W2_sw': jnp.full((HID, in_f), sig, jnp.float32), 'W2_sb': jnp.full((HID,), sig, jnp.float32), 'W3_w': u(ks[5], (EMB, HID), bnd3), 'W3_b': u(ks[6], (EMB,), bnd3), 'eps_in1': jax.random.normal(ks[7], (in_f,), jnp.float32), 'eps_out1': jax.random.normal(ks[8], (HID,), jnp.float32), 'eps_in2': jax.random.normal(ks[9], (in_f,), jnp.float32), 'eps_out2': jax.random.normal(ks[10], (HID,), jnp.float32)}
    _L0_tok_all = _L0_tok_setup()
    _L0_tok_in = {k: v for k, v in _L0_tok_all.items() if k in ('W1_w', 'W1_b', 'W1_sw', 'W1_sb', 'W2_w', 'W2_b', 'W2_sw', 'W2_sb', 'W3_w', 'W3_b', 'eps_in1', 'eps_out1', 'eps_in2', 'eps_out2')}
    del _L0_tok_all

    def _L0_attn_setup():
        import jax, jax.numpy as jnp
        import numpy as np
        DIM = 128
        B, T = (32, 512)

        def _lstm(x, W_ih, W_hh, b_ih, b_hh):
            Bb, Tt, D = x.shape
            xg = jnp.einsum('btd,gd->btg', x, W_ih) + b_ih + b_hh
            xg = jnp.swapaxes(xg, 0, 1)

            def step(carry, xt):
                h, c = carry
                gates = xt + h @ W_hh.T
                i, f, g, o = jnp.split(gates, 4, axis=-1)
                i = jax.nn.sigmoid(i)
                f = jax.nn.sigmoid(f)
                g = jnp.tanh(g)
                o = jax.nn.sigmoid(o)
                c = f * c + i * g
                h = o * jnp.tanh(c)
                return ((h, c), h)
            h0 = jnp.zeros((Bb, D), dtype=x.dtype)
            (_, _), hs = jax.lax.scan(step, (h0, h0), xg)
            return jnp.swapaxes(hs, 0, 1)
        key = jax.random.key(seed)
        k_x, k_wih, k_whh, k_bih, k_bhh = jax.random.split(key, 5)
        s = 1.0 / np.sqrt(DIM)
        return {'x': jax.random.normal(k_x, (B, T, DIM), dtype=jnp.float32), 'W_ih': jax.random.uniform(k_wih, (4 * DIM, DIM), minval=-s, maxval=s, dtype=jnp.float32), 'W_hh': jax.random.uniform(k_whh, (4 * DIM, DIM), minval=-s, maxval=s, dtype=jnp.float32), 'b_ih': jax.random.uniform(k_bih, (4 * DIM,), minval=-s, maxval=s, dtype=jnp.float32), 'b_hh': jax.random.uniform(k_bhh, (4 * DIM,), minval=-s, maxval=s, dtype=jnp.float32)}
    _L0_attn_all = _L0_attn_setup()
    _L0_attn_in = {k: v for k, v in _L0_attn_all.items() if k in ('W_ih', 'W_hh', 'b_ih', 'b_hh')}
    del _L0_attn_all

    def _L0_ffn_setup():
        import jax, jax.numpy as jnp
        import numpy as np
        B, S, D = (32, 128, 128)
        E, H, O, K = (8, 512, 128, 2)
        key = jax.random.key(seed)
        ks = jax.random.split(key, 5)
        sc = lambda k, shape, scale: jax.random.normal(k, shape, jnp.float32) * scale
        return {'x': sc(ks[0], (B, S, D), 1.0), 'attn_w': sc(ks[1], (D, 1), 0.05), 'attn_b': jnp.zeros((1,), jnp.float32), 'gate_w': sc(ks[2], (D, E), 0.05), 'gate_b': jnp.zeros((E,), jnp.float32), 'w1': sc(ks[3], (E, D, H), 0.02), 'b1': jnp.zeros((E, H), jnp.float32), 'w2': sc(ks[4], (E, H, O), 0.02), 'b2': jnp.zeros((E, O), jnp.float32)}
    _L0_ffn_all = _L0_ffn_setup()
    _L0_ffn_in = {k: v for k, v in _L0_ffn_all.items() if k in ('attn_w', 'attn_b', 'gate_w', 'gate_b', 'w1', 'b1', 'w2', 'b2')}
    del _L0_ffn_all

    def _L1_attn_setup():
        import jax, jax.numpy as jnp
        import numpy as np
        NUM_HEADS = 8
        TOP_K = 32
        key = jax.random.key(seed)
        k1, k2, k3 = jax.random.split(key, 3)
        B, N, D, E = (4, 512, 128, 128)
        x = jax.random.normal(k1, (B, N, D), dtype=jnp.float32)
        W_qkv = jax.random.normal(k2, (3 * E, D), dtype=jnp.float32) * 0.02
        W_o = jax.random.normal(k3, (E, E), dtype=jnp.float32) * 0.02
        return {'x': x, 'W_qkv': W_qkv, 'W_o': W_o}
    _L1_attn_all = _L1_attn_setup()
    _L1_attn_in = {k: v for k, v in _L1_attn_all.items() if k in ('W_qkv', 'W_o')}
    del _L1_attn_all

    def _L1_ffn_setup():
        import jax, jax.numpy as jnp
        import numpy as np
        B, S, D = (8, 1024, 128)
        H = 512
        O = 128
        E = 8
        TOP_K = 1
        key = jax.random.key(seed)
        ks = jax.random.split(key, 8)
        sc = 0.02
        return {'x': jax.random.normal(ks[0], (B, S, D), dtype=jnp.float32), 'Wr': jax.random.normal(ks[1], (D, E), dtype=jnp.float32) * sc, 'br': jnp.zeros((E,), dtype=jnp.float32), 'W1': jax.random.normal(ks[2], (E, D, H), dtype=jnp.float32) * sc, 'b1': jnp.zeros((E, H), dtype=jnp.float32), 'W2': jax.random.normal(ks[3], (E, H, O), dtype=jnp.float32) * sc, 'b2': jnp.zeros((E, O), dtype=jnp.float32)}
    _L1_ffn_all = _L1_ffn_setup()
    _L1_ffn_in = {k: v for k, v in _L1_ffn_all.items() if k in ('Wr', 'br', 'W1', 'b1', 'W2', 'b2')}
    del _L1_ffn_all
    return {'x': x, 'txt': txt, 'L0_tok_W1_w': _L0_tok_in['W1_w'], 'L0_tok_W1_b': _L0_tok_in['W1_b'], 'L0_tok_W1_sw': _L0_tok_in['W1_sw'], 'L0_tok_W1_sb': _L0_tok_in['W1_sb'], 'L0_tok_W2_w': _L0_tok_in['W2_w'], 'L0_tok_W2_b': _L0_tok_in['W2_b'], 'L0_tok_W2_sw': _L0_tok_in['W2_sw'], 'L0_tok_W2_sb': _L0_tok_in['W2_sb'], 'L0_tok_W3_w': _L0_tok_in['W3_w'], 'L0_tok_W3_b': _L0_tok_in['W3_b'], 'L0_tok_eps_in1': _L0_tok_in['eps_in1'], 'L0_tok_eps_out1': _L0_tok_in['eps_out1'], 'L0_tok_eps_in2': _L0_tok_in['eps_in2'], 'L0_tok_eps_out2': _L0_tok_in['eps_out2'], 'L0_attn_W_ih': _L0_attn_in['W_ih'], 'L0_attn_W_hh': _L0_attn_in['W_hh'], 'L0_attn_b_ih': _L0_attn_in['b_ih'], 'L0_attn_b_hh': _L0_attn_in['b_hh'], 'L0_ffn_attn_w': _L0_ffn_in['attn_w'], 'L0_ffn_attn_b': _L0_ffn_in['attn_b'], 'L0_ffn_gate_w': _L0_ffn_in['gate_w'], 'L0_ffn_gate_b': _L0_ffn_in['gate_b'], 'L0_ffn_w1': _L0_ffn_in['w1'], 'L0_ffn_b1': _L0_ffn_in['b1'], 'L0_ffn_w2': _L0_ffn_in['w2'], 'L0_ffn_b2': _L0_ffn_in['b2'], 'L1_attn_W_qkv': _L1_attn_in['W_qkv'], 'L1_attn_W_o': _L1_attn_in['W_o'], 'L1_ffn_Wr': _L1_ffn_in['Wr'], 'L1_ffn_br': _L1_ffn_in['br'], 'L1_ffn_W1': _L1_ffn_in['W1'], 'L1_ffn_b1': _L1_ffn_in['b1'], 'L1_ffn_W2': _L1_ffn_in['W2'], 'L1_ffn_b2': _L1_ffn_in['b2']}

def reference(x, txt, L0_tok_W1_w, L0_tok_W1_b, L0_tok_W1_sw, L0_tok_W1_sb, L0_tok_W2_w, L0_tok_W2_b, L0_tok_W2_sw, L0_tok_W2_sb, L0_tok_W3_w, L0_tok_W3_b, L0_tok_eps_in1, L0_tok_eps_out1, L0_tok_eps_in2, L0_tok_eps_out2, L0_attn_W_ih, L0_attn_W_hh, L0_attn_b_ih, L0_attn_b_hh, L0_ffn_attn_w, L0_ffn_attn_b, L0_ffn_gate_w, L0_ffn_gate_b, L0_ffn_w1, L0_ffn_b1, L0_ffn_w2, L0_ffn_b2, L1_attn_W_qkv, L1_attn_W_o, L1_ffn_Wr, L1_ffn_br, L1_ffn_W1, L1_ffn_b1, L1_ffn_W2, L1_ffn_b2):
    import jax
    import jax.numpy as jnp

    def _L0_tok_ref(inputs, W1_w, W1_b, W1_sw, W1_sb, W2_w, W2_b, W2_sw, W2_sb, W3_w, W3_b, eps_in1, eps_out1, eps_in2, eps_out2):
        import math
        import jax, jax.numpy as jnp
        import numpy as np
        PW = PH = 16
        EMB = 128
        HID = 128
        B, H, W = (64, 128, 128)
        L = H // PW * (W // PH)
        SIGMA_ZERO = 0.1

        def _f_noise(x):
            return jnp.sign(x) * jnp.sqrt(jnp.abs(x))

        def _noisy_linear(x, w, b, sw, sb, eps_in, eps_out):
            ei = _f_noise(eps_in)
            eo = _f_noise(eps_out)
            w_n = w + sw * (eo[:, None] * ei[None, :])
            b_n = b + sb * eo
            return x @ w_n.T + b_n

        def _unfold_patches(x):
            b = x.shape[0]
            p = x.reshape(b, H // PW, PW, W // PH, PH)
            p = p.transpose(0, 1, 3, 2, 4)
            return p.reshape(b, L, PW * PH)

        def _pos_encoding(x):
            pos = jnp.arange(L, dtype=jnp.float32)[:, None]
            div = jnp.exp(jnp.arange(0, EMB, 2, dtype=jnp.float32) * (-math.log(10000.0) / EMB))
            ang = pos * div
            pe = jnp.stack([jnp.sin(ang), jnp.cos(ang)], axis=-1).reshape(L, EMB)
            return x + pe[None, :, :]
        x = _unfold_patches(inputs)
        g = _noisy_linear(x, W1_w, W1_b, W1_sw, W1_sb, eps_in1, eps_out1)
        x_gate = g * jnp.tanh(jax.nn.softplus(g))
        x_inner = _noisy_linear(x, W2_w, W2_b, W2_sw, W2_sb, eps_in2, eps_out2)
        x = x_gate * x_inner
        x = x @ W3_w.T + W3_b
        return _pos_encoding(x)

    def _L0_attn_ref(x, W_ih, W_hh, b_ih, b_hh):
        import jax, jax.numpy as jnp
        import numpy as np
        DIM = 128
        B, T = (32, 512)

        def _lstm(x, W_ih, W_hh, b_ih, b_hh):
            Bb, Tt, D = x.shape
            xg = jnp.einsum('btd,gd->btg', x, W_ih) + b_ih + b_hh
            xg = jnp.swapaxes(xg, 0, 1)

            def step(carry, xt):
                h, c = carry
                gates = xt + h @ W_hh.T
                i, f, g, o = jnp.split(gates, 4, axis=-1)
                i = jax.nn.sigmoid(i)
                f = jax.nn.sigmoid(f)
                g = jnp.tanh(g)
                o = jax.nn.sigmoid(o)
                c = f * c + i * g
                h = o * jnp.tanh(c)
                return ((h, c), h)
            h0 = jnp.zeros((Bb, D), dtype=x.dtype)
            (_, _), hs = jax.lax.scan(step, (h0, h0), xg)
            return jnp.swapaxes(hs, 0, 1)
        return _lstm(x, W_ih, W_hh, b_ih, b_hh)

    def _L0_ffn_ref(x, attn_w, attn_b, gate_w, gate_b, w1, b1, w2, b2):
        import jax, jax.numpy as jnp
        import numpy as np
        B, S, D = (32, 128, 128)
        E, H, O, K = (8, 512, 128, 2)
        scores = x @ attn_w + attn_b
        aw = jax.nn.softmax(scores, axis=1)
        pooled = jnp.sum(x * aw, axis=1)
        gates = jax.nn.softmax(pooled @ gate_w + gate_b, axis=-1)
        _, idx = jax.lax.top_k(gates, K)
        mask = jnp.sum(jax.nn.one_hot(idx, E, dtype=gates.dtype), axis=-2)
        g = gates * mask
        g = g / (jnp.sum(g, axis=-1, keepdims=True) + 1e-09)
        h = jax.nn.gelu(jnp.einsum('bsd,edh->ebsh', x, w1) + b1[:, None, None, :], approximate=False)
        eo = jax.nn.gelu(jnp.einsum('ebsh,eho->ebso', h, w2) + b2[:, None, None, :], approximate=False)
        return jnp.einsum('ebso,be->bso', eo, g)

    def _L1_attn_ref(x, W_qkv, W_o):
        import jax, jax.numpy as jnp
        import numpy as np
        NUM_HEADS = 8
        TOP_K = 32
        B, N, _ = x.shape
        E = W_o.shape[0]
        hd = E // NUM_HEADS
        qkv = x @ W_qkv.T
        qkv = qkv.reshape(B, N, NUM_HEADS, 3 * hd).transpose(0, 2, 1, 3)
        Q, K, V = jnp.split(qkv, 3, axis=-1)
        S = jnp.einsum('bhqd,bhkd->bhqk', Q, K) / jnp.sqrt(jnp.float32(hd))
        A = jax.nn.softmax(S, axis=-1)
        vals, idx = jax.lax.top_k(A, TOP_K)
        bi = jnp.arange(B)[:, None, None, None]
        hi = jnp.arange(NUM_HEADS)[None, :, None, None]
        qi = jnp.arange(N)[None, None, :, None]
        tkA = jnp.zeros_like(A).at[bi, hi, qi, idx].set(vals)
        Hd = jnp.einsum('bhqk,bhkd->bhqd', tkA, V)
        values = Hd.transpose(0, 2, 1, 3).reshape(B, N, E)
        return values @ W_o.T

    def _L1_ffn_ref(x, Wr, br, W1, b1, W2, b2):
        import jax, jax.numpy as jnp
        import numpy as np
        B, S, D = (8, 1024, 128)
        H = 512
        O = 128
        E = 8
        TOP_K = 1
        b, s, d = x.shape
        xf = x.reshape(-1, d)
        router_logits = xf @ Wr + br
        topk_logits, topk_idx = jax.lax.top_k(router_logits, TOP_K)
        topk_gates = jax.nn.softmax(topk_logits, axis=1)
        out = jnp.zeros((xf.shape[0], O), dtype=x.dtype)
        for k in range(TOP_K):
            idx_k = topk_idx[:, k]
            gate_k = topk_gates[:, k:k + 1]
            for e in range(E):
                h = jax.nn.relu(xf @ W1[e] + b1[e])
                oe = h @ W2[e] + b2[e]
                mask = (idx_k == e)[:, None]
                out = out + jnp.where(mask, gate_k * oe, 0.0)
        return out.reshape(b, s, O)
    h = _L0_tok_ref(x, L0_tok_W1_w, L0_tok_W1_b, L0_tok_W1_sw, L0_tok_W1_sb, L0_tok_W2_w, L0_tok_W2_b, L0_tok_W2_sw, L0_tok_W2_sb, L0_tok_W3_w, L0_tok_W3_b, L0_tok_eps_in1, L0_tok_eps_out1, L0_tok_eps_in2, L0_tok_eps_out2)
    h = jnp.concatenate([h, txt], axis=1)
    h = h + _L0_attn_ref(_layernorm(h, axis=-1), L0_attn_W_ih, L0_attn_W_hh, L0_attn_b_ih, L0_attn_b_hh)
    h = h + _L0_ffn_ref(_layernorm(h, axis=-1), L0_ffn_attn_w, L0_ffn_attn_b, L0_ffn_gate_w, L0_ffn_gate_b, L0_ffn_w1, L0_ffn_b1, L0_ffn_w2, L0_ffn_b2)
    h = h + _L1_attn_ref(_layernorm(h, axis=-1), L1_attn_W_qkv, L1_attn_W_o)
    h = h + _L1_ffn_ref(_layernorm(h, axis=-1), L1_ffn_Wr, L1_ffn_br, L1_ffn_W1, L1_ffn_b1, L1_ffn_W2, L1_ffn_b2)
    return h

_drawn_inputs = setup_inputs


def setup_inputs(seed=0):
    import zlib

    import numpy as np

    out = dict(_drawn_inputs(seed))
    spreads = {'L0_tok_W1_sw': (0.0062500000931322575, 0.6),
     'L0_tok_W1_sb': (0.0062500000931322575, 0.6),
     'L0_tok_W2_sw': (0.0062500000931322575, 0.6),
     'L0_tok_W2_sb': (0.0062500000931322575, 0.6),
     'L0_ffn_gate_b': (0.0, 0.1),
     'L0_ffn_b1': (0.0, 0.307),
     'L0_ffn_b2': (0.0, 0.1),
     'L1_ffn_br': (0.0, 0.1),
     'L1_ffn_b1': (0.0, 0.1),
     'L1_ffn_b2': (0.0, 0.1)}
    factors = {'L0_tok_W1_b': 5.747,
     'L0_tok_W2_b': 6.379,
     'L0_tok_eps_in1': 3.087,
     'L0_tok_eps_in2': 2.882,
     'L0_tok_eps_out2': 3.078,
     'L0_ffn_attn_w': 4.767,
     'L1_attn_W_qkv': 5.604,
     'L1_attn_W_o': 4.273}
    for name, (base, spread) in spreads.items():
        noise = np.random.default_rng([zlib.crc32(name.encode()), seed]).standard_normal(out[name].shape)
        drawn = base * np.exp(spread * noise) if base else spread * noise
        out[name] = jnp.asarray(drawn.astype(out[name].dtype))
    for name, factor in factors.items():
        out[name] = (out[name] * factor).astype(out[name].dtype)
    return out
```

```python
from contextlib import ExitStack

import numpy as np

import concourse.bass as bass
from concourse import mybir

F32 = mybir.dt.float32
BF16 = mybir.dt.bfloat16
F16 = mybir.dt.float16
U32 = mybir.dt.uint32
ALU = mybir.AluOpType
ACT = mybir.ActivationFunctionType
AX_X = mybir.AxisListType.X

P = 128
B = 8
T_IMG = 64
T_TXT = 128
T = T_IMG + T_TXT
N = B * T
NIMG = B * T_IMG
PATCH = 16
KIN = PATCH * PATCH // P
EPS = 1e-5
HEADS = 8
HD = P // HEADS
HPAD = 32
TOPK = 32
NE = 8
HID = 512
NJ = HID // P
KSEL = 2
XW = 2 * HID + NJ + 1
G = 4
GB = G * B
NLN = 2 * T
KC = T // 2
NEG = -3.0e38
SCALE = float(HD) ** -0.5

(C_W1B, C_W1SB, C_W2B, C_W2SB, C_W3B, C_AW, C_AB) = range(7)
NCOL = 7
NZ_EO, NZ_EI, NZ_EOC = 0, 2 * P, 2 * P + 2 * KIN
NNZ = NZ_EOC + 2
K_ID, K_CEN, K_AVG, K_PE, K_DESC = 0, P, 2 * P, 3 * P, 3 * P + T_IMG
NK = K_DESC + NE


def build(nc, xT, txtT, noise, cols, tokw, w3T, wihT, whhT, bias3, consts, gate_w, gate_b, expert0,
          wqkvT, woT, wr, br, expert1, b2rows, out):
    with ExitStack() as ctx:
        def sb(name, shape, dt=F32):
            return ctx.enter_context(nc.sbuf_tensor(name, shape, dt))

        def sem(name):
            return ctx.enter_context(nc.semaphore(name))

        bank = [ctx.enter_context(nc.psum_tensor(f"bank{i}", [P, 512], F32)) for i in range(8)]

        cst = sb("cst", [P, NK])
        col = sb("col", [P, NCOL])
        ident, center, average = cst[:, K_ID:K_ID + P], cst[:, K_CEN:K_CEN + P], cst[:, K_AVG:K_AVG + P]
        epsc = sb("epsc", [P, 1])
        h_in = sb("h_in", [P, N])
        xn_in = sb("xn_in", [P, N + GB])
        hseq = sb("hseq", [P, N])
        wi = sb("wi", [P, 4 * P])
        wh = [sb(f"wh{k}", [P, 4 * P], BF16) for k in range(3)]
        bias_parts = sb("bias_parts", [3, 4 * P], BF16)
        ones3 = sb("ones3", [3, GB], BF16)

        s_const, s_x, s_txt, s_tokw, s_noise, s_lstmw = (sem(n) for n in (
            "s_const", "s_x", "s_txt", "s_tokw", "s_noise", "s_lstmw"))

        with ExitStack() as tok:
            def tb(name, shape, dt=F32):
                return tok.enter_context(nc.sbuf_tensor(name, shape, dt))

            def tsem(name):
                return ctx.enter_context(nc.semaphore(name))

            x_sb = tb("x_sb", [P, KIN, NIMG])
            nz = tb("nz", [P, NNZ])
            nabs = tb("nabs", [P, NNZ])
            nsgn = tb("nsgn", [P, NNZ])
            tw = tb("tw", [P, 4, KIN, P])
            wn = tb("wn", [P, 2, KIN, P])
            bn = tb("bn", [P, 2])
            w3 = tb("w3", [P, P])
            gt = tb("gt", [P, NIMG])
            gz = tb("gz", [P, NIMG])
            ge = tb("ge", [P, NIMG])
            gn = tb("gn", [P, NIMG])
            gd = tb("gd", [P, NIMG])
            u = tb("u", [P, NIMG])
            xc = tb("xc", [P, 3, 512])
            sq = tb("sq", [P, 3, 512])
            sd = tb("sd", [P, 3, 512])
            wh_raw = tb("wh_raw", [P, 4 * P])
            wh_r1 = tb("wh_r1", [P, 4 * P])
            wh_r2 = tb("wh_r2", [P, 4 * P])
            b_raw = tb("b_raw", [3, 2, 4 * P])
            b_r1 = tb("b_r1", [3, 4 * P])
            b_r2 = tb("b_r2", [3, 4 * P])
            b_p = tb("b_p", [3, 3, 4 * P], BF16)

            s_fill, s_root, s_noisy, s_wn, s_lin, s_clip, s_exp, s_u, s_h, s_dve = (tsem(n) for n in (
                "s_fill", "s_root", "s_noisy", "s_wn", "s_lin", "s_clip", "s_exp", "s_u", "s_h", "s_dve"))
            s_cen, s_sq, s_var, s_std, s_img, s_pool = (tsem(n) for n in (
                "s_cen", "s_sq", "s_var", "s_std", "s_img", "s_pool"))
            g_ps, in_ps, h_ps = bank[0], bank[1], bank[2]
            order = [1, 2, 0]

            with nc.Block() as block:
                @block.sync
                def _(sp):
                    sp.dma_start(nz[:, :], noise).then_inc(s_noise, 16)
                    sp.dma_start(tw[:, :, :, :], tokw).then_inc(s_tokw, 16)
                    sp.dma_start(x_sb[:, :, :], xT.rearrange("(h p) n -> p h n", p=P)).then_inc(s_x, 16)
                    sp.dma_start(w3[:, :], w3T).then_inc(s_x, 16)
                    sp.dma_start(wi[:, :], wihT).then_inc(s_lstmw, 16)
                    sp.dma_start(wh_raw[:, :], whhT).then_inc(s_lstmw, 16)
                    sp.dma_start(b_raw[:, :, :], bias3).then_inc(s_lstmw, 16)

                @block.gpsimd
                def _(pool):
                    pool.memset(epsc[:, :], EPS).then_inc(s_fill, 1)
                    pool.memset(xn_in[:, N:N + GB], 0.0)
                    pool.memset(ones3[:, :], 1.0).then_inc(s_fill, 1)
                    n = 0

                    def link(ins):
                        nonlocal n
                        n += 1
                        ins.then_inc(s_pool, 1)
                        pool.wait_ge(s_pool, n)

                    pool.wait_ge(s_lstmw, 48)
                    link(pool.tensor_scalar(wi[:, 2 * P:3 * P], wi[:, 2 * P:3 * P], 2.0, None, ALU.mult))
                    link(pool.tensor_scalar(wh_raw[:, 2 * P:3 * P], wh_raw[:, 2 * P:3 * P], 2.0, None, ALU.mult))
                    link(pool.tensor_copy(wh[0][:, :], wh_raw[:, :]))
                    link(pool.tensor_tensor(wh_r1[:, :], wh_raw[:, :], wh[0][:, :], ALU.subtract))
                    link(pool.tensor_copy(wh[1][:, :], wh_r1[:, :]))
                    link(pool.tensor_tensor(wh_r2[:, :], wh_r1[:, :], wh[1][:, :], ALU.subtract))
                    link(pool.tensor_copy(wh[2][:, :], wh_r2[:, :]))

                @block.scalar
                def _(act):
                    act.dma_start(cst[:, :], consts).then_inc(s_const, 16)
                    act.dma_start(h_in[:, NIMG:], txtT).then_inc(s_txt, 16)
                    act.dma_start(col[:, :], cols).then_inc(s_const, 16)
                    act.wait_ge(s_noise, 16)
                    act.activation(nabs[:, :], nz[:, :], ACT.Abs).then_inc(s_root, 1)
                    act.activation(nsgn[:, :], nz[:, :], ACT.Sign).then_inc(s_root, 1)
                    act.wait_ge(s_root, 1)
                    act.activation(nabs[:, :], nabs[:, :], ACT.Sqrt).then_inc(s_root, 1)

                    def squares(i):
                        c = order[i]
                        act.wait_ge(s_cen, i + 1)
                        act.activation(xc[:, c, :], bank[3 + i][:, :], ACT.Copy)
                        act.activation(sq[:, c, :], bank[3 + i][:, :], ACT.Square).then_inc(s_sq, 1)

                    def std(i):
                        c = order[i]
                        act.wait_ge(s_var, i + 1)
                        act.activation(sd[:, c, :], bank[3 + i][:, :], ACT.Sqrt, bias=epsc[:, 0:1]).then_inc(s_std, 1)

                    act.wait_ge(s_fill, 2)
                    squares(0)
                    squares(1)
                    std(0)
                    std(1)
                    act.wait_ge(s_clip, 2)
                    act.activation(ge[:, :], gz[:, :], ACT.Exp).then_inc(s_exp, 1)
                    squares(2)
                    std(2)

                @block.vector
                def _(dve):
                    n = 0

                    def link(ins):
                        nonlocal n
                        n += 1
                        ins.then_inc(s_dve, 1)
                        dve.wait_ge(s_dve, n)

                    dve.wait_ge(s_root, 3)
                    link(dve.tensor_tensor(nz[:, :], nabs[:, :], nsgn[:, :], ALU.mult))
                    dve.wait_ge(s_tokw, 16)
                    for w in range(2):
                        for h in range(KIN):
                            e = NZ_EI + w * KIN + h
                            last = dve.scalar_tensor_tensor(wn[:, w, h, :], nz[:, NZ_EO + w * P:NZ_EO + (w + 1) * P],
                                                            nz[:, e:e + 1], tw[:, 2 * w + 1, h, :], ALU.mult, ALU.mult)
                    link(last)
                    for w in range(2):
                        dve.tensor_tensor(wn[:, w, :, :], wn[:, w, :, :], tw[:, 2 * w, :, :], ALU.add)\
                           .then_inc(s_wn, 1)
                    dve.wait_ge(s_const, 32)
                    for w in range(2):
                        last = dve.scalar_tensor_tensor(bn[:, w:w + 1], col[:, C_W1SB + 2 * w:C_W1SB + 2 * w + 1],
                                                        nz[:, NZ_EOC + w:NZ_EOC + w + 1],
                                                        col[:, C_W1B + 2 * w:C_W1B + 2 * w + 1], ALU.mult, ALU.add)
                    link(last)
                    dve.wait_ge(s_lin, 1)
                    dve.tensor_scalar(gt[:, :], g_ps[:, :], bn[:, 0:1], None, ALU.add).then_inc(s_clip, 1)
                    dve.tensor_scalar(gz[:, :], g_ps[:, :], bn[:, 0:1], 20.0, ALU.add, ALU.min).then_inc(s_clip, 1)

                    def norm(i):
                        c = order[i]
                        dve.wait_ge(s_std, i + 1)
                        link(dve.reciprocal(sd[:, c, :], sd[:, c, :]))
                        link(dve.tensor_tensor(xn_in[:, 512 * c:512 * c + 512], xc[:, c, :], sd[:, c, :], ALU.mult))

                    dve.wait_ge(s_exp, 1)
                    link(dve.scalar_tensor_tensor(gn[:, :], ge[:, :], 2.0, ge[:, :], ALU.add, ALU.mult))
                    link(dve.tensor_scalar(gd[:, :], gn[:, :], 2.0, None, ALU.add))
                    link(dve.reciprocal(gd[:, :], gd[:, :]))
                    link(dve.tensor_tensor(gn[:, :], gn[:, :], gd[:, :], ALU.mult))
                    dve.wait_ge(s_clip, 2)
                    link(dve.tensor_tensor(gt[:, :], gt[:, :], gn[:, :], ALU.mult))
                    dve.wait_ge(s_lin, 2)
                    dve.scalar_tensor_tensor(u[:, :], in_ps[:, :], bn[:, 1:2], gt[:, :], ALU.add, ALU.mult)\
                       .then_inc(s_u, 1)
                    dve.wait_ge(s_lstmw, 48)
                    link(dve.tensor_tensor(b_raw[:, 0, :], b_raw[:, 0, :], b_raw[:, 1, :], ALU.add))
                    link(dve.tensor_scalar(b_raw[:, 0, 2 * P:3 * P], b_raw[:, 0, 2 * P:3 * P], 2.0, None, ALU.mult))
                    link(dve.tensor_copy(b_p[:, 0, :], b_raw[:, 0, :]))
                    link(dve.tensor_tensor(b_r1[:, :], b_raw[:, 0, :], b_p[:, 0, :], ALU.subtract))
                    link(dve.tensor_copy(b_p[:, 1, :], b_r1[:, :]))
                    link(dve.tensor_tensor(b_r2[:, :], b_r1[:, :], b_p[:, 1, :], ALU.subtract))
                    link(dve.tensor_copy(b_p[:, 2, :], b_r2[:, :]))
                    link(dve.tensor_scalar(b_r1[:, :], b_p[:, 0, :], cst[0:3, 0:1], None, ALU.mult))
                    link(dve.scalar_tensor_tensor(b_r2[:, :], b_p[:, 1, :], cst[0:3, 1:2], b_r1[:, :],
                                                  ALU.mult, ALU.add))
                    link(dve.scalar_tensor_tensor(bias_parts[:, :], b_p[:, 2, :], cst[0:3, 2:3], b_r2[:, :],
                                                  ALU.mult, ALU.add))
                    norm(0)
                    norm(1)
                    dve.wait_ge(s_h, 1)
                    dve.scalar_tensor_tensor(
                        h_in[:, 0:NIMG].rearrange("p (t b) -> p t b", b=B),
                        h_ps[:, :].rearrange("p (t b) -> p t b", b=B), col[:, C_W3B:C_W3B + 1],
                        cst[:, K_PE:K_PE + T_IMG].unsqueeze(2).to_broadcast([P, T_IMG, B]),
                        ALU.add, ALU.add).then_inc(s_img, 1)
                    norm(2)

                @block.tensor
                def _(pe):
                    def centered(i):
                        c = order[i]
                        pe.matmul(bank[3 + i][:, :], center, h_in[:, 512 * c:512 * c + 512], start=True, stop=True)\
                          .then_inc(s_cen, 1)

                    def variance(i):
                        pe.wait_ge(s_sq, i + 1)
                        pe.matmul(bank[3 + i][:, :], average, sq[:, order[i], :], start=True, stop=True)\
                          .then_inc(s_var, 1)

                    pe.wait_ge(s_const, 32)
                    pe.wait_ge(s_txt, 16)
                    centered(0)
                    centered(1)
                    pe.wait_ge(s_x, 32)
                    for w in range(2):
                        pe.wait_ge(s_wn, w + 1)
                        for h in range(KIN):
                            last = pe.matmul(bank[w][:, :], wn[:, w, h, :], x_sb[:, h, :], start=(h == 0),
                                             stop=(h == KIN - 1))
                        last.then_inc(s_lin, 1)
                    variance(0)
                    variance(1)
                    pe.wait_ge(s_u, 1)
                    pe.matmul(h_ps[:, :], w3[:, :], u[:, :], start=True, stop=True).then_inc(s_h, 1)
                    pe.wait_ge(s_img, 1)
                    centered(2)
                    variance(2)

        with ExitStack() as lstm:
            def lb(name, shape, dt=F32):
                return lstm.enter_context(nc.sbuf_tensor(name, shape, dt))

            sig = lb("sig", [P, 3, B, 2])
            sig_o = lb("sig_o", [P, B])
            tanh_c = lb("tanh_c", [P, B])
            cell = lb("cell", [P, 2, 2 * B + 2])
            h_hi = lb("h_hi", [P, B], F16)
            h_lo = lb("h_lo", [P, B], F16)
            ifg_ps, o_ps = [bank[0], bank[1]], [bank[2], bank[3]]
            s_zero, s_hi, s_lo, s_h32, s_ifg, s_o, s_sig, s_sigo, s_ig, s_c, s_tanh = (sem(n) for n in (
                "s_zero", "s_hi", "s_lo", "s_h32", "s_ifg", "s_o", "s_sig", "s_sigo", "s_ig", "s_c", "s_tanh"))
            ITER = T // (2 * G)

            with nc.Block() as block:
                @block.gpsimd
                def _(pool):
                    pool.memset(sig[:, :, :, :], 0.0)
                    pool.memset(cell[:, :, :], 0.0).then_inc(s_zero, 1)

                @block.vector
                def _(dve):
                    dve.memset(h_hi[:, :], 0.0).then_inc(s_hi, 1)
                    dve.memset(h_lo[:, :], 0.0).then_inc(s_lo, 1)
                    dve.wait_ge(s_zero, 1)
                    with dve.Fori(0, ITER) as it:
                        for s in range(2 * G):
                            t, p = it * (2 * G) + s, s % 2
                            dve.wait_ge(s_sig, t + 1)
                            dve.scalar_tensor_tensor(cell[:, p, 2:2 * B + 2:2], sig[:, 2, :, 1], -0.5, sig[:, 0, :, 1],
                                                     ALU.add, ALU.mult).then_inc(s_ig, 1)
                            dve.wait_ge(s_ig, t + 1)
                            dve.tensor_tensor_scan(cell[:, 1 - p, 0:2 * B], sig[:, 1, :, :].rearrange("p b k -> p (b k)"),
                                                   cell[:, p, 1:2 * B + 1], 0.0, ALU.mult, ALU.add).then_inc(s_c, 1)
                            dve.wait_ge(s_tanh, t + 1)
                            dve.tensor_tensor(h_hi[:, :], sig_o[:, :], tanh_c[:, :], ALU.mult).then_inc(s_hi, 1)
                            h32 = hseq[:, bass.ds(it * (2 * GB) + s * B, B)]
                            dve.tensor_tensor(h32, sig_o[:, :], tanh_c[:, :], ALU.mult).then_inc(s_h32, 1)
                            dve.wait_ge(s_h32, t + 1)
                            dve.tensor_tensor(h_lo[:, :], h32, h_hi[:, :], ALU.subtract).then_inc(s_lo, 1)

                @block.scalar
                def _(act):
                    act.wait_ge(s_zero, 1)
                    with act.Fori(0, ITER) as it:
                        for s in range(2 * G):
                            t, k, q, p = it * (2 * G) + s, s // G, s % G, s % 2
                            act.wait_ge(s_ifg, t + 1)
                            act.activation(sig[:, :, :, 1],
                                           ifg_ps[k][:, 0:3 * GB].rearrange("p (g s b) -> p g s b", g=3, s=G)[:, :, q, :],
                                           ACT.Sigmoid).then_inc(s_sig, 1)
                            act.wait_ge(s_o, t + 1)
                            act.activation(sig_o[:, :], o_ps[k][:, q * B:(q + 1) * B], ACT.Sigmoid).then_inc(s_sigo, 1)
                            act.wait_ge(s_c, t + 1)
                            act.activation(tanh_c[:, :], cell[:, 1 - p, 1:2 * B + 1:2], ACT.Tanh, scale=2.0)\
                               .then_inc(s_tanh, 1)

                @block.tensor
                def _(pe):
                    def gate_out(j, k, lo, hi):
                        return ifg_ps[k][:, j * GB + lo:j * GB + hi] if j < 3 else o_ps[k][:, lo:hi]

                    def input_part(j, k, cols):
                        o = gate_out(j, k, 0, GB)
                        pe.matmul(o, wi[:, j * P:(j + 1) * P], xn_in[:, cols], start=(j in (0, 3)), stop=False,
                                  skip_group_check=True)
                        pe.matmul(o, bias_parts[:, j * P:(j + 1) * P], ones3[:, :], start=False, stop=False,
                                  skip_group_check=True)

                    for j in range(4):
                        input_part(j, 0, slice(0, GB))
                    with pe.Fori(0, ITER) as it:
                        for s in range(2 * G):
                            t, k, q = it * (2 * G) + s, s // G, s % G

                            def recur(w, j, h):
                                return pe.matmul(gate_out(j, k, q * B, (q + 1) * B), wh[w][:, j * P:(j + 1) * P], h[:, :],
                                                 start=False, stop=False, skip_group_check=True)

                            pe.wait_ge(s_hi, t + 1)
                            for w in range(3):
                                for j in range(3):
                                    recur(w, j, h_hi)
                            pe.wait_ge(s_lo, t + 1)
                            for j in range(3):
                                last = recur(0, j, h_lo)
                            last.then_inc(s_ifg, 1)
                            for w in range(3):
                                recur(w, 3, h_hi)
                            recur(0, 3, h_lo).then_inc(s_o, 1)
                            input_part(q, 1 - k, bass.ds(it * (2 * GB) + (1 + k) * GB, GB))

        h_res = sb("h_res", [P, N])
        xn_b = sb("xn_b", [P, N])
        gates = sb("gates", [P, B * KSEL])
        chosen = sb("chosen", [1, B * KSEL], U32)

        NCH = N // NLN
        with ExitStack() as gst:
            def gb(name, shape, dt=F32):
                return gst.enter_context(nc.sbuf_tensor(name, shape, dt))

            def gsem(name):
                return ctx.enter_context(nc.semaphore(name))

            xc = gb("xc2", [P, NCH, NLN])
            sq = gb("sq2", [P, NCH, NLN])
            sd = gb("sd2", [P, NCH, NLN])
            aw_bc = gb("aw_bc", [P, P])
            gw = gb("gw", [P, NE])
            gbias = gb("gbias", [B, NE])
            smax = gb("smax", [P, B])
            sbias = gb("sbias", [P, B])
            esc = gb("esc", [P, B, T])
            scr = gb("scr", [P, T])
            esum = gb("esum", [P, B])
            pooled = gb("pooled", [P, B])
            lg = gb("lg", [B, NE])
            lmax = gb("lmax", [B, 1])
            le = gb("le", [B, NE])
            lsum = gb("lsum", [B, 1])
            lp = gb("lp", [B, NE])
            top = gb("top", [B, 8])
            topi = gb("topi", [B, 8], U32)
            gsum = gb("gsum", [B, 1])
            g2 = gb("g2", [B, KSEL])
            diag = gb("diag", [B, B, KSEL])
            ones8 = gb("ones8", [B, P])
            s_gw, s_res, s_cen, s_sq, s_var, s_std, s_xn, s_ch, s_aw, s_sc, s_sb, s_es = (gsem("g_" + n) for n in (
                "gw", "res", "cen", "sq", "var", "std", "xn", "chain", "aw", "score", "sbias", "escore"))
            s_pool, s_lg, s_lm, s_le, s_dg, s_gp, s_idx, s_idxd = (gsem("g_" + n) for n in (
                "pooled", "logits", "lmax", "lexp", "diag", "gatesps", "index", "indexdma"))
            s_ones = gsem("g_ones")
            with nc.Block() as block:
                @block.sync
                def _(sp):
                    sp.dma_start(gw[:, :], gate_w).then_inc(s_gw, 16)
                    sp.dma_start(gbias[:, :], gate_b).then_inc(s_gw, 16)
                    sp.wait_ge(s_idx, 1)
                    sp.dma_start(chosen[0:1, :], topi[:, 0:KSEL]).then_inc(s_idxd, 16)
                    sp.wait_ge(s_idxd, 16)

                @block.gpsimd
                def _(pool):
                    pool.memset(ones8[:, :], 1.0).then_inc(s_ones, 1)

                @block.scalar
                def _(act):
                    for c in range(NCH):
                        act.wait_ge(s_cen, c + 1)
                        act.activation(xc[:, c, :], bank[c][:, 0:NLN], ACT.Copy)
                        act.activation(sq[:, c, :], bank[c][:, 0:NLN], ACT.Square).then_inc(s_sq, 1)
                    for c in range(NCH):
                        act.wait_ge(s_var, c + 1)
                        act.activation(sd[:, c, :], bank[c][:, 0:NLN], ACT.Sqrt, bias=epsc[:, 0:1]).then_inc(s_std, 1)
                    for b in range(B):
                        act.wait_ge(s_sb, b // 2 + 1)
                        act.activation(esc[:, b, :], bank[4 + b // 2][:, T * (b % 2):T * (b % 2 + 1)], ACT.Exp,
                                       bias=sbias[:, b:b + 1], accum_out=esum[:, b:b + 1]).then_inc(s_es, 1)
                    act.wait_ge(s_lm, 1)
                    act.activation(le[:, :], lg[:, :], ACT.Exp, bias=lmax[:, 0:1], accum_out=lsum[:, 0:1])\
                       .then_inc(s_le, 1)

                @block.vector
                def _(dve):
                    n = 0

                    def link(ins):
                        nonlocal n
                        n += 1
                        ins.then_inc(s_ch, 1)
                        dve.wait_ge(s_ch, n)

                    def by_t(a, c):
                        return a[:, 0:N].rearrange("p (t b) -> p b t", b=B)[:, 2 * c:2 * c + 2, :]

                    dve.tensor_scalar(aw_bc[:, :], average, float(P), col[:, C_AW:C_AW + 1], ALU.mult, ALU.mult)\
                       .then_inc(s_aw, 1)
                    for c in range(NCH):
                        dve.tensor_tensor(h_res[:, NLN * c:NLN * (c + 1)].rearrange("p (b t) -> p b t", b=2),
                                          by_t(h_in, c), by_t(hseq, c), ALU.add).then_inc(s_res, 1)
                    for c in range(NCH):
                        dve.wait_ge(s_std, c + 1)
                        link(dve.reciprocal(sd[:, c, :], sd[:, c, :]))
                        dve.tensor_tensor(xn_b[:, NLN * c:NLN * (c + 1)], xc[:, c, :], sd[:, c, :], ALU.mult)\
                           .then_inc(s_xn, 1)
                    for c in range(NCH):
                        dve.wait_ge(s_sc, c + 1)
                        link(dve.tensor_reduce(smax[:, 2 * c:2 * c + 2],
                                               bank[4 + c][:, 0:NLN].rearrange("p (b t) -> p b t", b=2), AX_X, ALU.max))
                        link(dve.tensor_scalar(sbias[:, 2 * c:2 * c + 2], smax[:, 2 * c:2 * c + 2],
                                               col[:, C_AB:C_AB + 1], -1.0, ALU.add, ALU.mult))
                        dve.tensor_scalar(sbias[:, 2 * c:2 * c + 2], sbias[:, 2 * c:2 * c + 2],
                                          col[:, C_AB:C_AB + 1], None, ALU.add).then_inc(s_sb, 1)
                    dve.wait_ge(s_xn, NCH)
                    for b in range(B):
                        dve.wait_ge(s_es, b + 1)
                        link(dve.tensor_tensor_reduce(scr[:, :], esc[:, b, :], xn_b[:, T * b:T * (b + 1)], 1.0, 0.0,
                                                      ALU.mult, ALU.add, pooled[:, b:b + 1]))
                    link(dve.reciprocal(esum[:, :], esum[:, :]))
                    dve.tensor_tensor(pooled[:, :], pooled[:, :], esum[:, :], ALU.mult).then_inc(s_pool, 1)
                    dve.wait_ge(s_lg, 1)
                    dve.wait_ge(s_gw, 32)
                    link(dve.tensor_tensor(lg[:, :], bank[0][0:B, 0:NE], gbias[:, :], ALU.add))
                    link(dve.tensor_reduce(lmax[:, :], lg[:, :], AX_X, ALU.max))
                    dve.tensor_scalar(lmax[:, :], lmax[:, :], -1.0, None, ALU.mult).then_inc(s_lm, 1)
                    dve.wait_ge(s_le, 1)
                    link(dve.reciprocal(lsum[:, :], lsum[:, :]))
                    link(dve.tensor_scalar(lp[:, :], le[:, :], lsum[:, 0:1], None, ALU.mult))
                    link(dve.max(top[:, :], lp[:, :]))
                    dve.max_index(topi[:, :], top[:, :], lp[:, :]).then_inc(s_idx, 1)
                    link(dve.tensor_reduce(gsum[:, :], top[:, 0:KSEL], AX_X, ALU.add))
                    link(dve.tensor_scalar(gsum[:, :], gsum[:, :], 1e-9, None, ALU.add))
                    link(dve.reciprocal(gsum[:, :], gsum[:, :]))
                    link(dve.tensor_scalar(g2[:, :], top[:, 0:KSEL], gsum[:, 0:1], None, ALU.mult))
                    for k in range(KSEL):
                        last = dve.tensor_scalar(diag[:, :, k], cst[0:B, 0:B], g2[:, k:k + 1], None, ALU.mult)
                    last.then_inc(s_dg, 1)
                    dve.wait_ge(s_gp, 1)
                    link(dve.tensor_copy(gates[:, :], bank[1][:, 0:B * KSEL]))

                @block.tensor
                def _(pe):
                    for c in range(NCH):
                        pe.wait_ge(s_res, c + 1)
                        pe.matmul(bank[c][:, 0:NLN], center, h_res[:, NLN * c:NLN * (c + 1)], start=True, stop=True)\
                          .then_inc(s_cen, 1)
                    for c in range(NCH):
                        pe.wait_ge(s_sq, c + 1)
                        pe.matmul(bank[c][:, 0:NLN], average, sq[:, c, :], start=True, stop=True).then_inc(s_var, 1)
                    pe.wait_ge(s_aw, 1)
                    for c in range(NCH):
                        pe.wait_ge(s_xn, c + 1)
                        pe.matmul(bank[4 + c][:, 0:NLN], aw_bc[:, :], xn_b[:, NLN * c:NLN * (c + 1)],
                                  start=True, stop=True).then_inc(s_sc, 1)
                    pe.wait_ge(s_pool, 1)
                    pe.wait_ge(s_gw, 32)
                    pe.matmul(bank[0][0:B, 0:NE], pooled[:, :], gw[:, :], start=True, stop=True).then_inc(s_lg, 1)
                    pe.wait_ge(s_dg, 1)
                    pe.wait_ge(s_ones, 1)
                    pe.matmul(bank[1][:, 0:B * KSEL], ones8[:, :], diag[:, :, :].rearrange("p b k -> p (b k)"),
                              start=True, stop=True).then_inc(s_gp, 1)


        h_res2 = sb("h_res2", [P, N])
        h_res3 = sb("h_res3", [P, N])
        with ExitStack() as ast:
            def ab(name, shape, dt=F32):
                return ast.enter_context(nc.sbuf_tensor(name, shape, dt))

            def asem(name):
                return ctx.enter_context(nc.semaphore("a_" + name))

            NP = HEADS // 2
            NT = 3
            QR = T - P
            OPS = 24
            ew = ab("ew", [P, KSEL, XW])
            wqkv = ab("wqkv", [P, 3, HEADS * HPAD])
            wo = ab("wo", [P, 2, P])
            hid = ab("hid", [P, KSEL, NJ, T])
            eo = ab("eo", [P, KSEL, T])
            gcur = ab("gcur", [P, KSEL])
            xc = ab("xc3", [P, T])
            sq = ab("sq3", [P, T])
            lnv = ab("lnv", [P, T])
            rstd = ab("rstd", [P, T])
            xn = ab("xn3", [P, T])
            qt = ab("qt", [P, 2, T])
            kt = ab("kt", [P, 2, T])
            vt = ab("vt", [KC, 2, HEADS * HPAD])
            ot = ab("ot", [P, 2, T])
            s_sb = ab("s_sb", [P, 2, NT, T])
            rest = ab("rest", [P, 2, NT, T])
            m8 = ab("m8", [P, 2, NT, TOPK // 8, 8])
            nbias = ab("nbias", [P, 2, NT])
            ex = ab("ex", [P, 2, NT, T])
            zsum = ab("zsum", [P, 2, NT])
            rz = ab("rz", [P, 2, NT])
            keep = ab("keep", [P, 2, NT, T])
            prob = ab("prob", [P, 2, NT, T])
            pt = ab("pt", [KC, NT, 2, P])
            hid_ps = [bank[0], bank[1]]
            eo_ps, ln_ps, sa_ps, sb_ps, tp_ps, out_ps = bank[2:8]
            (s_ewd0, s_ewd1, s_wat, s_head) = (asem(n) for n in ("ew0", "ew1", "weights", "scores0"))
            s_ewd = [s_ewd0, s_ewd1]
            (s_h, s_eo, s_cen, s_var, s_q, s_k, s_v, s_sa, s_sbt, s_tpa, s_tpb, s_av, s_wo) = (asem(n) for n in (
                "hidden_ps", "eo_ps", "cen", "var", "q_ps", "k_ps", "v_ps", "scores01", "scores2", "turned01",
                "turned2", "av", "wo_ps"))
            (c_gelu, c_eo, c_sq, c_ln, c_rstd, c_q, c_k, c_v, c_sa, c_sb, c_e, c_tpa, c_tpb, c_o) = (
                asem(n) for n in ("gelu", "eo", "square", "ln", "rstd", "q", "k", "v", "copied01", "copied2", "exp",
                                  "ptcopy01", "ptcopy2", "ocopy"))
            (d_top, d_rz, d_h2, d_h3, d_g) = (asem(n) for n in ("top", "rz", "h2", "h3", "gcol"))
            (p_nb, p_keep, p_prob, p_xn) = (asem(n) for n in ("nbias", "keep", "prob", "xn"))

            def wait(eng, s, value):
                if not isinstance(value, int) or value > 0:
                    eng.wait_ge(s, value)

            def wait_alone(eng, s, value):
                if not isinstance(value, int) or value > 0:
                    eng.wait_ge(s, value)
                    eng.nop(nofuse=True)

            def cols(b):
                return slice(b * T, (b + 1) * T) if isinstance(b, int) else bass.ds(b * T, T)

            def iterations(eng, body):
                body(0, False, True)
                with eng.Fori(1, B - 1) as b:
                    body(b, True, True)
                body(B - 1, True, False)

            with nc.Block() as block:
                @block.sync
                def _(sp):
                    sp.dma_start(wqkv[:, :, :], wqkvT).then_inc(s_wat, 16)
                    sp.dma_start(wo[:, :, :], woT).then_inc(s_wat, 16)

                    def load(b, k):
                        i = 2 * b + k
                        e = sp.value_load(chosen[0:1, i:i + 1] if isinstance(i, int) else chosen[0:1, bass.ds(i, 1)],
                                          min_val=0, max_val=NE - 1)
                        wait(sp, c_eo, i - 1)
                        sp.dma_start(ew[:, k, :], expert0[bass.ds(e, 1), :, :].rearrange("e p w -> (e p) w"))\
                          .then_inc(s_ewd[k], 16)

                    load(0, 0)
                    load(0, 1)
                    with sp.Fori(1, B) as b:
                        load(b, 0)
                        load(b, 1)

                @block.tensor
                def _(pe):
                    pe.wait_ge(s_wat, 32)

                    def experts(b):
                        for k in range(KSEL):
                            pe.wait_ge(s_ewd[k], 16 * (b + 1))
                            if k == 0:
                                wait(pe, c_k, b)
                            for j in range(NJ):
                                if k:
                                    pe.wait_ge(c_gelu, 8 * b + 2 * (j // 2) + 2)
                                pe.matmul(hid_ps[j // 2][:, T * (j % 2):T * (j % 2 + 1)], ew[:, k, j * P:(j + 1) * P],
                                          xn_b[:, cols(b)], start=True, stop=True).then_inc(s_h, 1)
                        for k in range(KSEL):
                            pe.wait_ge(c_gelu, 8 * b + 4 * k + 4)
                            wait(pe, c_v, b)
                            wait(pe, c_eo, 2 * b + k)
                            for j in range(NJ):
                                last = pe.matmul(eo_ps[:, 0:T], ew[:, k, HID + j * P:HID + (j + 1) * P],
                                                 hid[:, k, j, :], start=(j == 0), stop=(j == NJ - 1))
                            last.then_inc(s_eo, 1)

                    def norm_qk(b):
                        wait(pe, c_tpb, 4 * b - 2)
                        wait(pe, d_h3, b - 1)
                        pe.wait_ge(d_h2, 2 * b + 2)
                        pe.matmul(ln_ps[:, 0:T], center, h_res2[:, cols(b)], start=True, stop=True).then_inc(s_cen, 1)
                        pe.wait_ge(c_sq, b + 1)
                        pe.matmul(ln_ps[:, 0:T], average, sq[:, :], start=True, stop=True).then_inc(s_var, 1)
                        pe.wait_ge(p_xn, b + 1)
                        for a, (bk, s) in enumerate(((hid_ps[0], s_q), (hid_ps[1], s_k))):
                            for half in range(2):
                                last = pe.matmul(bk[:, half * T:(half + 1) * T], wqkv[:, a, half * P:(half + 1) * P],
                                                 xn[:, :], start=True, stop=True)
                            last.then_inc(s, 1)

                    def values(b):
                        pe.wait_ge(c_eo, 2 * b + 2)
                        for kc in range(2):
                            last = pe.matmul(eo_ps[0:KC, kc * 256:kc * 256 + 256], xn[:, kc * KC:(kc + 1) * KC],
                                             wqkv[:, 2, :], start=True, stop=True)
                        last.then_inc(s_v, 1)

                    def pair_scores(b, p):
                        n, half, a = 4 * b + p, p // 2, HPAD * 2 * (p % 2)
                        if p == 0:
                            pe.wait_ge(c_k, b + 1)
                        wait(pe, c_sa, n)
                        wait(pe, c_sb, n)
                        for i in range(2):
                            r = slice(a + HPAD * i, a + HPAD * (i + 1))
                            if i:
                                pe.wait_ge(s_head, n + 1)
                            mm = pe.matmul(sa_ps[:, T * i:T * (i + 1)], qt[r, half, 0:P], kt[r, half, :],
                                           start=True, stop=True)
                            mm.then_inc(s_sa if i else s_head, 1)
                            mm = pe.matmul(sb_ps[QR * i:QR * (i + 1), 0:T], qt[r, half, P:T], kt[r, half, :],
                                           start=True, stop=True)
                        mm.then_inc(s_sbt, 1)

                    def weigh(b, p):
                        n, half, a = 4 * b + p, p // 2, HPAD * 2 * (p % 2)
                        wait(pe, c_tpa, n)
                        for i in range(2):
                            pe.wait_ge(p_prob, 3 * n + i + 1)
                            for kc in range(2):
                                last = pe.transpose(tp_ps[0:KC, (2 * i + kc) * P:(2 * i + kc + 1) * P],
                                                    prob[:, p % 2, i, kc * KC:(kc + 1) * KC], ident)
                        last.then_inc(s_tpa, 1)
                        wait(pe, c_tpb, n)
                        if p == 0:
                            wait(pe, d_h3, b)
                        pe.wait_ge(p_prob, 3 * n + 3)
                        for kc in range(2):
                            last = pe.transpose(ln_ps[0:KC, kc * P:(kc + 1) * P],
                                                prob[:, p % 2, 2, kc * KC:(kc + 1) * KC], ident)
                        last.then_inc(s_tpb, 1)
                        if p == 0:
                            pe.wait_ge(c_v, b + 1)
                            wait(pe, c_o, b)
                        pe.wait_ge(c_tpa, n + 1)
                        pe.wait_ge(c_tpb, n + 1)
                        for i in range(2):
                            h = 2 * p + i
                            o = out_ps[a + HPAD * i:a + HPAD * (i + 1), half * T:(half + 1) * T]
                            for lo, hi, rhs in ((0, P, pt[:, i, :, :]), (P, T, pt[:, 2, :, QR * i:QR * (i + 1)])):
                                for kc in range(2):
                                    last = pe.matmul(o[:, lo:hi], vt[:, kc, HPAD * h:HPAD * (h + 1)], rhs[:, kc, :],
                                                     start=(kc == 0), stop=(kc == 1))
                        last.then_inc(s_av, 1)

                    def project(b):
                        pe.wait_ge(c_o, b + 1)
                        for half in range(2):
                            last = pe.matmul(ln_ps[:, 256:256 + T], wo[:, half, :], ot[:, half, :],
                                             start=(half == 0), stop=(half == 1))
                        last.then_inc(s_wo, 1)

                    def body(b, prev, nxt):
                        pair_scores(b, 1)
                        if prev:
                            weigh(b - 1, 3)
                            project(b - 1)
                        values(b)
                        if nxt:
                            experts(b + 1)
                        pair_scores(b, 2)
                        weigh(b, 0)
                        pair_scores(b, 3)
                        weigh(b, 1)
                        if nxt:
                            norm_qk(b + 1)
                            pair_scores(b + 1, 0)
                        weigh(b, 2)

                    experts(0)
                    norm_qk(0)
                    pair_scores(0, 0)
                    iterations(pe, body)
                    weigh(B - 1, 3)
                    project(B - 1)

                @block.scalar
                def _(act):
                    def experts(b):
                        for k in range(KSEL):
                            if k == 0:
                                act.wait_ge(s_ewd[0], 16 * (b + 1))
                            else:
                                act.wait_ge(s_ewd[1], 16 * (b + 1))
                            wait(act, s_eo, 2 * b + k - 1)
                            for j in range(NJ):
                                act.wait_ge(s_h, 8 * b + 4 * k + 2 * (j // 2) + 2)
                                act.activation(hid[:, k, j, :], hid_ps[j // 2][:, T * (j % 2):T * (j % 2 + 1)],
                                               ACT.Gelu, bias=ew[:, k, 2 * HID + j:2 * HID + j + 1]).then_inc(c_gelu, 1)
                        for k in range(KSEL):
                            wait(act, d_h2, 2 * b + k - 1)
                            act.wait_ge(s_eo, 2 * b + k + 1)
                            act.activation(eo[:, k, :], eo_ps[:, 0:T], ACT.Gelu,
                                           bias=ew[:, k, 2 * HID + NJ:2 * HID + NJ + 1]).then_inc(c_eo, 1)

                    def norm_qk(b):
                        wait(act, p_xn, b)
                        act.wait_ge(s_cen, b + 1)
                        act.activation(xc[:, :], ln_ps[:, 0:T], ACT.Copy)
                        act.activation(sq[:, :], ln_ps[:, 0:T], ACT.Square).then_inc(c_sq, 1)
                        act.wait_ge(s_var, b + 1)
                        act.activation(lnv[:, :], ln_ps[:, 0:T], ACT.Ln, bias=epsc[:, 0:1]).then_inc(c_ln, 1)
                        act.wait_ge(c_ln, b + 1)
                        act.activation(rstd[:, :], lnv[:, :], ACT.Exp, scale=-0.5).then_inc(c_rstd, 1)
                        wait(act, s_sbt, 4 * b)
                        act.wait_ge(s_q, b + 1)
                        act.activation(qt[:, :, :], hid_ps[0][:, 0:2 * T].rearrange("p (h t) -> p h t", h=2),
                                       ACT.Copy).then_inc(c_q, 1)
                        act.wait_ge(s_k, b + 1)
                        act.activation(kt[:, :, :], hid_ps[1][:, 0:2 * T].rearrange("p (h t) -> p h t", h=2),
                                       ACT.Copy).then_inc(c_k, 1)

                    def copy_scores(b, p):
                        n = 4 * b + p
                        wait(act, d_top, OPS * (n - 2) + 6)
                        wait(act, c_e, 3 * (n - 2) + 3)
                        act.wait_ge(s_sa, n + 1)
                        act.activation(s_sb[:, p % 2, 0:2, :], sa_ps[:, 0:2 * T].rearrange("p (i t) -> p i t", i=2),
                                       ACT.Copy).then_inc(c_sa, 1)
                        act.wait_ge(s_sbt, n + 1)
                        act.activation(s_sb[:, p % 2, 2, :], sb_ps[:, 0:T], ACT.Copy).then_inc(c_sb, 1)

                    def exps(b, p):
                        n = 4 * b + p
                        wait(act, p_prob, 3 * (n - 2) + 3)
                        wait(act, d_rz, n - 1)
                        for i in range(NT):
                            act.wait_ge(p_nb, 3 * n + i + 1)
                            if i == 0:
                                act.wait_ge(c_sb, n + 1)
                            act.activation(ex[:, p % 2, i, :], s_sb[:, p % 2, i, :], ACT.Exp, scale=SCALE,
                                           bias=nbias[:, p % 2, i:i + 1], accum_out=zsum[:, p % 2, i:i + 1])\
                               .then_inc(c_e, 1)

                    def copy_turned(b, p):
                        n = 4 * b + p
                        wait(act, s_av, n)
                        act.wait_ge(s_tpa, n + 1)
                        act.activation(pt[:, 0:2, :, :], tp_ps[0:KC, :].rearrange("p (i c q) -> p i c q", i=2, c=2),
                                       ACT.Copy).then_inc(c_tpa, 1)
                        act.wait_ge(s_tpb, n + 1)
                        act.activation(pt[:, 2, :, :], ln_ps[0:KC, 0:2 * P].rearrange("p (c q) -> p c q", c=2),
                                       ACT.Copy).then_inc(c_tpb, 1)

                    def copy_sums(b):
                        wait(act, s_wo, b)
                        act.wait_ge(s_av, 4 * b + 4)
                        act.activation(ot[:, :, :], out_ps[:, 0:2 * T].rearrange("p (h t) -> p h t", h=2),
                                       ACT.Copy).then_inc(c_o, 1)

                    def copy_values(b):
                        wait(act, s_av, 4 * b)
                        act.wait_ge(s_v, b + 1)
                        act.activation(vt[:, :, :], eo_ps[0:KC, :].rearrange("p (c d) -> p c d", c=2), ACT.Copy)\
                           .then_inc(c_v, 1)

                    def body(b, prev, nxt):
                        copy_scores(b, 1)
                        exps(b, 0)
                        if prev:
                            copy_turned(b - 1, 3)
                            copy_sums(b - 1)
                        copy_values(b)
                        if nxt:
                            experts(b + 1)
                        copy_scores(b, 2)
                        exps(b, 1)
                        copy_turned(b, 0)
                        copy_scores(b, 3)
                        exps(b, 2)
                        copy_turned(b, 1)
                        if nxt:
                            norm_qk(b + 1)
                            copy_scores(b + 1, 0)
                        exps(b, 3)
                        copy_turned(b, 2)

                    experts(0)
                    norm_qk(0)
                    copy_scores(0, 0)
                    iterations(act, body)
                    copy_turned(B - 1, 3)
                    copy_sums(B - 1)

                @block.vector
                def _(dve):
                    def combine(b):
                        wait(dve, d_h2, 2 * b)
                        dve.tensor_copy(gcur[:, :], gates[:, 2 * b:2 * b + 2] if isinstance(b, int)
                                        else gates[:, bass.ds(2 * b, 2)]).then_inc(d_g, 1)
                        dve.wait_ge(d_g, b + 1)
                        for k in range(KSEL):
                            dve.wait_ge(c_eo, 2 * b + k + 1)
                            if k:
                                dve.wait_ge(d_h2, 2 * b + 1)
                            dve.scalar_tensor_tensor(h_res2[:, cols(b)], eo[:, k, :], gcur[:, k:k + 1],
                                                     (h_res2 if k else h_res)[:, cols(b)], ALU.mult, ALU.add)\
                               .then_inc(d_h2, 1)

                    def top(b, p):
                        n, r = 4 * b + p, p % 2
                        step = OPS * n
                        for rnd in range(TOPK // 8):
                            for i in range(NT):
                                if rnd:
                                    wait_alone(dve, d_top, step + 6 * rnd - 3 + i + 1)
                                else:
                                    wait(dve, p_nb, 3 * (n - 2) + i + 1)
                                    wait_alone(dve, c_sa if i < 2 else c_sb, n + 1)
                                dve.max(m8[:, r, i, rnd, :], (rest if rnd else s_sb)[:, r, i, :]).then_inc(d_top, 1)
                            for i in range(NT):
                                if not rnd:
                                    wait(dve, p_prob, 3 * (n - 2) + i + 1)
                                wait_alone(dve, d_top, step + 6 * rnd + i + 1)
                                dve.match_replace(rest[:, r, i, :], m8[:, r, i, rnd, :],
                                                  (rest if rnd else s_sb)[:, r, i, :], NEG).then_inc(d_top, 1)
                        dve.wait_ge(c_e, 3 * n + 3)
                        wait(dve, p_keep, 3 * (n - 2) + 3)
                        dve.reciprocal(rz[:, r, :], zsum[:, r, :]).then_inc(d_rz, 1)

                    def residual(b):
                        dve.wait_ge(s_wo, b + 1)
                        dve.tensor_tensor(h_res3[:, cols(b)], ln_ps[:, 256:256 + T], h_res2[:, cols(b)], ALU.add)\
                           .then_inc(d_h3, 1)

                    def body(b, prev, nxt):
                        top(b, 0)
                        if prev:
                            residual(b - 1)
                        top(b, 1)
                        if nxt:
                            combine(b + 1)
                        top(b, 2)
                        top(b, 3)

                    combine(0)
                    iterations(dve, body)
                    residual(B - 1)

                @block.gpsimd
                def _(pool):
                    def bias(b, p):
                        n, r = 4 * b + p, p % 2
                        for i in range(NT):
                            wait(pool, c_e, 3 * (n - 2) + i + 1)
                            wait_alone(pool, d_top, OPS * n + i + 1)
                            pool.tensor_scalar(nbias[:, r, i:i + 1], m8[:, r, i, 0, 0:1], -SCALE, None, ALU.mult)\
                                .then_inc(p_nb, 1)

                    def kept(b, p):
                        n, r = 4 * b + p, p % 2
                        for i in range(NT):
                            wait(pool, p_prob, 3 * (n - 2) + i + 1)
                            if i == 0:
                                pool.wait_ge(d_rz, n + 1)
                            wait_alone(pool, d_top, OPS * n + 21 + i + 1)
                            pool.tensor_scalar(keep[:, r, i, :], rest[:, r, i, :], NEG, rz[:, r, i:i + 1],
                                               ALU.is_equal, ALU.mult).then_inc(p_keep, 1)
                        for i in range(NT):
                            wait(pool, s_tpb, n - 1)
                            pool.wait_ge(p_keep, 3 * n + i + 1)
                            pool.tensor_tensor(prob[:, r, i, :], keep[:, r, i, :], ex[:, r, i, :], ALU.mult)\
                                .then_inc(p_prob, 1)

                    def norm(b):
                        wait(pool, s_v, b)
                        pool.wait_ge(c_rstd, b + 1)
                        pool.tensor_tensor(xn[:, :], xc[:, :], rstd[:, :], ALU.mult).then_inc(p_xn, 1)

                    def body(b, prev, nxt):
                        bias(b, 0)
                        kept(b, 0)
                        bias(b, 1)
                        kept(b, 1)
                        bias(b, 2)
                        if nxt:
                            norm(b + 1)
                        kept(b, 2)
                        bias(b, 3)
                        kept(b, 3)

                    norm(0)
                    iterations(pool, body)

        xw = sb("xw", [P, NE, XW])
        b2r = sb("b2r", [NE, P])
        route = sb("route", [NE, N])
        route16 = sb("route16", [NE, N], BF16)
        pick = sb("pick", [NE, NE, P], BF16)
        s_xw = sem("s_xw")
        NTT = N // P
        with ExitStack() as rst:
            def rb(name, shape, dt=F32):
                return rst.enter_context(nc.sbuf_tensor(name, shape, dt))

            def rsem(name):
                return ctx.enter_context(nc.semaphore("r_" + name))

            xc = rb("xc4", [P, NCH, NLN])
            sq = rb("sq4", [P, NCH, NLN])
            sd = rb("sd4", [P, NCH, NLN])
            wr_sb = rb("wr_sb", [P, NE])
            br_sb = rb("br_sb", [P, NE])
            lgt = rb("lgt", [P, NTT, NE])
            mx = rb("mx", [P, NTT])
            hit = rb("hit", [P, NTT, NE])
            s_wr, s_cen, s_sq, s_var, s_std, s_xn, s_ch, s_lg, s_hit, s_turn, s_pick = (rsem(n) for n in (
                "weights", "cen", "sq", "var", "std", "xn", "chain", "logits", "hit", "turned", "pick"))

            with nc.Block() as block:
                @block.sync
                def _(sp):
                    sp.dma_start(wr_sb[:, :], wr).then_inc(s_wr, 16)
                    sp.dma_start(br_sb[:, :], br).then_inc(s_wr, 16)
                    sp.dma_start(xw[:, :, :], expert1).then_inc(s_xw, 16)
                    sp.dma_start(b2r[:, :], b2rows).then_inc(s_xw, 16)

                @block.gpsimd
                def _(pool):
                    pool.tensor_copy(pick[:, :, :], cst[0:NE, 0:NE].unsqueeze(2).to_broadcast([NE, NE, P]))\
                        .then_inc(s_pick, 1)

                @block.scalar
                def _(act):
                    for c in range(NCH):
                        act.wait_ge(s_cen, c + 1)
                        act.activation(xc[:, c, :], bank[c][:, 0:NLN], ACT.Copy)
                        act.activation(sq[:, c, :], bank[c][:, 0:NLN], ACT.Square).then_inc(s_sq, 1)
                    for c in range(NCH):
                        act.wait_ge(s_var, c + 1)
                        act.activation(sd[:, c, :], bank[c][:, 0:NLN], ACT.Sqrt, bias=epsc[:, 0:1]).then_inc(s_std, 1)

                @block.vector
                def _(dve):
                    n = 0

                    def link(ins):
                        nonlocal n
                        n += 1
                        ins.then_inc(s_ch, 1)
                        dve.wait_ge(s_ch, n)

                    for c in range(NCH):
                        dve.wait_ge(s_std, c + 1)
                        link(dve.reciprocal(sd[:, c, :], sd[:, c, :]))
                        dve.tensor_tensor(xn_b[:, NLN * c:NLN * (c + 1)], xc[:, c, :], sd[:, c, :], ALU.mult)\
                           .then_inc(s_xn, 1)
                    dve.wait_ge(s_lg, 1)
                    dve.wait_ge(s_wr, 32)
                    every = [P, NTT, NE]
                    link(dve.tensor_tensor(lgt[:, :, :], bank[4][:, 0:NTT * NE].rearrange("p (i e) -> p i e", e=NE),
                                           br_sb[:, :].unsqueeze(1).to_broadcast(every), ALU.add))
                    link(dve.tensor_reduce(mx[:, :], lgt[:, :, :], AX_X, ALU.max))
                    link(dve.tensor_tensor(hit[:, :, :], lgt[:, :, :], mx[:, :].unsqueeze(2).to_broadcast(every),
                                           ALU.is_ge))
                    link(dve.tensor_tensor(hit[:, :, :], hit[:, :, :],
                                           cst[:, K_DESC:K_DESC + NE].unsqueeze(1).to_broadcast(every), ALU.mult))
                    link(dve.tensor_reduce(mx[:, :], hit[:, :, :], AX_X, ALU.max))
                    dve.tensor_tensor(hit[:, :, :], hit[:, :, :], mx[:, :].unsqueeze(2).to_broadcast(every),
                                      ALU.is_equal).then_inc(s_hit, 1)
                    for g in range(NTT // 4):
                        dve.wait_ge(s_turn, g + 1)
                        dve.tensor_copy(route[:, 512 * g:512 * g + 512], bank[5 + g][0:NE, :])
                        link(dve.tensor_copy(route16[:, 512 * g:512 * g + 512], bank[5 + g][0:NE, :]))

                @block.tensor
                def _(pe):
                    for c in range(NCH):
                        pe.matmul(bank[c][:, 0:NLN], center, h_res3[:, NLN * c:NLN * (c + 1)], start=True, stop=True)\
                          .then_inc(s_cen, 1)
                    for c in range(NCH):
                        pe.wait_ge(s_sq, c + 1)
                        pe.matmul(bank[c][:, 0:NLN], average, sq[:, c, :], start=True, stop=True).then_inc(s_var, 1)
                    pe.wait_ge(s_wr, 32)
                    for i in range(NTT):
                        pe.wait_ge(s_xn, (i * P + P - 1) // NLN + 1)
                        last = pe.matmul(bank[4][:, NE * i:NE * i + NE], xn_b[:, P * i:P * i + P], wr_sb[:, :],
                                         start=True, stop=True)
                    last.then_inc(s_lg, 1)
                    pe.wait_ge(s_hit, 1)
                    for i in range(NTT):
                        mm = pe.transpose(bank[5 + i // 4][0:NE, P * (i % 4):P * (i % 4) + P], hit[:, i, :], ident)
                        if i % 4 == 3:
                            mm.then_inc(s_turn, 1)

        with ExitStack() as fst:
            def fb(name, shape, dt=F32):
                return fst.enter_context(nc.sbuf_tensor(name, shape, dt))

            def fsem(name):
                return ctx.enter_context(nc.semaphore("f_" + name))

            CW = 512
            NC3 = N // CW
            STEPS = NE * NJ
            LAG = 3
            act_sb = fb("act_sb", [P, 4, CW])
            msk_sb = fb("msk_sb", [P, 4, CW])
            y = fb("y", [P, CW])
            h_ps, m_ps, y_ps = bank[0:4], bank[4:6], bank[6]
            f_h, f_m, f_y, c_relu, d_msk, d_y, s_out = (fsem(n) for n in (
                "hidden_ps", "mask_ps", "y_ps", "relu", "masked", "y", "out"))

            def wait(eng, s, value):
                if not isinstance(value, int) or value > 0:
                    eng.wait_ge(s, value)

            def chunks(eng, body):
                body(0)
                with eng.Fori(1, NC3) as c:
                    body(c)

            def cols(c):
                return slice(0, CW) if isinstance(c, int) else bass.ds(c * CW, CW)

            with nc.Block() as block:
                @block.tensor
                def _(pe):
                    pe.wait_ge(s_xw, 32)
                    pe.wait_ge(s_pick, 1)

                    def mask(c, e):
                        wait(pe, d_msk, STEPS * c + NJ * (e - 1))
                        pe.nop(nofuse=True)
                        pe.matmul(m_ps[e % 2][:, :], pick[:, e, :], route16[:, cols(c)], start=True, stop=True)\
                          .then_inc(f_m, 1)

                    def hidden(c, i):
                        e, j = divmod(i, NJ)
                        wait(pe, c_relu, STEPS * c + i - 3)
                        pe.matmul(h_ps[i % 4][:, :], xw[:, e, j * P:(j + 1) * P], xn_b[:, cols(c)],
                                  start=True, stop=True).then_inc(f_h, 1)

                    def output(c, i):
                        e, j = divmod(i, NJ)
                        pe.wait_ge(d_msk, STEPS * c + i + 1)
                        pe.matmul(y_ps[:, :], xw[:, e, HID + j * P:HID + (j + 1) * P], msk_sb[:, i % 4, :],
                                  start=False, stop=(i == STEPS - 1), skip_group_check=True).then_inc(f_y, 1)

                    def body(c):
                        mask(c, 0)
                        for i in range(STEPS + LAG):
                            if i < STEPS:
                                hidden(c, i)
                            if i % NJ == 1 and i // NJ + 1 < NE:
                                mask(c, i // NJ + 1)
                            if i == LAG - 1:
                                wait(pe, d_y, c)
                                pe.nop(nofuse=True)
                                pe.matmul(y_ps[:, :], b2r[:, :], route[:, cols(c)], start=True, stop=False,
                                          skip_group_check=True)
                            if i >= LAG:
                                output(c, i - LAG)

                    chunks(pe, body)

                @block.scalar
                def _(act):
                    def body(c):
                        for i in range(STEPS):
                            e, j = divmod(i, NJ)
                            wait(act, d_msk, STEPS * c + i - 3)
                            act.wait_ge(f_h, STEPS * c + i + 1)
                            act.activation(act_sb[:, i % 4, :], h_ps[i % 4][:, :], ACT.Relu,
                                           bias=xw[:, e, 2 * HID + j:2 * HID + j + 1]).then_inc(c_relu, 1)

                    act.wait_ge(s_xw, 32)
                    chunks(act, body)

                @block.vector
                def _(dve):
                    def body(c):
                        for i in range(STEPS):
                            e, j = divmod(i, NJ)
                            if j == 0:
                                dve.wait_ge(f_m, NE * c + e + 1)
                            wait(dve, f_y, STEPS * c + i - 3)
                            dve.wait_ge(c_relu, STEPS * c + i + 1)
                            dve.tensor_tensor(msk_sb[:, i % 4, :], m_ps[e % 2][:, :], act_sb[:, i % 4, :], ALU.mult)\
                               .then_inc(d_msk, 1)
                        wait(dve, s_out, 16 * c)
                        dve.wait_ge(f_y, STEPS * (c + 1))
                        dve.tensor_tensor(y[:, :], y_ps[:, :], h_res3[:, cols(c)], ALU.add).then_inc(d_y, 1)

                    chunks(dve, body)

                @block.sync
                def _(sp):
                    def body(c):
                        sp.wait_ge(d_y, c + 1)
                        sp.dma_start(out[:, cols(c)], y[:, :]).then_inc(s_out, 16)

                    chunks(sp, body)
                    sp.wait_ge(s_out, 16 * NC3)


def layouts(a):
    f = {k: np.asarray(v) for k, v in a.items()}
    side = T_IMG_SIDE = P // PATCH
    d = {}
    d["xT"] = f["x"].reshape(B, side, PATCH, side, PATCH).transpose(2, 4, 1, 3, 0).reshape(PATCH * PATCH, NIMG)
    d["txtT"] = f["txt"].transpose(2, 1, 0).reshape(P, T_TXT * B)

    def halves(v):
        return v.reshape(KIN, P).T

    eo = [f[f"L0_tok_eps_out{w}"] for w in (1, 2)]
    d["noise"] = np.concatenate([np.broadcast_to(np.concatenate(eo), (P, 2 * P)),
                                 halves(f["L0_tok_eps_in1"]), halves(f["L0_tok_eps_in2"]),
                                 np.stack(eo, 1)], 1)
    d["cols"] = np.stack([f["L0_tok_W1_b"], f["L0_tok_W1_sb"], f["L0_tok_W2_b"], f["L0_tok_W2_sb"],
                          f["L0_tok_W3_b"], f["L0_ffn_attn_w"][:, 0], np.broadcast_to(f["L0_ffn_attn_b"], (P,))], 1)
    d["tokw"] = np.stack([f["L0_tok_" + n].T.reshape(KIN, P, P).transpose(1, 0, 2)
                          for n in ("W1_w", "W1_sw", "W2_w", "W2_sw")], 1)
    d["w3T"] = f["L0_tok_W3_w"].T
    d["wihT"] = f["L0_attn_W_ih"].T
    d["whhT"] = f["L0_attn_W_hh"].T
    d["bias3"] = np.broadcast_to(np.stack([f["L0_attn_b_ih"], f["L0_attn_b_hh"]]), (3, 2, 4 * P))
    pos = np.arange(T_IMG, dtype=np.float32)[:, None]
    div = np.exp(np.arange(0, P, 2, dtype=np.float32) * np.float32(-np.log(10000.0) / P))
    ang = (pos * div).astype(np.float32)
    pe = np.stack([np.sin(ang), np.cos(ang)], -1).reshape(T_IMG, P).astype(np.float32)
    eye = np.eye(P, dtype=np.float32)
    avg = np.full((P, P), 1.0 / P, np.float32)
    desc = np.broadcast_to(NE - np.arange(NE, dtype=np.float32), (P, NE))
    d["consts"] = np.concatenate([eye, eye - avg, avg, pe.T, desc], 1)
    d["gate_w"] = f["L0_ffn_gate_w"]
    d["gate_b"] = np.broadcast_to(f["L0_ffn_gate_b"], (B, NE))

    def expert_rows(w1, b1, w2, b2):
        return np.concatenate([w1, w2.reshape(NE, NJ, P, P).transpose(0, 2, 1, 3).reshape(NE, P, HID),
                               b1.reshape(NE, NJ, P).transpose(0, 2, 1), b2[:, :, None]], 2)

    d["expert0"] = expert_rows(f["L0_ffn_w1"], f["L0_ffn_b1"], f["L0_ffn_w2"], f["L0_ffn_b2"])
    w = f["L1_attn_W_qkv"].reshape(HEADS, 3, HD, P).transpose(3, 1, 0, 2)
    d["wqkvT"] = np.pad(w, ((0, 0), (0, 0), (0, 0), (0, HPAD - HD))).reshape(P, 3, HEADS * HPAD)
    wo = f["L1_attn_W_o"].T.reshape(HEADS, HD, P)
    d["woT"] = np.pad(wo, ((0, 0), (0, HPAD - HD), (0, 0))).reshape(2, P, P).transpose(1, 0, 2)
    d["wr"] = f["L1_ffn_Wr"]
    d["br"] = np.broadcast_to(f["L1_ffn_br"], (P, NE))
    d["expert1"] = expert_rows(f["L1_ffn_W1"], f["L1_ffn_b1"], f["L1_ffn_W2"], f["L1_ffn_b2"]).transpose(1, 0, 2)
    d["b2rows"] = f["L1_ffn_b2"]
    return {k: np.ascontiguousarray(v) for k, v in d.items()}


def kernel(**inputs):
    import concourse.bacc as bacc
    from concourse.bass_utils import run_bass_kernel_spmd

    nc = bacc.Bacc("TRN2", target_bir_lowering=False, num_devices=1)
    arrays = layouts(inputs)
    aps = {n: nc.dram_tensor(n, v.shape, mybir.dt.from_np(v.dtype), kind="ExternalInput").ap()
           for n, v in arrays.items()}
    out = nc.dram_tensor("out", (P, N), F32, kind="ExternalOutput").ap()
    build(nc, out=out, **aps)
    got = run_bass_kernel_spmd(nc, [arrays], core_ids=[0]).results[0]["out"]
    return got.reshape(P, B, T).transpose(1, 2, 0)
```

```python
from contextlib import ExitStack

import numpy as np

import concourse.bass as bass
from concourse import mybir

F32 = mybir.dt.float32
BF16 = mybir.dt.bfloat16
F16 = mybir.dt.float16
U32 = mybir.dt.uint32
ALU = mybir.AluOpType
ACT = mybir.ActivationFunctionType
AX_X = mybir.AxisListType.X

P = 128
B = 8
T_IMG = 64
T_TXT = 128
T = T_IMG + T_TXT
N = B * T
NIMG = B * T_IMG
PATCH = 16
KIN = PATCH * PATCH // P
EPS = 1e-5
HEADS = 8
HD = P // HEADS
HPAD = 32
TOPK = 32
NE = 8
HID = 512
NJ = HID // P
KSEL = 2
XW = 2 * HID + NJ + 1
G = 4
GB = G * B
NLN = 2 * T
KC = T // 2
NTT = N // P
NBLK = NTT + NE - 1
NEG = -3.0e38
SCALE = float(HD) ** -0.5

(C_W1B, C_W1SB, C_W2B, C_W2SB, C_W3B, C_AW, C_AB) = range(7)
NCOL = 7
NZ_EO, NZ_EI, NZ_EOC = 0, 2 * P, 2 * P + 2 * KIN
NNZ = NZ_EOC + 2
K_ID, K_CEN, K_AVG, K_PE, K_DESC = 0, P, 2 * P, 3 * P, 3 * P + T_IMG
K_TRI = K_DESC + NE
K_MULT = K_TRI + 2 * P
K_BEFORE = K_MULT + NTT
K_UPTO = K_BEFORE + NE * NE
K_BLOCK = K_UPTO + NE * NE
NK = K_BLOCK + NBLK


def build(nc, xT, txtT, noise, cols, tokw, w3T, wihT, whhT, bias3, consts, gate_w, gate_b, expert0,
          wqkvT, woT, wr, br, expert1, b2rows, out):
    with ExitStack() as ctx:
        def sb(name, shape, dt=F32):
            return ctx.enter_context(nc.sbuf_tensor(name, shape, dt))

        def sem(name):
            return ctx.enter_context(nc.semaphore(name))

        bank = [ctx.enter_context(nc.psum_tensor(f"bank{i}", [P, 512], F32)) for i in range(8)]

        cst = sb("cst", [P, NK])
        col = sb("col", [P, NCOL])
        ident, center, average = cst[:, K_ID:K_ID + P], cst[:, K_CEN:K_CEN + P], cst[:, K_AVG:K_AVG + P]
        epsc = sb("epsc", [P, 1])
        h_in = sb("h_in", [P, N])
        xn_in = sb("xn_in", [P, N + GB])
        hseq = sb("hseq", [P, N])
        wi = sb("wi", [P, 4 * P])
        wh = [sb(f"wh{k}", [P, 4 * P], BF16) for k in range(3)]
        bias_parts = sb("bias_parts", [3, 4 * P], BF16)
        ones3 = sb("ones3", [3, GB], BF16)

        s_const, s_x, s_txt, s_tokw, s_noise, s_lstmw = (sem(n) for n in (
            "s_const", "s_x", "s_txt", "s_tokw", "s_noise", "s_lstmw"))

        with ExitStack() as tok:
            def tb(name, shape, dt=F32):
                return tok.enter_context(nc.sbuf_tensor(name, shape, dt))

            def tsem(name):
                return ctx.enter_context(nc.semaphore(name))

            x_sb = tb("x_sb", [P, KIN, NIMG])
            nz = tb("nz", [P, NNZ])
            nabs = tb("nabs", [P, NNZ])
            nsgn = tb("nsgn", [P, NNZ])
            tw = tb("tw", [P, 4, KIN, P])
            wn = tb("wn", [P, 2, KIN, P])
            bn = tb("bn", [P, 2])
            w3 = tb("w3", [P, P])
            gt = tb("gt", [P, NIMG])
            gz = tb("gz", [P, NIMG])
            ge = tb("ge", [P, NIMG])
            gn = tb("gn", [P, NIMG])
            gd = tb("gd", [P, NIMG])
            u = tb("u", [P, NIMG])
            xc = tb("xc", [P, 3, 512])
            sq = tb("sq", [P, 3, 512])
            sd = tb("sd", [P, 3, 512])
            wh_raw = tb("wh_raw", [P, 4 * P])
            wh_r1 = tb("wh_r1", [P, 4 * P])
            wh_r2 = tb("wh_r2", [P, 4 * P])
            b_raw = tb("b_raw", [3, 2, 4 * P])
            b_r1 = tb("b_r1", [3, 4 * P])
            b_r2 = tb("b_r2", [3, 4 * P])
            b_p = tb("b_p", [3, 3, 4 * P], BF16)

            s_fill, s_root, s_noisy, s_wn, s_lin, s_clip, s_exp, s_u, s_h, s_dve = (tsem(n) for n in (
                "s_fill", "s_root", "s_noisy", "s_wn", "s_lin", "s_clip", "s_exp", "s_u", "s_h", "s_dve"))
            s_cen, s_sq, s_var, s_std, s_img, s_pool = (tsem(n) for n in (
                "s_cen", "s_sq", "s_var", "s_std", "s_img", "s_pool"))
            g_ps, in_ps, h_ps = bank[0], bank[1], bank[2]
            order = [1, 2, 0]

            with nc.Block() as block:
                @block.sync
                def _(sp):
                    sp.dma_start(nz[:, :], noise).then_inc(s_noise, 16)
                    sp.dma_start(tw[:, :, :, :], tokw).then_inc(s_tokw, 16)
                    sp.dma_start(x_sb[:, :, :], xT.rearrange("(h p) n -> p h n", p=P)).then_inc(s_x, 16)
                    sp.dma_start(w3[:, :], w3T).then_inc(s_x, 16)
                    sp.dma_start(wi[:, :], wihT).then_inc(s_lstmw, 16)
                    sp.dma_start(wh_raw[:, :], whhT).then_inc(s_lstmw, 16)
                    sp.dma_start(b_raw[:, :, :], bias3).then_inc(s_lstmw, 16)

                @block.gpsimd
                def _(pool):
                    pool.memset(epsc[:, :], EPS).then_inc(s_fill, 1)
                    pool.memset(xn_in[:, N:N + GB], 0.0)
                    pool.memset(ones3[:, :], 1.0).then_inc(s_fill, 1)
                    n = 0

                    def link(ins):
                        nonlocal n
                        n += 1
                        ins.then_inc(s_pool, 1)
                        pool.wait_ge(s_pool, n)

                    pool.wait_ge(s_lstmw, 48)
                    link(pool.tensor_scalar(wi[:, 2 * P:3 * P], wi[:, 2 * P:3 * P], 2.0, None, ALU.mult))
                    link(pool.tensor_scalar(wh_raw[:, 2 * P:3 * P], wh_raw[:, 2 * P:3 * P], 2.0, None, ALU.mult))
                    link(pool.tensor_copy(wh[0][:, :], wh_raw[:, :]))
                    link(pool.tensor_tensor(wh_r1[:, :], wh_raw[:, :], wh[0][:, :], ALU.subtract))
                    link(pool.tensor_copy(wh[1][:, :], wh_r1[:, :]))
                    link(pool.tensor_tensor(wh_r2[:, :], wh_r1[:, :], wh[1][:, :], ALU.subtract))
                    link(pool.tensor_copy(wh[2][:, :], wh_r2[:, :]))

                @block.scalar
                def _(act):
                    act.dma_start(cst[:, :], consts).then_inc(s_const, 16)
                    act.dma_start(h_in[:, NIMG:], txtT).then_inc(s_txt, 16)
                    act.dma_start(col[:, :], cols).then_inc(s_const, 16)
                    act.wait_ge(s_noise, 16)
                    act.activation(nabs[:, :], nz[:, :], ACT.Abs).then_inc(s_root, 1)
                    act.activation(nsgn[:, :], nz[:, :], ACT.Sign).then_inc(s_root, 1)
                    act.wait_ge(s_root, 1)
                    act.activation(nabs[:, :], nabs[:, :], ACT.Sqrt).then_inc(s_root, 1)

                    def squares(i):
                        c = order[i]
                        act.wait_ge(s_cen, i + 1)
                        act.activation(xc[:, c, :], bank[3 + i][:, :], ACT.Copy)
                        act.activation(sq[:, c, :], bank[3 + i][:, :], ACT.Square).then_inc(s_sq, 1)

                    def std(i):
                        c = order[i]
                        act.wait_ge(s_var, i + 1)
                        act.activation(sd[:, c, :], bank[3 + i][:, :], ACT.Sqrt, bias=epsc[:, 0:1]).then_inc(s_std, 1)

                    act.wait_ge(s_fill, 2)
                    squares(0)
                    squares(1)
                    std(0)
                    std(1)
                    act.wait_ge(s_clip, 2)
                    act.activation(ge[:, :], gz[:, :], ACT.Exp).then_inc(s_exp, 1)
                    squares(2)
                    std(2)

                @block.vector
                def _(dve):
                    n = 0

                    def link(ins):
                        nonlocal n
                        n += 1
                        ins.then_inc(s_dve, 1)
                        dve.wait_ge(s_dve, n)

                    dve.wait_ge(s_root, 3)
                    link(dve.tensor_tensor(nz[:, :], nabs[:, :], nsgn[:, :], ALU.mult))
                    dve.wait_ge(s_tokw, 16)
                    for w in range(2):
                        for h in range(KIN):
                            e = NZ_EI + w * KIN + h
                            last = dve.scalar_tensor_tensor(wn[:, w, h, :], nz[:, NZ_EO + w * P:NZ_EO + (w + 1) * P],
                                                            nz[:, e:e + 1], tw[:, 2 * w + 1, h, :], ALU.mult, ALU.mult)
                    link(last)
                    for w in range(2):
                        dve.tensor_tensor(wn[:, w, :, :], wn[:, w, :, :], tw[:, 2 * w, :, :], ALU.add)\
                           .then_inc(s_wn, 1)
                    dve.wait_ge(s_const, 32)
                    for w in range(2):
                        last = dve.scalar_tensor_tensor(bn[:, w:w + 1], col[:, C_W1SB + 2 * w:C_W1SB + 2 * w + 1],
                                                        nz[:, NZ_EOC + w:NZ_EOC + w + 1],
                                                        col[:, C_W1B + 2 * w:C_W1B + 2 * w + 1], ALU.mult, ALU.add)
                    link(last)
                    dve.wait_ge(s_lin, 1)
                    dve.tensor_scalar(gt[:, :], g_ps[:, :], bn[:, 0:1], None, ALU.add).then_inc(s_clip, 1)
                    dve.tensor_scalar(gz[:, :], g_ps[:, :], bn[:, 0:1], 20.0, ALU.add, ALU.min).then_inc(s_clip, 1)

                    def norm(i):
                        c = order[i]
                        dve.wait_ge(s_std, i + 1)
                        link(dve.reciprocal(sd[:, c, :], sd[:, c, :]))
                        link(dve.tensor_tensor(xn_in[:, 512 * c:512 * c + 512], xc[:, c, :], sd[:, c, :], ALU.mult))

                    dve.wait_ge(s_exp, 1)
                    link(dve.scalar_tensor_tensor(gn[:, :], ge[:, :], 2.0, ge[:, :], ALU.add, ALU.mult))
                    link(dve.tensor_scalar(gd[:, :], gn[:, :], 2.0, None, ALU.add))
                    link(dve.reciprocal(gd[:, :], gd[:, :]))
                    link(dve.tensor_tensor(gn[:, :], gn[:, :], gd[:, :], ALU.mult))
                    dve.wait_ge(s_clip, 2)
                    link(dve.tensor_tensor(gt[:, :], gt[:, :], gn[:, :], ALU.mult))
                    dve.wait_ge(s_lin, 2)
                    dve.scalar_tensor_tensor(u[:, :], in_ps[:, :], bn[:, 1:2], gt[:, :], ALU.add, ALU.mult)\
                       .then_inc(s_u, 1)
                    dve.wait_ge(s_lstmw, 48)
                    link(dve.tensor_tensor(b_raw[:, 0, :], b_raw[:, 0, :], b_raw[:, 1, :], ALU.add))
                    link(dve.tensor_scalar(b_raw[:, 0, 2 * P:3 * P], b_raw[:, 0, 2 * P:3 * P], 2.0, None, ALU.mult))
                    link(dve.tensor_copy(b_p[:, 0, :], b_raw[:, 0, :]))
                    link(dve.tensor_tensor(b_r1[:, :], b_raw[:, 0, :], b_p[:, 0, :], ALU.subtract))
                    link(dve.tensor_copy(b_p[:, 1, :], b_r1[:, :]))
                    link(dve.tensor_tensor(b_r2[:, :], b_r1[:, :], b_p[:, 1, :], ALU.subtract))
                    link(dve.tensor_copy(b_p[:, 2, :], b_r2[:, :]))
                    link(dve.tensor_scalar(b_r1[:, :], b_p[:, 0, :], cst[0:3, 0:1], None, ALU.mult))
                    link(dve.scalar_tensor_tensor(b_r2[:, :], b_p[:, 1, :], cst[0:3, 1:2], b_r1[:, :],
                                                  ALU.mult, ALU.add))
                    link(dve.scalar_tensor_tensor(bias_parts[:, :], b_p[:, 2, :], cst[0:3, 2:3], b_r2[:, :],
                                                  ALU.mult, ALU.add))
                    norm(0)
                    norm(1)
                    dve.wait_ge(s_h, 1)
                    dve.scalar_tensor_tensor(
                        h_in[:, 0:NIMG].rearrange("p (t b) -> p t b", b=B),
                        h_ps[:, :].rearrange("p (t b) -> p t b", b=B), col[:, C_W3B:C_W3B + 1],
                        cst[:, K_PE:K_PE + T_IMG].unsqueeze(2).to_broadcast([P, T_IMG, B]),
                        ALU.add, ALU.add).then_inc(s_img, 1)
                    norm(2)

                @block.tensor
                def _(pe):
                    def centered(i):
                        c = order[i]
                        pe.matmul(bank[3 + i][:, :], center, h_in[:, 512 * c:512 * c + 512], start=True, stop=True)\
                          .then_inc(s_cen, 1)

                    def variance(i):
                        pe.wait_ge(s_sq, i + 1)
                        pe.matmul(bank[3 + i][:, :], average, sq[:, order[i], :], start=True, stop=True)\
                          .then_inc(s_var, 1)

                    pe.wait_ge(s_const, 32)
                    pe.wait_ge(s_txt, 16)
                    centered(0)
                    centered(1)
                    pe.wait_ge(s_x, 32)
                    for w in range(2):
                        pe.wait_ge(s_wn, w + 1)
                        for h in range(KIN):
                            last = pe.matmul(bank[w][:, :], wn[:, w, h, :], x_sb[:, h, :], start=(h == 0),
                                             stop=(h == KIN - 1))
                        last.then_inc(s_lin, 1)
                    variance(0)
                    variance(1)
                    pe.wait_ge(s_u, 1)
                    pe.matmul(h_ps[:, :], w3[:, :], u[:, :], start=True, stop=True).then_inc(s_h, 1)
                    pe.wait_ge(s_img, 1)
                    centered(2)
                    variance(2)

        with ExitStack() as lstm:
            def lb(name, shape, dt=F32):
                return lstm.enter_context(nc.sbuf_tensor(name, shape, dt))

            sig = lb("sig", [P, 3, B, 2])
            sig_o = lb("sig_o", [P, B])
            tanh_c = lb("tanh_c", [P, B])
            cell = lb("cell", [P, 2, 2 * B + 2])
            h_hi = lb("h_hi", [P, B], F16)
            h_lo = lb("h_lo", [P, B], F16)
            ifg_ps, o_ps = [bank[0], bank[1]], [bank[2], bank[3]]
            s_zero, s_hi, s_lo, s_h32, s_ifg, s_o, s_sig, s_sigo, s_ig, s_c, s_tanh = (sem(n) for n in (
                "s_zero", "s_hi", "s_lo", "s_h32", "s_ifg", "s_o", "s_sig", "s_sigo", "s_ig", "s_c", "s_tanh"))
            ITER = T // (2 * G)

            with nc.Block() as block:
                @block.gpsimd
                def _(pool):
                    pool.memset(sig[:, :, :, :], 0.0)
                    pool.memset(cell[:, :, :], 0.0).then_inc(s_zero, 1)

                @block.vector
                def _(dve):
                    dve.memset(h_hi[:, :], 0.0).then_inc(s_hi, 1)
                    dve.memset(h_lo[:, :], 0.0).then_inc(s_lo, 1)
                    dve.wait_ge(s_zero, 1)
                    with dve.Fori(0, ITER) as it:
                        for s in range(2 * G):
                            t, p = it * (2 * G) + s, s % 2
                            dve.wait_ge(s_sig, t + 1)
                            dve.scalar_tensor_tensor(cell[:, p, 2:2 * B + 2:2], sig[:, 2, :, 1], -0.5, sig[:, 0, :, 1],
                                                     ALU.add, ALU.mult).then_inc(s_ig, 1)
                            dve.wait_ge(s_ig, t + 1)
                            dve.tensor_tensor_scan(cell[:, 1 - p, 0:2 * B], sig[:, 1, :, :].rearrange("p b k -> p (b k)"),
                                                   cell[:, p, 1:2 * B + 1], 0.0, ALU.mult, ALU.add).then_inc(s_c, 1)
                            dve.wait_ge(s_tanh, t + 1)
                            dve.tensor_tensor(h_hi[:, :], sig_o[:, :], tanh_c[:, :], ALU.mult).then_inc(s_hi, 1)
                            h32 = hseq[:, bass.ds(it * (2 * GB) + s * B, B)]
                            dve.tensor_tensor(h32, sig_o[:, :], tanh_c[:, :], ALU.mult).then_inc(s_h32, 1)
                            dve.wait_ge(s_h32, t + 1)
                            dve.tensor_tensor(h_lo[:, :], h32, h_hi[:, :], ALU.subtract).then_inc(s_lo, 1)

                @block.scalar
                def _(act):
                    act.preload_act_table_set("sigmoid_and_others")
                    act.wait_ge(s_zero, 1)
                    with act.Fori(0, ITER) as it:
                        for s in range(2 * G):
                            t, k, q, p = it * (2 * G) + s, s // G, s % G, s % 2
                            act.wait_ge(s_ifg, t + 1)
                            act.activation(sig[:, :, :, 1],
                                           ifg_ps[k][:, 0:3 * GB].rearrange("p (g s b) -> p g s b", g=3, s=G)[:, :, q, :],
                                           ACT.Sigmoid).then_inc(s_sig, 1)
                            act.wait_ge(s_o, t + 1)
                            act.activation(sig_o[:, :], o_ps[k][:, q * B:(q + 1) * B], ACT.Sigmoid).then_inc(s_sigo, 1)
                            act.wait_ge(s_c, t + 1)
                            act.activation(tanh_c[:, :], cell[:, 1 - p, 1:2 * B + 1:2], ACT.Tanh, scale=2.0)\
                               .then_inc(s_tanh, 1)

                @block.tensor
                def _(pe):
                    def gate_out(j, k, lo, hi):
                        return ifg_ps[k][:, j * GB + lo:j * GB + hi] if j < 3 else o_ps[k][:, lo:hi]

                    def input_part(j, k, cols):
                        o = gate_out(j, k, 0, GB)
                        pe.matmul(o, wi[:, j * P:(j + 1) * P], xn_in[:, cols], start=(j in (0, 3)), stop=False,
                                  skip_group_check=True)
                        pe.matmul(o, bias_parts[:, j * P:(j + 1) * P], ones3[:, :], start=False, stop=False,
                                  skip_group_check=True)

                    for j in range(4):
                        input_part(j, 0, slice(0, GB))
                    with pe.Fori(0, ITER) as it:
                        for s in range(2 * G):
                            t, k, q = it * (2 * G) + s, s // G, s % G

                            def recur(w, j, h):
                                return pe.matmul(gate_out(j, k, q * B, (q + 1) * B), wh[w][:, j * P:(j + 1) * P], h[:, :],
                                                 start=False, stop=False, skip_group_check=True)

                            pe.wait_ge(s_hi, t + 1)
                            for w in range(3):
                                for j in range(3):
                                    recur(w, j, h_hi)
                            pe.wait_ge(s_lo, t + 1)
                            for j in range(3):
                                last = recur(0, j, h_lo)
                            last.then_inc(s_ifg, 1)
                            for w in range(3):
                                recur(w, 3, h_hi)
                            recur(0, 3, h_lo).then_inc(s_o, 1)
                            input_part(q, 1 - k, bass.ds(it * (2 * GB) + (1 + k) * GB, GB))

        h_res = sb("h_res", [P, N])
        xn_b = sb("xn_b", [P, N])
        gates = sb("gates", [P, B * KSEL])
        chosen = sb("chosen", [1, B * KSEL], U32)

        NCH = N // NLN
        with ExitStack() as gst:
            def gb(name, shape, dt=F32):
                return gst.enter_context(nc.sbuf_tensor(name, shape, dt))

            def gsem(name):
                return ctx.enter_context(nc.semaphore(name))

            xc = gb("xc2", [P, NCH, NLN])
            sq = gb("sq2", [P, NCH, NLN])
            sd = gb("sd2", [P, NCH, NLN])
            aw_bc = gb("aw_bc", [P, P])
            gw = gb("gw", [P, NE])
            gbias = gb("gbias", [B, NE])
            smax = gb("smax", [P, B])
            sbias = gb("sbias", [P, B])
            esc = gb("esc", [P, B, T])
            scr = gb("scr", [P, T])
            esum = gb("esum", [P, B])
            pooled = gb("pooled", [P, B])
            lg = gb("lg", [B, NE])
            lmax = gb("lmax", [B, 1])
            le = gb("le", [B, NE])
            lsum = gb("lsum", [B, 1])
            lp = gb("lp", [B, NE])
            top = gb("top", [B, 8])
            topi = gb("topi", [B, 8], U32)
            gsum = gb("gsum", [B, 1])
            g2 = gb("g2", [B, KSEL])
            diag = gb("diag", [B, B, KSEL])
            ones8 = gb("ones8", [B, P])
            s_gw, s_res, s_cen, s_sq, s_var, s_std, s_xn, s_ch, s_aw, s_sc, s_sb, s_es = (gsem("g_" + n) for n in (
                "gw", "res", "cen", "sq", "var", "std", "xn", "chain", "aw", "score", "sbias", "escore"))
            s_pool, s_lg, s_lm, s_le, s_dg, s_gp, s_idx, s_idxd = (gsem("g_" + n) for n in (
                "pooled", "logits", "lmax", "lexp", "diag", "gatesps", "index", "indexdma"))
            s_ones = gsem("g_ones")
            with nc.Block() as block:
                @block.sync
                def _(sp):
                    sp.dma_start(gw[:, :], gate_w).then_inc(s_gw, 16)
                    sp.dma_start(gbias[:, :], gate_b).then_inc(s_gw, 16)
                    sp.wait_ge(s_idx, 1)
                    sp.dma_start(chosen[0:1, :], topi[:, 0:KSEL]).then_inc(s_idxd, 16)
                    sp.wait_ge(s_idxd, 16)

                @block.gpsimd
                def _(pool):
                    pool.memset(ones8[:, :], 1.0).then_inc(s_ones, 1)

                @block.scalar
                def _(act):
                    for c in range(NCH):
                        act.wait_ge(s_cen, c + 1)
                        act.activation(xc[:, c, :], bank[c][:, 0:NLN], ACT.Copy)
                        act.activation(sq[:, c, :], bank[c][:, 0:NLN], ACT.Square).then_inc(s_sq, 1)
                    for c in range(NCH):
                        act.wait_ge(s_var, c + 1)
                        act.activation(sd[:, c, :], bank[c][:, 0:NLN], ACT.Sqrt, bias=epsc[:, 0:1]).then_inc(s_std, 1)
                    for b in range(B):
                        act.wait_ge(s_sb, b // 2 + 1)
                        act.activation(esc[:, b, :], bank[4 + b // 2][:, T * (b % 2):T * (b % 2 + 1)], ACT.Exp,
                                       bias=sbias[:, b:b + 1], accum_out=esum[:, b:b + 1]).then_inc(s_es, 1)
                    act.wait_ge(s_lm, 1)
                    act.activation(le[:, :], lg[:, :], ACT.Exp, bias=lmax[:, 0:1], accum_out=lsum[:, 0:1])\
                       .then_inc(s_le, 1)

                @block.vector
                def _(dve):
                    n = 0

                    def link(ins):
                        nonlocal n
                        n += 1
                        ins.then_inc(s_ch, 1)
                        dve.wait_ge(s_ch, n)

                    def by_t(a, c):
                        return a[:, 0:N].rearrange("p (t b) -> p b t", b=B)[:, 2 * c:2 * c + 2, :]

                    dve.tensor_scalar(aw_bc[:, :], average, float(P), col[:, C_AW:C_AW + 1], ALU.mult, ALU.mult)\
                       .then_inc(s_aw, 1)
                    for c in range(NCH):
                        dve.tensor_tensor(h_res[:, NLN * c:NLN * (c + 1)].rearrange("p (b t) -> p b t", b=2),
                                          by_t(h_in, c), by_t(hseq, c), ALU.add).then_inc(s_res, 1)
                    for c in range(NCH):
                        dve.wait_ge(s_std, c + 1)
                        link(dve.reciprocal(sd[:, c, :], sd[:, c, :]))
                        dve.tensor_tensor(xn_b[:, NLN * c:NLN * (c + 1)], xc[:, c, :], sd[:, c, :], ALU.mult)\
                           .then_inc(s_xn, 1)
                    for c in range(NCH):
                        dve.wait_ge(s_sc, c + 1)
                        link(dve.tensor_reduce(smax[:, 2 * c:2 * c + 2],
                                               bank[4 + c][:, 0:NLN].rearrange("p (b t) -> p b t", b=2), AX_X, ALU.max))
                        link(dve.tensor_scalar(sbias[:, 2 * c:2 * c + 2], smax[:, 2 * c:2 * c + 2],
                                               col[:, C_AB:C_AB + 1], -1.0, ALU.add, ALU.mult))
                        dve.tensor_scalar(sbias[:, 2 * c:2 * c + 2], sbias[:, 2 * c:2 * c + 2],
                                          col[:, C_AB:C_AB + 1], None, ALU.add).then_inc(s_sb, 1)
                    dve.wait_ge(s_xn, NCH)
                    for b in range(B):
                        dve.wait_ge(s_es, b + 1)
                        link(dve.tensor_tensor_reduce(scr[:, :], esc[:, b, :], xn_b[:, T * b:T * (b + 1)], 1.0, 0.0,
                                                      ALU.mult, ALU.add, pooled[:, b:b + 1]))
                    link(dve.reciprocal(esum[:, :], esum[:, :]))
                    dve.tensor_tensor(pooled[:, :], pooled[:, :], esum[:, :], ALU.mult).then_inc(s_pool, 1)
                    dve.wait_ge(s_lg, 1)
                    dve.wait_ge(s_gw, 32)
                    link(dve.tensor_tensor(lg[:, :], bank[0][0:B, 0:NE], gbias[:, :], ALU.add))
                    link(dve.tensor_reduce(lmax[:, :], lg[:, :], AX_X, ALU.max))
                    dve.tensor_scalar(lmax[:, :], lmax[:, :], -1.0, None, ALU.mult).then_inc(s_lm, 1)
                    dve.wait_ge(s_le, 1)
                    link(dve.reciprocal(lsum[:, :], lsum[:, :]))
                    link(dve.tensor_scalar(lp[:, :], le[:, :], lsum[:, 0:1], None, ALU.mult))
                    link(dve.max(top[:, :], lp[:, :]))
                    dve.max_index(topi[:, :], top[:, :], lp[:, :]).then_inc(s_idx, 1)
                    link(dve.tensor_reduce(gsum[:, :], top[:, 0:KSEL], AX_X, ALU.add))
                    link(dve.tensor_scalar(gsum[:, :], gsum[:, :], 1e-9, None, ALU.add))
                    link(dve.reciprocal(gsum[:, :], gsum[:, :]))
                    link(dve.tensor_scalar(g2[:, :], top[:, 0:KSEL], gsum[:, 0:1], None, ALU.mult))
                    for k in range(KSEL):
                        last = dve.tensor_scalar(diag[:, :, k], cst[0:B, 0:B], g2[:, k:k + 1], None, ALU.mult)
                    last.then_inc(s_dg, 1)
                    dve.wait_ge(s_gp, 1)
                    link(dve.tensor_copy(gates[:, :], bank[1][:, 0:B * KSEL]))

                @block.tensor
                def _(pe):
                    for c in range(NCH):
                        pe.wait_ge(s_res, c + 1)
                        pe.matmul(bank[c][:, 0:NLN], center, h_res[:, NLN * c:NLN * (c + 1)], start=True, stop=True)\
                          .then_inc(s_cen, 1)
                    for c in range(NCH):
                        pe.wait_ge(s_sq, c + 1)
                        pe.matmul(bank[c][:, 0:NLN], average, sq[:, c, :], start=True, stop=True).then_inc(s_var, 1)
                    pe.wait_ge(s_aw, 1)
                    for c in range(NCH):
                        pe.wait_ge(s_xn, c + 1)
                        pe.matmul(bank[4 + c][:, 0:NLN], aw_bc[:, :], xn_b[:, NLN * c:NLN * (c + 1)],
                                  start=True, stop=True).then_inc(s_sc, 1)
                    pe.wait_ge(s_pool, 1)
                    pe.wait_ge(s_gw, 32)
                    pe.matmul(bank[0][0:B, 0:NE], pooled[:, :], gw[:, :], start=True, stop=True).then_inc(s_lg, 1)
                    pe.wait_ge(s_dg, 1)
                    pe.wait_ge(s_ones, 1)
                    pe.matmul(bank[1][:, 0:B * KSEL], ones8[:, :], diag[:, :, :].rearrange("p b k -> p (b k)"),
                              start=True, stop=True).then_inc(s_gp, 1)


        h_res2 = sb("h_res2", [P, N])
        h_res3 = sb("h_res3", [P, N])
        xw = sb("xw", [P, NE, XW - 1])
        empty = sb("empty", [P, P])
        scr_x = nc.dram_tensor("scr_x", (NBLK * P, P), F32).ap()
        s_xw, s_zero_x, s_empty = sem("s_xw"), sem("s_zero_x"), sem("s_empty")
        with ExitStack() as ast:
            def ab(name, shape, dt=F32):
                return ast.enter_context(nc.sbuf_tensor(name, shape, dt))

            def asem(name):
                return ctx.enter_context(nc.semaphore("a_" + name))

            NP = HEADS // 2
            NT = 3
            QR = T - P
            OPS = 24
            ew = ab("ew", [P, KSEL, XW])
            wqkv = ab("wqkv", [P, 3, HEADS * HPAD])
            wo = ab("wo", [P, 2, P])
            hid = ab("hid", [P, KSEL, NJ, T])
            eo = ab("eo", [P, KSEL, T])
            gcur = ab("gcur", [P, KSEL])
            xc = ab("xc3", [P, T])
            sq = ab("sq3", [P, T])
            lnv = ab("lnv", [P, T])
            rstd = ab("rstd", [P, T])
            xn = ab("xn3", [P, T])
            qt = ab("qt", [P, 2, T])
            kt = ab("kt", [P, 2, T])
            vt = ab("vt", [KC, 2, HEADS * HPAD])
            ot = ab("ot", [P, 2, T])
            pr = ab("pr", [P, T])
            s_sb = ab("s_sb", [P, NP, NT, T])
            rest = ab("rest", [P, NP, NT, T])
            m8 = ab("m8", [P, NP, NT, TOPK // 8, 8])
            nbias = ab("nbias", [P, NP, NT])
            ex = ab("ex", [P, NP, NT, T])
            zsum = ab("zsum", [P, NP, NT])
            rz = ab("rz", [P, NP, NT])
            keep = ab("keep", [P, NP, NT, T])
            prob = ab("prob", [P, NP, NT, T])
            pt = ab("pt", [KC, NT, 2, P])
            hid_ps = [bank[0], bank[1]]
            v_ps, ln_ps, sa_ps, sb_ps, tp_ps, out_ps = bank[2:8]
            (s_ewd0, s_ewd1, s_wat, s_head) = (asem(n) for n in ("ew0", "ew1", "weights", "scores0"))
            s_ewd = [s_ewd0, s_ewd1]
            (s_h, s_eo, s_cen, s_var, s_q, s_k, s_v, s_sa, s_sbt, s_tpa, s_tpb, s_av, s_wo) = (asem(n) for n in (
                "hidden_ps", "eo_ps", "cen", "var", "q_ps", "k_ps", "v_ps", "scores01", "scores2", "turned01",
                "turned2", "av", "wo_ps"))
            (c_gelu, c_eo, c_sq, c_ln, c_rstd, c_q, c_k, c_v, c_sa, c_sb, c_e, c_tpa, c_tpb, c_o, c_pr) = (
                asem(n) for n in ("gelu", "eo", "square", "ln", "rstd", "q", "k", "v", "copied01", "copied2", "exp",
                                  "ptcopy01", "ptcopy2", "ocopy", "product"))
            (d_top, d_rz, d_keep, d_h2, d_g) = (asem(n) for n in ("top", "rz", "keep", "h2", "gcol"))
            (p_nb, p_prob, p_xn, p_h3) = (asem(n) for n in ("nbias", "prob", "xn", "h3"))

            def wait(eng, s, value):
                if not isinstance(value, int) or value > 0:
                    eng.wait_ge(s, value)

            def wait_alone(eng, s, value):
                if not isinstance(value, int) or value > 0:
                    eng.wait_ge(s, value)
                    eng.nop(nofuse=True)

            def cols(b):
                return slice(b * T, (b + 1) * T) if isinstance(b, int) else bass.ds(b * T, T)

            def iterations(eng, body):
                body(0, False, True)
                with eng.Fori(1, B - 1) as b:
                    body(b, True, True)
                body(B - 1, True, False)

            with nc.Block() as block:
                @block.sync
                def _(sp):
                    sp.dma_start(wqkv[:, :, :], wqkvT).then_inc(s_wat, 16)
                    sp.dma_start(wo[:, :, :], woT).then_inc(s_wat, 16)

                    def load(b, k):
                        i = 2 * b + k
                        e = sp.value_load(chosen[0:1, i:i + 1] if isinstance(i, int) else chosen[0:1, bass.ds(i, 1)],
                                          min_val=0, max_val=NE - 1)
                        wait(sp, c_eo, i - 1)
                        sp.dma_start(ew[:, k, :], expert0[bass.ds(e, 1), :, :].rearrange("e p w -> (e p) w"))\
                          .then_inc(s_ewd[k], 16)

                    load(0, 0)
                    load(0, 1)
                    sp.dma_start(xw[:, :, :], expert1).then_inc(s_xw, 16)
                    sp.wait_ge(s_empty, 1)
                    sp.dma_start(scr_x.rearrange("(k p) f -> p k f", p=P),
                                 empty[:, :].unsqueeze(1).to_broadcast([P, NBLK, P])).then_inc(s_zero_x, 16)
                    with sp.Fori(1, B) as b:
                        load(b, 0)
                        load(b, 1)

                @block.tensor
                def _(pe):
                    pe.wait_ge(s_wat, 32)

                    def hidden(b, k):
                        pe.wait_ge(s_ewd[k], 16 * (b + 1))
                        if k == 0:
                            wait(pe, c_k, b)
                        for j in range(NJ):
                            if k:
                                pe.wait_ge(c_gelu, 8 * b + 2 * (j // 2) + 2)
                            pe.matmul(hid_ps[j // 2][:, T * (j % 2):T * (j % 2 + 1)], ew[:, k, j * P:(j + 1) * P],
                                      xn_b[:, cols(b)], start=True, stop=True).then_inc(s_h, 1)

                    def output(b, k):
                        pe.wait_ge(c_gelu, 8 * b + 4 * k + 4)
                        wait(pe, c_tpb, 4 * (b - 2) + 3 + k)
                        wait(pe, c_eo, 2 * b + k)
                        for j in range(NJ):
                            last = pe.matmul(ln_ps[:, 0:T], ew[:, k, HID + j * P:HID + (j + 1) * P],
                                             hid[:, k, j, :], start=(j == 0), stop=(j == NJ - 1))
                        last.then_inc(s_eo, 1)

                    def centered(b):
                        wait(pe, c_tpb, 4 * (b - 1))
                        pe.wait_ge(d_h2, 2 * b + 2)
                        pe.matmul(ln_ps[:, 0:T], center, h_res2[:, cols(b)], start=True, stop=True).then_inc(s_cen, 1)

                    def variance(b):
                        wait(pe, c_tpb, 4 * (b - 1) + 1)
                        pe.wait_ge(c_sq, b + 1)
                        pe.matmul(ln_ps[:, 0:T], average, sq[:, :], start=True, stop=True).then_inc(s_var, 1)

                    def qkv(b):
                        pe.wait_ge(p_xn, b + 1)
                        for a, (bk, s) in enumerate(((hid_ps[0], s_q), (hid_ps[1], s_k))):
                            for half in range(2):
                                last = pe.matmul(bk[:, half * T:(half + 1) * T], wqkv[:, a, half * P:(half + 1) * P],
                                                 xn[:, :], start=True, stop=True)
                            last.then_inc(s, 1)
                        wait(pe, c_v, b)
                        for kc in range(2):
                            last = pe.matmul(v_ps[0:KC, kc * 256:kc * 256 + 256], xn[:, kc * KC:(kc + 1) * KC],
                                             wqkv[:, 2, :], start=True, stop=True)
                        last.then_inc(s_v, 1)

                    def pair_scores(b, p):
                        n, half, a = 4 * b + p, p // 2, HPAD * 2 * (p % 2)
                        if p == 0:
                            pe.wait_ge(c_k, b + 1)
                        wait(pe, c_sa, n)
                        wait(pe, c_sb, n)
                        for i in range(2):
                            r = slice(a + HPAD * i, a + HPAD * (i + 1))
                            if i:
                                pe.wait_ge(s_head, n + 1)
                            mm = pe.matmul(sa_ps[:, T * i:T * (i + 1)], qt[r, half, 0:P], kt[r, half, :],
                                           start=True, stop=True)
                            mm.then_inc(s_sa if i else s_head, 1)
                            mm = pe.matmul(sb_ps[QR * i:QR * (i + 1), 0:T], qt[r, half, P:T], kt[r, half, :],
                                           start=True, stop=True)
                        mm.then_inc(s_sbt, 1)

                    def turn(b, p, ln_free=None):
                        n = 4 * b + p
                        wait(pe, c_tpa, n)
                        for i in range(2):
                            pe.wait_ge(p_prob, 3 * n + i + 1)
                            for kc in range(2):
                                last = pe.transpose(tp_ps[0:KC, (2 * i + kc) * P:(2 * i + kc + 1) * P],
                                                    prob[:, p, i, kc * KC:(kc + 1) * KC], ident)
                        last.then_inc(s_tpa, 1)
                        wait(pe, c_tpb, n)
                        if ln_free:
                            wait(pe, *ln_free)
                        pe.wait_ge(p_prob, 3 * n + 3)
                        for kc in range(2):
                            last = pe.transpose(ln_ps[0:KC, kc * P:(kc + 1) * P],
                                                prob[:, p, 2, kc * KC:(kc + 1) * KC], ident)
                        last.then_inc(s_tpb, 1)

                    def weigh(b, p):
                        n, half, a = 4 * b + p, p // 2, HPAD * 2 * (p % 2)
                        if p == 0:
                            pe.wait_ge(c_v, b + 1)
                            wait(pe, c_pr, b)
                        pe.wait_ge(c_tpa, n + 1)
                        pe.wait_ge(c_tpb, n + 1)
                        for i in range(2):
                            h = 2 * p + i
                            o = out_ps[a + HPAD * i:a + HPAD * (i + 1), half * T:(half + 1) * T]
                            for lo, hi, rhs in ((0, P, pt[:, i, :, :]), (P, T, pt[:, 2, :, QR * i:QR * (i + 1)])):
                                for kc in range(2):
                                    last = pe.matmul(o[:, lo:hi], vt[:, kc, HPAD * h:HPAD * (h + 1)], rhs[:, kc, :],
                                                     start=(kc == 0), stop=(kc == 1))
                        last.then_inc(s_av, 1)

                    def project(b):
                        pe.wait_ge(c_o, b + 1)
                        for half in range(2):
                            last = pe.matmul(out_ps[:, 0:T], wo[:, half, :], ot[:, half, :],
                                             start=(half == 0), stop=(half == 1))
                        last.then_inc(s_wo, 1)

                    def body(b, prev, nxt):
                        pair_scores(b, 2)
                        if nxt:
                            hidden(b + 1, 0)
                        pair_scores(b, 3)
                        if prev:
                            turn(b - 1, 2)
                        if nxt:
                            hidden(b + 1, 1)
                            output(b + 1, 0)
                        if prev:
                            weigh(b - 1, 2)
                            turn(b - 1, 3, (c_eo, 2 * b + 3) if nxt else None)
                        if nxt:
                            output(b + 1, 1)
                        if prev:
                            weigh(b - 1, 3)
                        if nxt:
                            centered(b + 1)
                        if prev:
                            project(b - 1)
                        turn(b, 0, (c_sq, b + 2) if nxt else None)
                        if nxt:
                            variance(b + 1)
                        weigh(b, 0)
                        if nxt:
                            qkv(b + 1)
                        turn(b, 1, (c_ln, b + 2) if nxt else None)
                        if nxt:
                            pair_scores(b + 1, 0)
                        weigh(b, 1)
                        if nxt:
                            pair_scores(b + 1, 1)

                    hidden(0, 0)
                    hidden(0, 1)
                    output(0, 0)
                    output(0, 1)
                    centered(0)
                    variance(0)
                    qkv(0)
                    pair_scores(0, 0)
                    pair_scores(0, 1)
                    iterations(pe, body)
                    turn(B - 1, 2)
                    weigh(B - 1, 2)
                    turn(B - 1, 3)
                    weigh(B - 1, 3)
                    project(B - 1)

                @block.scalar
                def _(act):
                    def hidden(b, k):
                        act.wait_ge(s_ewd[k], 16 * (b + 1))
                        wait(act, s_eo, 2 * b + k - 1)
                        for j in range(NJ):
                            act.wait_ge(s_h, 8 * b + 4 * k + 2 * (j // 2) + 2)
                            act.activation(hid[:, k, j, :], hid_ps[j // 2][:, T * (j % 2):T * (j % 2 + 1)],
                                           ACT.Gelu, bias=ew[:, k, 2 * HID + j:2 * HID + j + 1]).then_inc(c_gelu, 1)

                    def output(b, k):
                        wait(act, d_h2, 2 * b + k - 1)
                        act.wait_ge(s_eo, 2 * b + k + 1)
                        act.activation(eo[:, k, :], ln_ps[:, 0:T], ACT.Gelu,
                                       bias=ew[:, k, 2 * HID + NJ:2 * HID + NJ + 1]).then_inc(c_eo, 1)
                        if k:
                            act.preload_act_table_set("natural_log_exp_and_others")

                    def squares(b):
                        wait(act, p_xn, b)
                        act.wait_ge(s_cen, b + 1)
                        act.activation(xc[:, :], ln_ps[:, 0:T], ACT.Copy)
                        act.activation(sq[:, :], ln_ps[:, 0:T], ACT.Square).then_inc(c_sq, 1)

                    def inverse_root(b):
                        act.wait_ge(s_var, b + 1)
                        act.activation(lnv[:, :], ln_ps[:, 0:T], ACT.Ln, bias=epsc[:, 0:1]).then_inc(c_ln, 1)
                        act.wait_ge(c_ln, b + 1)
                        act.activation(rstd[:, :], lnv[:, :], ACT.Exp, scale=-0.5).then_inc(c_rstd, 1)

                    def copy_qk(b):
                        wait(act, s_sbt, 4 * b)
                        act.wait_ge(s_q, b + 1)
                        act.activation(qt[:, :, :], hid_ps[0][:, 0:2 * T].rearrange("p (h t) -> p h t", h=2),
                                       ACT.Copy).then_inc(c_q, 1)
                        act.wait_ge(s_k, b + 1)
                        act.activation(kt[:, :, :], hid_ps[1][:, 0:2 * T].rearrange("p (h t) -> p h t", h=2),
                                       ACT.Copy).then_inc(c_k, 1)

                    def copy_scores(b, p):
                        n = 4 * b + p
                        wait(act, d_top, OPS * (n - NP) + 6)
                        wait(act, c_e, 3 * (n - NP) + 3)
                        act.wait_ge(s_sa, n + 1)
                        act.activation(s_sb[:, p, 0:2, :], sa_ps[:, 0:2 * T].rearrange("p (i t) -> p i t", i=2),
                                       ACT.Copy).then_inc(c_sa, 1)
                        act.wait_ge(s_sbt, n + 1)
                        act.activation(s_sb[:, p, 2, :], sb_ps[:, 0:T], ACT.Copy).then_inc(c_sb, 1)

                    def exps(b, p):
                        n = 4 * b + p
                        wait(act, p_prob, 3 * (n - NP) + 3)
                        wait(act, d_rz, n - NP + 1)
                        for i in range(NT):
                            act.wait_ge(p_nb, 3 * n + i + 1)
                            if i == 0:
                                act.wait_ge(c_sb, n + 1)
                            act.activation(ex[:, p, i, :], s_sb[:, p, i, :], ACT.Exp, scale=SCALE,
                                           bias=nbias[:, p, i:i + 1], accum_out=zsum[:, p, i:i + 1])\
                               .then_inc(c_e, 1)

                    def copy_turned(b, p):
                        n = 4 * b + p
                        wait(act, s_av, n)
                        act.wait_ge(s_tpa, n + 1)
                        act.activation(pt[:, 0:2, :, :], tp_ps[0:KC, :].rearrange("p (i c q) -> p i c q", i=2, c=2),
                                       ACT.Copy).then_inc(c_tpa, 1)
                        act.wait_ge(s_tpb, n + 1)
                        act.activation(pt[:, 2, :, :], ln_ps[0:KC, 0:2 * P].rearrange("p (c q) -> p c q", c=2),
                                       ACT.Copy).then_inc(c_tpb, 1)

                    def copy_sums(b):
                        act.wait_ge(s_av, 4 * b + 4)
                        act.activation(ot[:, :, :], out_ps[:, 0:2 * T].rearrange("p (h t) -> p h t", h=2),
                                       ACT.Copy).then_inc(c_o, 1)

                    def copy_product(b):
                        act.wait_ge(s_wo, b + 1)
                        act.activation(pr[:, :], out_ps[:, 0:T], ACT.Copy).then_inc(c_pr, 1)

                    def copy_values(b):
                        wait(act, s_av, 4 * b)
                        act.wait_ge(s_v, b + 1)
                        act.activation(vt[:, :, :], v_ps[0:KC, :].rearrange("p (c d) -> p c d", c=2), ACT.Copy)\
                           .then_inc(c_v, 1)

                    def body(b, prev, nxt):
                        copy_scores(b, 2)
                        exps(b, 0)
                        if nxt:
                            hidden(b + 1, 0)
                        copy_scores(b, 3)
                        if prev:
                            copy_turned(b - 1, 2)
                        if nxt:
                            hidden(b + 1, 1)
                            output(b + 1, 0)
                        if prev:
                            copy_turned(b - 1, 3)
                        if nxt:
                            output(b + 1, 1)
                        exps(b, 1)
                        if prev:
                            copy_sums(b - 1)
                        copy_values(b)
                        if nxt:
                            squares(b + 1)
                        if prev:
                            copy_product(b - 1)
                        copy_turned(b, 0)
                        if nxt:
                            inverse_root(b + 1)
                        exps(b, 2)
                        if nxt:
                            copy_qk(b + 1)
                        copy_turned(b, 1)
                        if nxt:
                            copy_scores(b + 1, 0)
                            copy_scores(b + 1, 1)
                        exps(b, 3)

                    hidden(0, 0)
                    hidden(0, 1)
                    output(0, 0)
                    output(0, 1)
                    squares(0)
                    inverse_root(0)
                    copy_qk(0)
                    copy_scores(0, 0)
                    copy_scores(0, 1)
                    iterations(act, body)
                    copy_turned(B - 1, 2)
                    copy_turned(B - 1, 3)
                    copy_sums(B - 1)
                    copy_product(B - 1)

                @block.vector
                def _(dve):
                    def combine(b):
                        wait(dve, d_h2, 2 * b)
                        dve.tensor_copy(gcur[:, :], gates[:, 2 * b:2 * b + 2] if isinstance(b, int)
                                        else gates[:, bass.ds(2 * b, 2)]).then_inc(d_g, 1)
                        dve.wait_ge(d_g, b + 1)
                        for k in range(KSEL):
                            dve.wait_ge(c_eo, 2 * b + k + 1)
                            if k:
                                dve.wait_ge(d_h2, 2 * b + 1)
                            dve.scalar_tensor_tensor(h_res2[:, cols(b)], eo[:, k, :], gcur[:, k:k + 1],
                                                     (h_res2 if k else h_res)[:, cols(b)], ALU.mult, ALU.add)\
                               .then_inc(d_h2, 1)

                    def top(b, p, between=None):
                        n, r = 4 * b + p, p
                        step = OPS * n
                        for rnd in range(TOPK // 8):
                            if rnd == 2 and between:
                                between()
                            for i in range(NT):
                                if rnd:
                                    wait_alone(dve, d_top, step + 6 * rnd - 3 + i + 1)
                                else:
                                    wait(dve, p_nb, 3 * (n - NP) + i + 1)
                                    wait_alone(dve, c_sa if i < 2 else c_sb, n + 1)
                                dve.max(m8[:, r, i, rnd, :], (rest if rnd else s_sb)[:, r, i, :]).then_inc(d_top, 1)
                            for i in range(NT):
                                if not rnd:
                                    wait(dve, p_prob, 3 * (n - NP) + i + 1)
                                wait_alone(dve, d_top, step + 6 * rnd + i + 1)
                                dve.match_replace(rest[:, r, i, :], m8[:, r, i, rnd, :],
                                                  (rest if rnd else s_sb)[:, r, i, :], NEG).then_inc(d_top, 1)

                    def mask(b, p):
                        n = 4 * b + p
                        dve.wait_ge(c_e, 3 * n + 3)
                        dve.reciprocal(rz[:, p, :], zsum[:, p, :]).then_inc(d_rz, 1)
                        for i in range(NT):
                            dve.wait_ge(d_rz, n + 1)
                            dve.wait_ge(d_top, OPS * n + 21 + i + 1)
                            dve.tensor_scalar(keep[:, p, i, :], rest[:, p, i, :], NEG, rz[:, p, i:i + 1],
                                              ALU.is_equal, ALU.mult).then_inc(d_keep, 1)

                    def body(b, prev, nxt):
                        top(b, 0, (lambda: mask(b - 1, 3)) if prev else None)
                        top(b, 1, lambda: mask(b, 0))
                        if nxt:
                            combine(b + 1)
                        top(b, 2, lambda: mask(b, 1))
                        top(b, 3, lambda: mask(b, 2))

                    combine(0)
                    iterations(dve, body)
                    mask(B - 1, 3)

                @block.gpsimd
                def _(pool):
                    def bias(b, p):
                        n, r = 4 * b + p, p
                        for i in range(NT):
                            wait(pool, c_e, 3 * (n - NP) + i + 1)
                            wait_alone(pool, d_top, OPS * n + i + 1)
                            pool.tensor_scalar(nbias[:, r, i:i + 1], m8[:, r, i, 0, 0:1], -SCALE, None, ALU.mult)\
                                .then_inc(p_nb, 1)

                    def kept(b, p):
                        n, r = 4 * b + p, p
                        for i in range(NT):
                            if p < NP - 1:
                                wait(pool, s_tpb, n - NP + 1)
                            pool.wait_ge(d_keep, 3 * n + i + 1)
                            pool.tensor_tensor(prob[:, r, i, :], keep[:, r, i, :], ex[:, r, i, :], ALU.mult)\
                                .then_inc(p_prob, 1)

                    def residual(b):
                        wait_alone(pool, c_pr, b + 1)
                        pool.tensor_tensor(h_res3[:, cols(b)], pr[:, :], h_res2[:, cols(b)], ALU.add).then_inc(p_h3, 1)

                    def norm(b):
                        wait(pool, s_v, b)
                        pool.wait_ge(c_rstd, b + 1)
                        pool.tensor_tensor(xn[:, :], xc[:, :], rstd[:, :], ALU.mult).then_inc(p_xn, 1)

                    def body(b, prev, nxt):
                        bias(b, 0)
                        if prev:
                            kept(b - 1, 3)
                        bias(b, 1)
                        kept(b, 0)
                        bias(b, 2)
                        if nxt:
                            norm(b + 1)
                        kept(b, 1)
                        if prev:
                            residual(b - 1)
                        bias(b, 3)
                        kept(b, 2)

                    pool.memset(empty[:, :], 0.0).then_inc(s_empty, 1)
                    norm(0)
                    iterations(pool, body)
                    kept(B - 1, 3)
                    residual(B - 1)

        scr_y = nc.dram_tensor("scr_y", (NBLK * P, P), F32).ap()
        b2s = sb("b2s", [1, NE, P])
        xt = sb("xt", [P, NTT, P])
        ht = sb("ht", [P, NTT, P])
        slot = sb("slot", [P, NTT], U32)
        bexp = sb("bexp", [1, NBLK], U32)
        one_row = sb("one_row", [1, P])
        s_b2, s_slot, s_bexp, s_xt, s_ht, s_row = (sem(n) for n in (
            "s_b2", "s_slot", "s_bexp", "s_xt", "s_ht", "s_row"))
        with ExitStack() as rst:
            def rb(name, shape, dt=F32):
                return rst.enter_context(nc.sbuf_tensor(name, shape, dt))

            def rsem(name):
                return ctx.enter_context(nc.semaphore("r_" + name))

            every = [P, NTT, NE]
            wr_sb = rb("wr_sb", [P, NE])
            br_sb = rb("br_sb", [P, NE])
            cwr = rb("cwr", [P, NE])
            sq = rb("sq4", [P, NTT, P])
            ssum = rb("ssum", [P, NTT])
            lnv = rb("lnv4", [P, NTT])
            rstd = rb("rstd4", [P, NTT])
            lgt = rb("lgt", every)
            mx = rb("mx", [P, NTT])
            hit = rb("hit", every)
            hit16 = rb("hit16", [P, NTT + 1, NE], BF16)
            tri16 = rb("tri16", [P, 2, P], BF16)
            over = rb("over", [P, NE, NTT])
            nblk = rb("nblk", [P, NE])
            base = rb("base", [P, NE])
            upto = rb("upto", [P, NE])
            pairs = rb("pairs", [P, NE, NE])
            place = rb("place", every)
            placef = rb("placef", [P, NTT])
            past = rb("past", [P, NBLK, NE])
            bexpf = rb("bexpf", [P, NBLK])
            xc_ps, lg_ps, ht_ps, rank_ps = bank[0:3], bank[3], bank[4:7], bank[7]
            s_wr, s_cwr, s_cwc, s_cen, s_sq, s_ln, s_std, s_ch, s_lg, s_hit, s_tri, s_rank, s_tr = (
                rsem(n) for n in ("weights", "cwr", "cwcopy", "cen", "sq", "ln", "std", "chain", "logits", "hit",
                                  "tri", "rank", "turned"))

            with nc.Block() as block:
                @block.sync
                def _(sp):
                    sp.dma_start(wr_sb[:, :], wr).then_inc(s_wr, 16)
                    sp.dma_start(br_sb[:, :], br).then_inc(s_wr, 16)
                    sp.dma_start(b2s[:, :, :], b2rows).then_inc(s_b2, 16)

                @block.gpsimd
                def _(pool):
                    pool.memset(hit16[:, :, :], 0.0)
                    pool.tensor_copy(tri16[:, :, :], cst[:, K_TRI:K_TRI + 2 * P].rearrange("p (a q) -> p a q", a=2))\
                        .then_inc(s_tri, 1)
                    pool.memset(one_row[:, :], 1.0).then_inc(s_row, 1)

                @block.tensor
                def _(pe):
                    pe.wait_ge(s_wr, 32)
                    pe.matmul(lg_ps[:, NTT * NE:NTT * NE + NE], center, wr_sb[:, :], start=True, stop=True)\
                      .then_inc(s_cwr, 1)
                    for i in range(NTT):
                        pe.matmul(xc_ps[i // 4][:, P * (i % 4):P * (i % 4) + P], h_res3[:, P * i:P * i + P], center,
                                  start=True, stop=True).then_inc(s_cen, 1)
                    pe.wait_ge(s_cwc, 1)
                    for i in range(NTT):
                        last = pe.matmul(lg_ps[:, NE * i:NE * i + NE], h_res3[:, P * i:P * i + P], cwr[:, :],
                                         start=True, stop=True)
                    last.then_inc(s_lg, 1)
                    for i in range(NTT):
                        mm = pe.transpose(ht_ps[i // 4][:, P * (i % 4):P * (i % 4) + P], h_res3[:, P * i:P * i + P],
                                          ident)
                        if i % 4 == 3:
                            mm.then_inc(s_tr, 1)
                    pe.wait_ge(s_hit, 1)
                    pe.wait_ge(s_tri, 1)
                    last = pe.matmul(rank_ps[:, 0:(NTT + 1) * NE], tri16[:, 0, :], hit16[:, :, :], start=True,
                                     stop=False, skip_group_check=True)
                    for i in range(NTT):
                        last = pe.matmul(rank_ps[:, NE * (i + 1):NE * (NTT + 1)].rearrange("p (i e) -> p i e", e=NE),
                                         tri16[:, 1, :],
                                         hit16[:, i, :].unsqueeze(1).to_broadcast([P, NTT - i, NE]),
                                         start=False, stop=(i == NTT - 1), skip_group_check=True)
                    last.then_inc(s_rank, 1)

                @block.scalar
                def _(act):
                    for i in range(NTT):
                        act.wait_ge(s_cen, 4 * (i // 4) + 4)
                        act.activation(sq[:, i, :], xc_ps[i // 4][:, P * (i % 4):P * (i % 4) + P], ACT.Square,
                                       accum_out=ssum[:, i:i + 1]).then_inc(s_sq, 1)
                    act.wait_ge(s_sq, NTT)
                    act.activation(lnv[:, :], ssum[:, :], ACT.Ln, scale=1.0 / P, bias=epsc[:, 0:1]).then_inc(s_ln, 1)
                    act.wait_ge(s_ln, 1)
                    act.activation(rstd[:, :], lnv[:, :], ACT.Exp, scale=-0.5).then_inc(s_std, 1)
                    for g in range(NTT // 4):
                        act.wait_ge(s_tr, g + 1)
                        act.activation(ht[:, 4 * g:4 * g + 4, :], ht_ps[g][:, :].rearrange("p (i f) -> p i f", i=4),
                                       ACT.Copy).then_inc(s_ht, 1)

                @block.vector
                def _(dve):
                    n = 0

                    def link(ins):
                        nonlocal n
                        n += 1
                        ins.then_inc(s_ch, 1)
                        dve.wait_ge(s_ch, n)

                    dve.wait_ge(s_cwr, 1)
                    dve.tensor_copy(cwr[:, :], lg_ps[:, NTT * NE:NTT * NE + NE]).then_inc(s_cwc, 1)
                    dve.wait_ge(s_lg, 1)
                    dve.wait_ge(s_wr, 32)
                    dve.wait_ge(s_std, 1)
                    link(dve.tensor_tensor(lgt[:, :, :], lg_ps[:, 0:NTT * NE].rearrange("p (i e) -> p i e", e=NE),
                                           rstd[:, :].unsqueeze(2).to_broadcast(every), ALU.mult))
                    link(dve.tensor_tensor(lgt[:, :, :], lgt[:, :, :],
                                           br_sb[:, :].unsqueeze(1).to_broadcast(every), ALU.add))
                    link(dve.tensor_reduce(mx[:, :], lgt[:, :, :], AX_X, ALU.max))
                    link(dve.tensor_tensor(hit[:, :, :], lgt[:, :, :], mx[:, :].unsqueeze(2).to_broadcast(every),
                                           ALU.is_ge))
                    link(dve.tensor_tensor(hit[:, :, :], hit[:, :, :],
                                           cst[:, K_DESC:K_DESC + NE].unsqueeze(1).to_broadcast(every), ALU.mult))
                    link(dve.tensor_reduce(mx[:, :], hit[:, :, :], AX_X, ALU.max))
                    dve.wait_ge(s_tri, 1)
                    dve.tensor_tensor(hit16[:, 0:NTT, :], hit[:, :, :], mx[:, :].unsqueeze(2).to_broadcast(every),
                                      ALU.is_equal).then_inc(s_hit, 1)
                    dve.wait_ge(s_hit, 1)
                    for g in range(NTT // 4):
                        dve.tensor_tensor(xt[:, 4 * g:4 * g + 4, :], xc_ps[g][:, :].rearrange("p (i f) -> p i f", i=4),
                                          rstd[:, 4 * g:4 * g + 4].unsqueeze(2).to_broadcast([P, 4, P]), ALU.mult)\
                           .then_inc(s_xt, 1)
                    dve.wait_ge(s_rank, 1)
                    link(dve.tensor_tensor(over[:, :, :], rank_ps[:, NTT * NE:(NTT + 1) * NE].unsqueeze(2)
                                           .to_broadcast([P, NE, NTT]),
                                           cst[:, K_MULT:K_MULT + NTT].unsqueeze(1).to_broadcast([P, NE, NTT]),
                                           ALU.is_gt))
                    link(dve.tensor_reduce(nblk[:, :], over[:, :, :], AX_X, ALU.add))
                    link(dve.tensor_tensor(pairs[:, :, :], nblk[:, :].unsqueeze(1).to_broadcast([P, NE, NE]),
                                           cst[:, K_BEFORE:K_BEFORE + NE * NE].rearrange("p (e f) -> p e f", e=NE),
                                           ALU.mult))
                    link(dve.tensor_reduce(base[:, :], pairs[:, :, :], AX_X, ALU.add))
                    link(dve.tensor_tensor(place[:, :, :], rank_ps[:, 0:NTT * NE].rearrange("p (i e) -> p i e", e=NE),
                                           base[:, :].unsqueeze(1).to_broadcast(every), ALU.add))
                    link(dve.tensor_tensor(place[:, :, :], place[:, :, :], hit16[:, 0:NTT, :], ALU.mult))
                    link(dve.tensor_reduce(placef[:, :], place[:, :, :], AX_X, ALU.add))
                    dve.tensor_copy(slot[:, :], placef[:, :]).then_inc(s_slot, 1)
                    link(dve.tensor_tensor(pairs[:, :, :], nblk[:, :].unsqueeze(1).to_broadcast([P, NE, NE]),
                                           cst[:, K_UPTO:K_UPTO + NE * NE].rearrange("p (e f) -> p e f", e=NE),
                                           ALU.mult))
                    link(dve.tensor_reduce(upto[:, :], pairs[:, :, :], AX_X, ALU.add))
                    link(dve.tensor_tensor(past[:, :, :],
                                           cst[:, K_BLOCK:K_BLOCK + NBLK].unsqueeze(2).to_broadcast([P, NBLK, NE]),
                                           upto[:, :].unsqueeze(1).to_broadcast([P, NBLK, NE]), ALU.is_ge))
                    link(dve.tensor_reduce(bexpf[:, :], past[:, :, :], AX_X, ALU.add))
                    dve.tensor_scalar(bexp[:, :], bexpf[0:1, :], float(NE - 1), None, ALU.min).then_inc(s_bexp, 1)

        with ExitStack() as fst:
            def fb(name, shape, dt=F32):
                return fst.enter_context(nc.sbuf_tensor(name, shape, dt))

            def fsem(name):
                return ctx.enter_context(nc.semaphore("f_" + name))

            R = 3
            W1W = HID + NJ
            xs = fb("xs", [P, R, P])
            xf = fb("xf", [P, R, P])
            w1c = fb("w1c", [P, R, W1W])
            hid = fb("hid4", [P, R, NJ, P])
            ys = fb("ys", [P, R, P])
            yt = fb("yt", [P, NTT, P])
            res = fb("res", [P, NTT, P])
            h_ps, y_ps, x_ps = bank[0:3], bank[3:6], bank[6]
            s_put = fsem("scattered")
            s_ld = [fsem(f"loaded{r}") for r in range(R)]
            s_st = [fsem(f"stored{r}") for r in range(R)]
            s_got = [fsem(f"gathered{g}") for g in range(NTT // 4)]
            s_turn, s_h, s_y, c_relu, d_w, d_x, d_y, d_res, s_out = (fsem(n) for n in (
                "turned", "hidden_ps", "y_ps", "relu", "weights", "x", "y", "result", "out"))

            def wait(eng, s, value):
                if not isinstance(value, int) or value > 0:
                    eng.wait_ge(s, value)

            def wait_alone(eng, s, value):
                if not isinstance(value, int) or value > 0:
                    eng.wait_ge(s, value)
                    eng.nop(nofuse=True)

            ROUNDS = (NBLK - 1) // R

            def number(g, j):
                return R * g + (1 + j) if not isinstance(g, int) else 1 + R * g + j

            def uses(g, j):
                return g + 1 if j == R - 1 else g

            def back(g, j, n):
                return (g, j - n) if j >= n else (g - 1, j - n + R)

            def after(g, j):
                return (g, j + 1) if j < R - 1 else (g + 1, 0)

            def blocks(eng, step):
                step(-1, R - 1)
                for j in range(R):
                    step(0, j)
                with eng.Fori(1, ROUNDS - 1) as g:
                    for j in range(R):
                        step(g, j)
                for j in range(R):
                    step(ROUNDS - 1, j)

            def rows(k):
                return slice(k * P, (k + 1) * P) if isinstance(k, int) else bass.ds(k * P, P)

            def expert_of(eng, k):
                return eng.value_load(bexp[0:1, k:k + 1] if isinstance(k, int) else bexp[0:1, bass.ds(k, 1)],
                                      min_val=0, max_val=NE - 1)

            with nc.Block() as block:
                @block.gpsimd
                def _(pool):
                    pool.wait_ge(s_slot, 1)
                    pool.wait_ge(s_xt, NTT // 4)
                    pool.wait_ge(s_zero_x, 16)
                    for i in range(NTT):
                        pool.indirect_dma_start(scr_x, bass.IndirectOffsetOnAxis(ap=slot[:, i:i + 1], axis=0),
                                                xt[:, i, :], None).then_inc(s_put, 16)
                    for r in range(R):
                        pool.wait_ge(s_st[r], 16 * (ROUNDS + int(r == R - 1)))
                    for i in range(NTT):
                        pool.indirect_dma_start(yt[:, i, :], None, scr_y,
                                                bass.IndirectOffsetOnAxis(ap=slot[:, i:i + 1], axis=0))\
                            .then_inc(s_got[i // 4], 16)

                @block.sync
                def _(sp):
                    sp.wait_ge(s_put, 16 * NTT)

                    def step(g, r):
                        k = number(g, r)
                        wait(sp, s_turn, k - R + 1)
                        sp.dma_start(xs[:, r, :], scr_x[rows(k), :]).then_inc(s_ld[r], 16)

                    blocks(sp, step)
                    for g in range(NTT // 4):
                        sp.wait_ge(d_res, g + 1)
                        sp.dma_start(out.rearrange("(i p) f -> p i f", p=P)[:, 4 * g:4 * g + 4, :],
                                     res[:, 4 * g:4 * g + 4, :]).then_inc(s_out, 16)
                    sp.wait_ge(s_out, 16 * (NTT // 4))

                @block.tensor
                def _(pe):
                    def turn(g, r):
                        k = number(g, r)
                        wait_alone(pe, d_x, k)
                        wait_alone(pe, s_ld[r], 16 * (uses(g, r) + 1))
                        pe.transpose(x_ps[:, 0:P], xs[:, r, :], ident).then_inc(s_turn, 1)

                    def hidden(g, r):
                        k = number(g, r)
                        wait_alone(pe, c_relu, k - R + 1)
                        wait_alone(pe, d_w, k + 1)
                        wait_alone(pe, d_x, k + 1)
                        for j in range(NJ):
                            last = pe.matmul(h_ps[r][:, j * P:(j + 1) * P], w1c[:, r, j * P:(j + 1) * P], xf[:, r, :],
                                             start=True, stop=True)
                        last.then_inc(s_h, 1)

                    def output(g, r):
                        k = number(g, r)
                        e = expert_of(pe, k)
                        wait_alone(pe, d_y, k - R + 1)
                        wait_alone(pe, c_relu, k + 1)
                        for j in range(NJ):
                            pe.matmul(y_ps[r][:, 0:P], hid[:, r, j, :],
                                      xw[:, bass.ds(e, 1), W1W + j * P:W1W + (j + 1) * P].rearrange("p e f -> p (e f)"),
                                      start=(j == 0), stop=False)
                        pe.matmul(y_ps[r][:, 0:P], one_row[:, :], b2s[:, bass.ds(e, 1), :].rearrange("p e f -> p (e f)"),
                                  start=False, stop=True).then_inc(s_y, 1)

                    def step(g, r):
                        k = number(g, r)
                        hidden(g, r)
                        if not isinstance(k, int) or k < NBLK - 1:
                            turn(*after(g, r))
                        if not isinstance(k, int) or k > 0:
                            output(*back(g, r, 1))

                    pe.wait_ge(s_b2, 16)
                    pe.wait_ge(s_xw, 16)
                    pe.wait_ge(s_row, 1)
                    pe.wait_ge(s_bexp, 1)
                    turn(-1, R - 1)
                    blocks(pe, step)
                    output(ROUNDS - 1, R - 1)

                @block.scalar
                def _(act):
                    def store(g, r):
                        k = number(g, r)
                        act.wait_ge(d_y, k + 1)
                        act.dma_start(scr_y[rows(k), :], ys[:, r, :]).then_inc(s_st[r], 16)

                    def step(g, r):
                        k = number(g, r)
                        wait(act, s_y, k - R + 1)
                        act.wait_ge(s_h, k + 1)
                        for j in range(NJ):
                            ins = act.activation(hid[:, r, j, :], h_ps[r][:, j * P:(j + 1) * P], ACT.Relu,
                                                 bias=w1c[:, r, HID + j:HID + j + 1])
                        ins.then_inc(c_relu, 1)
                        if not isinstance(k, int) or k > 1:
                            store(*back(g, r, 2))

                    blocks(act, step)
                    store(ROUNDS - 1, R - 2)
                    store(ROUNDS - 1, R - 1)

                @block.vector
                def _(dve):
                    def weights(g, r):
                        k = number(g, r)
                        e = expert_of(dve, k)
                        wait_alone(dve, c_relu, k - R + 1)
                        dve.tensor_copy(w1c[:, r, :],
                                        xw[:, bass.ds(e, 1), 0:W1W].rearrange("p e f -> p (e f)")).then_inc(d_w, 1)

                    def turned(g, r):
                        k = number(g, r)
                        wait(dve, s_h, k - R + 1)
                        dve.wait_ge(s_turn, k + 1)
                        dve.tensor_copy(xf[:, r, :], x_ps[:, 0:P]).then_inc(d_x, 1)

                    def result(g, r):
                        k = number(g, r)
                        wait(dve, s_st[r], 16 * uses(g, r))
                        dve.wait_ge(s_y, k + 1)
                        dve.tensor_copy(ys[:, r, :], y_ps[r][:, 0:P]).then_inc(d_y, 1)

                    def step(g, r):
                        k = number(g, r)
                        weights(g, r)
                        turned(g, r)
                        if not isinstance(k, int) or k > 1:
                            result(*back(g, r, 2))

                    dve.wait_ge(s_xw, 16)
                    dve.wait_ge(s_bexp, 1)
                    blocks(dve, step)
                    result(ROUNDS - 1, R - 2)
                    result(ROUNDS - 1, R - 1)
                    for g in range(NTT // 4):
                        dve.wait_ge(s_ht, g + 1)
                        dve.wait_ge(s_got[g], 64)
                        dve.tensor_tensor(res[:, 4 * g:4 * g + 4, :], yt[:, 4 * g:4 * g + 4, :],
                                          ht[:, 4 * g:4 * g + 4, :], ALU.add).then_inc(d_res, 1)


def layouts(a):
    f = {k: np.asarray(v) for k, v in a.items()}
    side = T_IMG_SIDE = P // PATCH
    d = {}
    d["xT"] = f["x"].reshape(B, side, PATCH, side, PATCH).transpose(2, 4, 1, 3, 0).reshape(PATCH * PATCH, NIMG)
    d["txtT"] = f["txt"].transpose(2, 1, 0).reshape(P, T_TXT * B)

    def halves(v):
        return v.reshape(KIN, P).T

    eo = [f[f"L0_tok_eps_out{w}"] for w in (1, 2)]
    d["noise"] = np.concatenate([np.broadcast_to(np.concatenate(eo), (P, 2 * P)),
                                 halves(f["L0_tok_eps_in1"]), halves(f["L0_tok_eps_in2"]),
                                 np.stack(eo, 1)], 1)
    d["cols"] = np.stack([f["L0_tok_W1_b"], f["L0_tok_W1_sb"], f["L0_tok_W2_b"], f["L0_tok_W2_sb"],
                          f["L0_tok_W3_b"], f["L0_ffn_attn_w"][:, 0], np.broadcast_to(f["L0_ffn_attn_b"], (P,))], 1)
    d["tokw"] = np.stack([f["L0_tok_" + n].T.reshape(KIN, P, P).transpose(1, 0, 2)
                          for n in ("W1_w", "W1_sw", "W2_w", "W2_sw")], 1)
    d["w3T"] = f["L0_tok_W3_w"].T
    d["wihT"] = f["L0_attn_W_ih"].T
    d["whhT"] = f["L0_attn_W_hh"].T
    d["bias3"] = np.broadcast_to(np.stack([f["L0_attn_b_ih"], f["L0_attn_b_hh"]]), (3, 2, 4 * P))
    pos = np.arange(T_IMG, dtype=np.float32)[:, None]
    div = np.exp(np.arange(0, P, 2, dtype=np.float32) * np.float32(-np.log(10000.0) / P))
    ang = (pos * div).astype(np.float32)
    pe = np.stack([np.sin(ang), np.cos(ang)], -1).reshape(T_IMG, P).astype(np.float32)
    eye = np.eye(P, dtype=np.float32)
    avg = np.full((P, P), 1.0 / P, np.float32)
    desc = np.broadcast_to(NE - np.arange(NE, dtype=np.float32), (P, NE))
    expert = np.arange(NE)
    before = P * (expert[None, :] < expert[:, None])
    upto = expert[None, :] <= expert[:, None]
    rows = [np.broadcast_to(v.reshape(-1).astype(np.float32), (P, v.size))
            for v in (P * np.arange(NTT), before, upto, np.arange(NBLK))]
    earlier = np.triu(np.ones((P, P), np.float32), 1)
    d["consts"] = np.concatenate([eye, eye - avg, avg, pe.T, desc, earlier, np.ones((P, P), np.float32)] + rows, 1)
    d["gate_w"] = f["L0_ffn_gate_w"]
    d["gate_b"] = np.broadcast_to(f["L0_ffn_gate_b"], (B, NE))

    def expert_rows(w1, b1, w2, b2):
        return np.concatenate([w1, w2.reshape(NE, NJ, P, P).transpose(0, 2, 1, 3).reshape(NE, P, HID),
                               b1.reshape(NE, NJ, P).transpose(0, 2, 1), b2[:, :, None]], 2)

    d["expert0"] = expert_rows(f["L0_ffn_w1"], f["L0_ffn_b1"], f["L0_ffn_w2"], f["L0_ffn_b2"])
    w = f["L1_attn_W_qkv"].reshape(HEADS, 3, HD, P).transpose(3, 1, 0, 2)
    d["wqkvT"] = np.pad(w, ((0, 0), (0, 0), (0, 0), (0, HPAD - HD))).reshape(P, 3, HEADS * HPAD)
    wo = f["L1_attn_W_o"].T.reshape(HEADS, HD, P)
    d["woT"] = np.pad(wo, ((0, 0), (0, HPAD - HD), (0, 0))).reshape(2, P, P).transpose(1, 0, 2)
    d["wr"] = f["L1_ffn_Wr"]
    d["br"] = np.broadcast_to(f["L1_ffn_br"], (P, NE))
    d["expert1"] = expert_rows(f["L1_ffn_W1"], f["L1_ffn_b1"], f["L1_ffn_W2"], f["L1_ffn_b2"]).transpose(1, 0, 2)
    e1 = d["expert1"]
    d["expert1"] = np.concatenate([e1[:, :, :HID], e1[:, :, 2 * HID:2 * HID + NJ], e1[:, :, HID:2 * HID]], 2)
    d["b2rows"] = f["L1_ffn_b2"][None]
    return {k: np.ascontiguousarray(v) for k, v in d.items()}


def kernel(**inputs):
    import concourse.bacc as bacc
    from concourse.bass_utils import run_bass_kernel_spmd

    nc = bacc.Bacc("TRN2", target_bir_lowering=False, num_devices=1)
    arrays = layouts(inputs)
    aps = {n: nc.dram_tensor(n, v.shape, mybir.dt.from_np(v.dtype), kind="ExternalInput").ap()
           for n, v in arrays.items()}
    out = nc.dram_tensor("out", (N, P), F32, kind="ExternalOutput").ap()
    build(nc, out=out, **aps)
    got = run_bass_kernel_spmd(nc, [arrays], core_ids=[0]).results[0]["out"]
    return got.reshape(B, T, P)
```

```python
from contextlib import ExitStack

import numpy as np

import concourse.bass as bass
from concourse import mybir

F32 = mybir.dt.float32
BF16 = mybir.dt.bfloat16
F16 = mybir.dt.float16
U32 = mybir.dt.uint32
ALU = mybir.AluOpType
ACT = mybir.ActivationFunctionType
AX_X = mybir.AxisListType.X

P = 128
B = 8
T_IMG = 64
T_TXT = 128
T = T_IMG + T_TXT
N = B * T
NIMG = B * T_IMG
PATCH = 16
KIN = PATCH * PATCH // P
EPS = 1e-5
HEADS = 8
HD = P // HEADS
HPAD = 32
TOPK = 32
NE = 8
HID = 512
NJ = HID // P
KSEL = 2
W1W = HID + NJ
XW = W1W + HID + 1
G = 4
GB = G * B
NLN = 2 * T
KC = T // 2
NTT = N // P
NBLK = NTT + NE - 1
XR = 2 * P + 1
CW = P + NE
TPB = 512 // CW
EARLY = (B - 2) * T // P // TPB * TPB
NEG = -3.0e38
SCALE = float(HD) ** -0.5

(C_W1B, C_W1SB, C_W2B, C_W2SB, C_W3B, C_AW, C_AB) = range(7)
NCOL = 7
NZ_EO, NZ_EI, NZ_EOC = 0, 2 * P, 2 * P + 2 * KIN
NNZ = NZ_EOC + 2
K_ID, K_CEN, K_AVG, K_PE, K_DESC = 0, P, 2 * P, 3 * P, 3 * P + T_IMG
K_TRI = K_DESC + NE
K_MULT = K_TRI + 2 * P
K_BEFORE = K_MULT + NTT
K_UPTO = K_BEFORE + NE * NE
K_BLOCK = K_UPTO + NE * NE
K_EMPTY = K_BLOCK + NBLK
K_TOKEN = K_EMPTY + NBLK
NK = K_TOKEN + NTT


def build(nc, xT, txtT, noise, cols, tokw, w3T, wihT, whhT, bias3, consts, gate_w, gate_b, expert0,
          wqkvT, woT, wr, br, expert1, b2rows, out):
    with ExitStack() as ctx:
        def sb(name, shape, dt=F32):
            return ctx.enter_context(nc.sbuf_tensor(name, shape, dt))

        def sem(name):
            return ctx.enter_context(nc.semaphore(name))

        bank = [ctx.enter_context(nc.psum_tensor(f"bank{i}", [P, 512], F32)) for i in range(8)]

        scr_x = nc.dram_tensor("scr_x", (NBLK * P, XR), F32).ap()
        s_empty = sem("s_empty")
        cst = sb("cst", [P, NK])
        col = sb("col", [P, NCOL])
        ident, center, average = cst[:, K_ID:K_ID + P], cst[:, K_CEN:K_CEN + P], cst[:, K_AVG:K_AVG + P]
        epsc = sb("epsc", [P, 1])
        h_in = sb("h_in", [P, N])
        xn_in = sb("xn_in", [P, N + GB])
        hseq = sb("hseq", [P, N])
        wi = sb("wi", [P, 4 * P])
        wh = [sb(f"wh{k}", [P, 4 * P], BF16) for k in range(3)]
        bias_parts = sb("bias_parts", [3, 4 * P], BF16)
        ones3 = sb("ones3", [3, GB], BF16)

        s_const, s_x, s_txt, s_tokw, s_noise, s_lstmw = (sem(n) for n in (
            "s_const", "s_x", "s_txt", "s_tokw", "s_noise", "s_lstmw"))

        with ExitStack() as tok:
            def tb(name, shape, dt=F32):
                return tok.enter_context(nc.sbuf_tensor(name, shape, dt))

            def tsem(name):
                return ctx.enter_context(nc.semaphore(name))

            x_sb = tb("x_sb", [P, KIN, NIMG])
            nz = tb("nz", [P, NNZ])
            nabs = tb("nabs", [P, NNZ])
            nsgn = tb("nsgn", [P, NNZ])
            tw = tb("tw", [P, 4, KIN, P])
            wn = tb("wn", [P, 2, KIN, P])
            bn = tb("bn", [P, 2])
            w3 = tb("w3", [P, P])
            gt = tb("gt", [P, NIMG])
            gz = tb("gz", [P, NIMG])
            ge = tb("ge", [P, NIMG])
            gn = tb("gn", [P, NIMG])
            gd = tb("gd", [P, NIMG])
            u = tb("u", [P, NIMG])
            sq = tb("sq", [P, 3, 512])
            lnv = tb("lnv0", [P, 3, 512])
            rstd = tb("rstd0", [P, 3, 512])
            wh_raw = tb("wh_raw", [P, 4 * P])
            wh_r1 = tb("wh_r1", [P, 4 * P])
            wh_r2 = tb("wh_r2", [P, 4 * P])
            b_raw = tb("b_raw", [3, 2, 4 * P])
            b_r1 = tb("b_r1", [3, 4 * P])
            b_r2 = tb("b_r2", [3, 4 * P])
            b_p = tb("b_p", [3, 3, 4 * P], BF16)

            s_fill, s_root, s_wn, s_lin, s_clip, s_exp, s_u, s_h, s_dve = (tsem(n) for n in (
                "s_fill", "s_root", "s_wn", "s_lin", "s_clip", "s_exp", "s_u", "s_h", "s_dve"))
            s_cen, s_sq, s_var, s_std, s_img, s_pool = (tsem(n) for n in (
                "s_cen", "s_sq", "s_var", "s_std", "s_img", "s_pool"))
            g_ps, in_ps, h_ps = bank[0], bank[1], bank[2]
            order = [1, 2, 0]
            var_ps = [bank[6], bank[7], bank[0]]
            s_ln, s_col = tsem("s_ln"), tsem("s_col")

            with nc.Block() as block:
                @block.sync
                def _(sp):
                    sp.dma_start(nz[:, :], noise).then_inc(s_noise, 16)
                    sp.dma_start(tw[:, :, :, :], tokw).then_inc(s_tokw, 16)
                    sp.dma_start(x_sb[:, :, :], xT.rearrange("(h p) n -> p h n", p=P)).then_inc(s_x, 16)
                    sp.dma_start(w3[:, :], w3T).then_inc(s_x, 16)
                    sp.dma_start(cst[:, :], consts).then_inc(s_const, 16)
                    sp.dma_start(h_in[:, NIMG:], txtT).then_inc(s_txt, 16)
                    sp.dma_start(wi[:, :], wihT).then_inc(s_lstmw, 16)
                    sp.dma_start(wh_raw[:, :], whhT).then_inc(s_lstmw, 16)
                    sp.dma_start(b_raw[:, :, :], bias3).then_inc(s_lstmw, 16)

                @block.gpsimd
                def _(pool):
                    pool.memset(epsc[:, :], EPS).then_inc(s_fill, 1)
                    pool.memset(xn_in[:, N:N + GB], 0.0)
                    pool.memset(ones3[:, :], 1.0).then_inc(s_fill, 1)
                    n = 0

                    def link(ins):
                        nonlocal n
                        n += 1
                        ins.then_inc(s_pool, 1)
                        pool.wait_ge(s_pool, n)

                    pool.wait_ge(s_lstmw, 48)
                    link(pool.tensor_scalar(wi[:, 2 * P:3 * P], wi[:, 2 * P:3 * P], 2.0, None, ALU.mult))
                    link(pool.tensor_scalar(wh_raw[:, 2 * P:3 * P], wh_raw[:, 2 * P:3 * P], 2.0, None, ALU.mult))
                    link(pool.tensor_copy(wh[0][:, :], wh_raw[:, :]))
                    link(pool.tensor_tensor(wh_r1[:, :], wh_raw[:, :], wh[0][:, :], ALU.subtract))
                    link(pool.tensor_copy(wh[1][:, :], wh_r1[:, :]))
                    link(pool.tensor_tensor(wh_r2[:, :], wh_r1[:, :], wh[1][:, :], ALU.subtract))
                    link(pool.tensor_copy(wh[2][:, :], wh_r2[:, :]))

                @block.scalar
                def _(act):
                    act.dma_start(col[:, :], cols).then_inc(s_col, 16)
                    act.wait_ge(s_noise, 16)
                    act.activation(nabs[:, :], nz[:, :], ACT.Abs).then_inc(s_root, 1)
                    act.activation(nsgn[:, :], nz[:, :], ACT.Sign).then_inc(s_root, 1)
                    act.wait_ge(s_root, 1)
                    act.activation(nabs[:, :], nabs[:, :], ACT.Sqrt).then_inc(s_root, 1)

                    act.preload_act_table_set("natural_log_exp_and_others")

                    def squares(i):
                        act.wait_ge(s_cen, i + 1)
                        act.activation(sq[:, order[i], :], bank[3 + i][:, :], ACT.Square).then_inc(s_sq, 1)

                    def inverse_root(i):
                        c = order[i]
                        act.wait_ge(s_var, i + 1)
                        act.activation(lnv[:, c, :], var_ps[i][:, :], ACT.Ln, bias=epsc[:, 0:1]).then_inc(s_ln, 1)
                        act.wait_ge(s_ln, i + 1)
                        act.activation(rstd[:, c, :], lnv[:, c, :], ACT.Exp, scale=-0.5).then_inc(s_std, 1)

                    act.wait_ge(s_fill, 2)
                    act.wait_ge(s_clip, 2)
                    act.activation(ge[:, :], gz[:, :], ACT.Exp).then_inc(s_exp, 1)
                    squares(0)
                    squares(1)
                    inverse_root(0)
                    inverse_root(1)
                    squares(2)
                    inverse_root(2)
                    act.preload_act_table_set("sigmoid_and_others")

                @block.vector
                def _(dve):
                    n = 0

                    def link(ins):
                        nonlocal n
                        n += 1
                        ins.then_inc(s_dve, 1)
                        dve.wait_ge(s_dve, n)

                    dve.wait_ge(s_root, 3)
                    link(dve.tensor_tensor(nz[:, :], nabs[:, :], nsgn[:, :], ALU.mult))
                    dve.wait_ge(s_tokw, 16)
                    for w in range(2):
                        for h in range(KIN):
                            e = NZ_EI + w * KIN + h
                            last = dve.scalar_tensor_tensor(wn[:, w, h, :], nz[:, NZ_EO + w * P:NZ_EO + (w + 1) * P],
                                                            nz[:, e:e + 1], tw[:, 2 * w + 1, h, :], ALU.mult, ALU.mult)
                    link(last)
                    for w in range(2):
                        dve.tensor_tensor(wn[:, w, :, :], wn[:, w, :, :], tw[:, 2 * w, :, :], ALU.add)\
                           .then_inc(s_wn, 1)
                    dve.wait_ge(s_col, 16)
                    for w in range(2):
                        last = dve.scalar_tensor_tensor(bn[:, w:w + 1], col[:, C_W1SB + 2 * w:C_W1SB + 2 * w + 1],
                                                        nz[:, NZ_EOC + w:NZ_EOC + w + 1],
                                                        col[:, C_W1B + 2 * w:C_W1B + 2 * w + 1], ALU.mult, ALU.add)
                    link(last)
                    dve.wait_ge(s_lin, 1)
                    dve.tensor_scalar(gt[:, :], g_ps[:, :], bn[:, 0:1], None, ALU.add).then_inc(s_clip, 1)
                    dve.tensor_scalar(gz[:, :], g_ps[:, :], bn[:, 0:1], 20.0, ALU.add, ALU.min).then_inc(s_clip, 1)

                    def norm(i):
                        c = order[i]
                        dve.wait_ge(s_std, i + 1)
                        link(dve.tensor_tensor(xn_in[:, 512 * c:512 * c + 512], bank[3 + i][:, :], rstd[:, c, :],
                                               ALU.mult))

                    dve.wait_ge(s_exp, 1)
                    link(dve.scalar_tensor_tensor(gn[:, :], ge[:, :], 2.0, ge[:, :], ALU.add, ALU.mult))
                    link(dve.tensor_scalar(gd[:, :], gn[:, :], 2.0, None, ALU.add))
                    link(dve.reciprocal(gd[:, :], gd[:, :]))
                    link(dve.tensor_tensor(gn[:, :], gn[:, :], gd[:, :], ALU.mult))
                    dve.wait_ge(s_clip, 2)
                    link(dve.tensor_tensor(gt[:, :], gt[:, :], gn[:, :], ALU.mult))
                    dve.wait_ge(s_lin, 2)
                    dve.scalar_tensor_tensor(u[:, :], in_ps[:, :], bn[:, 1:2], gt[:, :], ALU.add, ALU.mult)\
                       .then_inc(s_u, 1)
                    dve.wait_ge(s_h, 1)
                    dve.scalar_tensor_tensor(
                        h_in[:, 0:NIMG].rearrange("p (t b) -> p t b", b=B),
                        h_ps[:, :].rearrange("p (t b) -> p t b", b=B), col[:, C_W3B:C_W3B + 1],
                        cst[:, K_PE:K_PE + T_IMG].unsqueeze(2).to_broadcast([P, T_IMG, B]),
                        ALU.add, ALU.add).then_inc(s_img, 1)
                    norm(0)
                    norm(1)
                    dve.wait_ge(s_lstmw, 48)
                    link(dve.tensor_tensor(b_raw[:, 0, :], b_raw[:, 0, :], b_raw[:, 1, :], ALU.add))
                    link(dve.tensor_scalar(b_raw[:, 0, 2 * P:3 * P], b_raw[:, 0, 2 * P:3 * P], 2.0, None, ALU.mult))
                    link(dve.tensor_copy(b_p[:, 0, :], b_raw[:, 0, :]))
                    link(dve.tensor_tensor(b_r1[:, :], b_raw[:, 0, :], b_p[:, 0, :], ALU.subtract))
                    link(dve.tensor_copy(b_p[:, 1, :], b_r1[:, :]))
                    link(dve.tensor_tensor(b_r2[:, :], b_r1[:, :], b_p[:, 1, :], ALU.subtract))
                    link(dve.tensor_copy(b_p[:, 2, :], b_r2[:, :]))
                    link(dve.tensor_scalar(b_r1[:, :], b_p[:, 0, :], cst[0:3, 0:1], None, ALU.mult))
                    link(dve.scalar_tensor_tensor(b_r2[:, :], b_p[:, 1, :], cst[0:3, 1:2], b_r1[:, :],
                                                  ALU.mult, ALU.add))
                    link(dve.scalar_tensor_tensor(bias_parts[:, :], b_p[:, 2, :], cst[0:3, 2:3], b_r2[:, :],
                                                  ALU.mult, ALU.add))
                    norm(2)

                @block.tensor
                def _(pe):
                    def centered(i):
                        c = order[i]
                        pe.matmul(bank[3 + i][:, :], center, h_in[:, 512 * c:512 * c + 512], start=True, stop=True)\
                          .then_inc(s_cen, 1)

                    def variance(i):
                        pe.wait_ge(s_sq, i + 1)
                        pe.matmul(var_ps[i][:, :], average, sq[:, order[i], :], start=True, stop=True)\
                          .then_inc(s_var, 1)

                    pe.wait_ge(s_const, 16)
                    pe.wait_ge(s_txt, 16)
                    pe.wait_ge(s_x, 32)
                    for w in range(2):
                        pe.wait_ge(s_wn, w + 1)
                        for h in range(KIN):
                            last = pe.matmul(bank[w][:, :], wn[:, w, h, :], x_sb[:, h, :], start=(h == 0),
                                             stop=(h == KIN - 1))
                        last.then_inc(s_lin, 1)
                    centered(0)
                    centered(1)
                    variance(0)
                    variance(1)
                    pe.wait_ge(s_u, 1)
                    pe.matmul(h_ps[:, :], w3[:, :], u[:, :], start=True, stop=True).then_inc(s_h, 1)
                    pe.wait_ge(s_img, 1)
                    centered(2)
                    variance(2)

        xw = sb("xw", [P, NE, XW - 1])
        b2_parts = sb("b2_parts", [3, NE * P], BF16)
        ones_p = sb("ones_p", [3, P], BF16)
        wr_sb = sb("wr_sb", [P, NE])
        br_sb = sb("br_sb", [P, NE])
        wqkv = sb("wqkv", [P, 3, HEADS * HPAD])
        wo = sb("wo", [P, 2, P])
        s_xw, s_b2, s_wr, s_wat = sem("s_xw"), sem("s_b2"), sem("s_wr"), sem("s_wat")
        with ExitStack() as lstm:
            def lb(name, shape, dt=F32):
                return lstm.enter_context(nc.sbuf_tensor(name, shape, dt))

            sig = lb("sig", [P, 3, B, 2])
            sig_o = lb("sig_o", [P, B])
            tanh_c = lb("tanh_c", [P, B])
            cell = lb("cell", [P, 2, 2 * B + 2])
            h_hi = lb("h_hi", [P, B], F16)
            h_lo = lb("h_lo", [P, B], F16)
            h32 = lb("h32", [P, 2, B])
            ifg_ps, o_ps = [bank[0], bank[1]], [bank[2], bank[3]]
            s_zero, s_hi, s_lo, s_h32, s_ifg, s_o, s_sig, s_sigo, s_ig, s_c, s_tanh = (sem(n) for n in (
                "s_zero", "s_hi", "s_lo", "s_h32", "s_ifg", "s_o", "s_sig", "s_sigo", "s_ig", "s_c", "s_tanh"))
            ITER = T // (2 * G)

            b2_raw = lb("b2_raw", [3, NE * P])
            b2_r1 = lb("b2_r1", [3, NE * P])
            b2_r2 = lb("b2_r2", [3, NE * P])
            b2_p = lb("b2_p", [3, 3, NE * P], BF16)
            s_b2c = sem("s_b2c")
            blank = lb("blank", [P, NBLK, XR])
            s_blank = sem("s_blank")

            with nc.Block() as block:
                @block.sync
                def _(sp):
                    sp.dma_start(wqkv[:, :, :], wqkvT).then_inc(s_wat, 16)
                    sp.dma_start(wo[:, :, :], woT).then_inc(s_wat, 16)
                    sp.dma_start(wr_sb[:, :], wr).then_inc(s_wr, 16)
                    sp.dma_start(br_sb[:, :], br).then_inc(s_wr, 16)
                    sp.dma_start(b2_raw[:, :], b2rows).then_inc(s_b2, 16)
                    sp.dma_start(xw[:, :, :], expert1).then_inc(s_xw, 16)
                    sp.wait_ge(s_blank, 1)
                    sp.dma_start(scr_x.rearrange("(k p) f -> p k f", p=P), blank[:, :, :]).then_inc(s_empty, 16)
                    sp.wait_ge(s_empty, 16)

                @block.gpsimd
                def _(pool):
                    pool.memset(sig[:, :, :, :], 0.0)
                    pool.memset(cell[:, :, :], 0.0).then_inc(s_zero, 1)
                    pool.memset(blank[:, :, 0:2 * P], 0.0)
                    pool.tensor_copy(blank[:, :, 2 * P], cst[:, K_EMPTY:K_EMPTY + NBLK]).then_inc(s_blank, 1)
                    pool.memset(ones_p[:, :], 1.0)
                    n = 0

                    def link(ins):
                        nonlocal n
                        n += 1
                        ins.then_inc(s_b2c, 1)
                        pool.wait_ge(s_b2c, n)

                    pool.wait_ge(s_b2, 16)
                    link(pool.tensor_copy(b2_p[:, 0, :], b2_raw[:, :]))
                    link(pool.tensor_tensor(b2_r1[:, :], b2_raw[:, :], b2_p[:, 0, :], ALU.subtract))
                    link(pool.tensor_copy(b2_p[:, 1, :], b2_r1[:, :]))
                    link(pool.tensor_tensor(b2_r2[:, :], b2_r1[:, :], b2_p[:, 1, :], ALU.subtract))
                    link(pool.tensor_copy(b2_p[:, 2, :], b2_r2[:, :]))
                    link(pool.tensor_scalar(b2_raw[:, :], b2_p[:, 0, :], cst[0:3, 0:1], None, ALU.mult))
                    link(pool.tensor_scalar(b2_r1[:, :], b2_p[:, 1, :], cst[0:3, 1:2], None, ALU.mult))
                    link(pool.tensor_scalar(b2_r2[:, :], b2_p[:, 2, :], cst[0:3, 2:3], None, ALU.mult))
                    link(pool.tensor_tensor(b2_r1[:, :], b2_r1[:, :], b2_r2[:, :], ALU.add))
                    link(pool.tensor_tensor(b2_parts[:, :], b2_raw[:, :], b2_r1[:, :], ALU.add))

                @block.vector
                def _(dve):
                    dve.memset(h_hi[:, :], 0.0).then_inc(s_hi, 1)
                    dve.memset(h_lo[:, :], 0.0).then_inc(s_lo, 1)
                    dve.wait_ge(s_zero, 1)
                    with dve.Fori(0, ITER) as it:
                        for s in range(2 * G):
                            t, p = it * (2 * G) + s, s % 2
                            dve.wait_ge(s_sig, t + 1)
                            dve.scalar_tensor_tensor(cell[:, p, 2:2 * B + 2:2], sig[:, 2, :, 1], -0.5, sig[:, 0, :, 1],
                                                     ALU.add, ALU.mult).then_inc(s_ig, 1)
                            dve.wait_ge(s_ig, t + 1)
                            dve.tensor_tensor_scan(cell[:, 1 - p, 0:2 * B], sig[:, 1, :, :].rearrange("p b k -> p (b k)"),
                                                   cell[:, p, 1:2 * B + 1], 0.0, ALU.mult, ALU.add).then_inc(s_c, 1)
                            dve.wait_ge(s_tanh, t + 1)
                            dve.tensor_tensor(h_hi[:, :], sig_o[:, :], tanh_c[:, :], ALU.mult).then_inc(s_hi, 1)
                            dve.tensor_tensor(h32[:, p, :], sig_o[:, :], tanh_c[:, :], ALU.mult).then_inc(s_h32, 1)
                            dve.wait_ge(s_h32, t + 1)
                            dve.tensor_tensor(h_lo[:, :], h32[:, p, :], h_hi[:, :], ALU.subtract).then_inc(s_lo, 1)
                            dve.tensor_copy(hseq[:, bass.ds(it * (2 * GB) + s * B, B)], h32[:, p, :])

                @block.scalar
                def _(act):
                    act.wait_ge(s_zero, 1)
                    with act.Fori(0, ITER) as it:
                        for s in range(2 * G):
                            t, k, q, p = it * (2 * G) + s, s // G, s % G, s % 2
                            act.wait_ge(s_ifg, t + 1)
                            act.activation(sig[:, :, :, 1],
                                           ifg_ps[k][:, 0:3 * GB].rearrange("p (g s b) -> p g s b", g=3, s=G)[:, :, q, :],
                                           ACT.Sigmoid).then_inc(s_sig, 1)
                            act.wait_ge(s_o, t + 1)
                            act.activation(sig_o[:, :], o_ps[k][:, q * B:(q + 1) * B], ACT.Sigmoid).then_inc(s_sigo, 1)
                            act.wait_ge(s_c, t + 1)
                            act.activation(tanh_c[:, :], cell[:, 1 - p, 1:2 * B + 1:2], ACT.Tanh, scale=2.0)\
                               .then_inc(s_tanh, 1)

                @block.tensor
                def _(pe):
                    def gate_out(j, k, lo, hi):
                        return ifg_ps[k][:, j * GB + lo:j * GB + hi] if j < 3 else o_ps[k][:, lo:hi]

                    def input_part(j, k, cols):
                        o = gate_out(j, k, 0, GB)
                        pe.matmul(o, wi[:, j * P:(j + 1) * P], xn_in[:, cols], start=(j in (0, 3)), stop=False,
                                  skip_group_check=True)
                        pe.matmul(o, bias_parts[:, j * P:(j + 1) * P], ones3[:, :], start=False, stop=False,
                                  skip_group_check=True)

                    for j in range(4):
                        input_part(j, 0, slice(0, GB))
                    with pe.Fori(0, ITER) as it:
                        for s in range(2 * G):
                            t, k, q = it * (2 * G) + s, s // G, s % G

                            def recur(w, j, h):
                                return pe.matmul(gate_out(j, k, q * B, (q + 1) * B), wh[w][:, j * P:(j + 1) * P], h[:, :],
                                                 start=False, stop=False, skip_group_check=True)

                            pe.wait_ge(s_hi, t + 1)
                            for w in range(3):
                                for j in range(3):
                                    recur(w, j, h_hi)
                            pe.wait_ge(s_lo, t + 1)
                            for j in range(3):
                                last = recur(0, j, h_lo)
                            last.then_inc(s_ifg, 1)
                            for w in range(3):
                                recur(w, 3, h_hi)
                            recur(0, 3, h_lo).then_inc(s_o, 1)
                            input_part(q, 1 - k, bass.ds(it * (2 * GB) + (1 + k) * GB, GB))

        h_res = sb("h_res", [P, N])
        xn_b = sb("xn_b", [P, N])
        gates = sb("gates", [P, B * KSEL])
        chosen = sb("chosen", [1, B * KSEL], U32)

        NCH = N // NLN
        with ExitStack() as gst:
            def gb(name, shape, dt=F32):
                return gst.enter_context(nc.sbuf_tensor(name, shape, dt))

            def gsem(name):
                return ctx.enter_context(nc.semaphore(name))

            sq = gb("sq2", [P, NCH, NLN])
            lnv = gb("lnv2", [P, NCH, NLN])
            rstd = gb("rstd2", [P, NCH, NLN])
            aw_bc = gb("aw_bc", [P, P])
            gw = gb("gw", [P, NE])
            gbias = gb("gbias", [B, NE])
            smax = gb("smax", [P, B])
            sbias = gb("sbias", [P, B])
            esc = gb("esc", [P, B, T])
            scr = gb("scr", [P, B, T])
            esum = gb("esum", [P, B])
            pooled = gb("pooled", [P, B])
            lg = gb("lg", [B, NE])
            lmax = gb("lmax", [B, 1])
            le = gb("le", [B, NE])
            lsum = gb("lsum", [B, 1])
            lp = gb("lp", [B, NE])
            top = gb("top", [B, 8])
            topi = gb("topi", [B, 8], U32)
            gsum = gb("gsum", [B, 1])
            g2 = gb("g2", [B, KSEL])
            diag = gb("diag", [B, B, KSEL])
            ones8 = gb("ones8", [B, P])
            s_gw, s_res, s_cen, s_sq, s_var, s_std, s_xn, s_ch, s_aw, s_sc, s_sb, s_es = (gsem("g_" + n) for n in (
                "gw", "res", "cen", "sq", "var", "std", "xn", "chain", "aw", "score", "sbias", "escore"))
            s_pool, s_lg, s_lm, s_le, s_dg, s_gp, s_idx, s_idxd = (gsem("g_" + n) for n in (
                "pooled", "logits", "lmax", "lexp", "diag", "gatesps", "index", "indexdma"))
            s_ones, s_ln = gsem("g_ones"), gsem("g_ln")
            with nc.Block() as block:
                @block.sync
                def _(sp):
                    sp.dma_start(gw[:, :], gate_w).then_inc(s_gw, 16)
                    sp.dma_start(gbias[:, :], gate_b).then_inc(s_gw, 16)
                    sp.wait_ge(s_idx, 1)
                    sp.dma_start(chosen[0:1, :], topi[:, 0:KSEL]).then_inc(s_idxd, 16)
                    sp.wait_ge(s_idxd, 16)

                @block.gpsimd
                def _(pool):
                    pool.memset(ones8[:, :], 1.0).then_inc(s_ones, 1)

                @block.scalar
                def _(act):
                    def inverse_root(c):
                        act.wait_ge(s_var, c + 1)
                        act.activation(lnv[:, c, :], bank[4 + c][:, 0:NLN], ACT.Ln, bias=epsc[:, 0:1]).then_inc(s_ln, 1)
                        act.wait_ge(s_ln, c + 1)
                        act.activation(rstd[:, c, :], lnv[:, c, :], ACT.Exp, scale=-0.5).then_inc(s_std, 1)

                    act.preload_act_table_set("natural_log_exp_and_others")
                    for c in range(NCH):
                        act.wait_ge(s_cen, c + 1)
                        act.activation(sq[:, c, :], bank[c][:, 0:NLN], ACT.Square).then_inc(s_sq, 1)
                        if c:
                            inverse_root(c - 1)
                    inverse_root(NCH - 1)
                    for b in range(B):
                        act.wait_ge(s_sb, b // 2 + 1)
                        act.activation(esc[:, b, :], bank[4 + b // 2][:, T * (b % 2):T * (b % 2 + 1)], ACT.Exp,
                                       bias=sbias[:, b:b + 1], accum_out=esum[:, b:b + 1]).then_inc(s_es, 1)
                    act.wait_ge(s_lm, 1)
                    act.activation(le[:, :], lg[:, :], ACT.Exp, bias=lmax[:, 0:1], accum_out=lsum[:, 0:1])\
                       .then_inc(s_le, 1)

                @block.vector
                def _(dve):
                    n = 0

                    def link(ins):
                        nonlocal n
                        n += 1
                        ins.then_inc(s_ch, 1)
                        dve.wait_ge(s_ch, n)

                    def by_t(a, c):
                        return a[:, 0:N].rearrange("p (t b) -> p b t", b=B)[:, 2 * c:2 * c + 2, :]

                    dve.tensor_scalar(aw_bc[:, :], average, float(P), col[:, C_AW:C_AW + 1], ALU.mult, ALU.mult)\
                       .then_inc(s_aw, 1)
                    for c in range(NCH):
                        dve.tensor_tensor(h_res[:, NLN * c:NLN * (c + 1)].rearrange("p (b t) -> p b t", b=2),
                                          by_t(h_in, c), by_t(hseq, c), ALU.add).then_inc(s_res, 1)
                    for c in range(NCH):
                        dve.wait_ge(s_std, c + 1)
                        dve.tensor_tensor(xn_b[:, NLN * c:NLN * (c + 1)], bank[c][:, 0:NLN], rstd[:, c, :], ALU.mult)\
                           .then_inc(s_xn, 1)

                    def pool_tokens(c):
                        for b in (2 * c, 2 * c + 1):
                            dve.wait_ge(s_es, b + 1)
                            link(dve.tensor_tensor_reduce(scr[:, b, :], esc[:, b, :], xn_b[:, T * b:T * (b + 1)], 1.0,
                                                          0.0, ALU.mult, ALU.add, pooled[:, b:b + 1]))

                    dve.wait_ge(s_xn, NCH)
                    for c in range(NCH):
                        dve.wait_ge(s_sc, c + 1)
                        link(dve.tensor_reduce(smax[:, 2 * c:2 * c + 2],
                                               bank[4 + c][:, 0:NLN].rearrange("p (b t) -> p b t", b=2), AX_X, ALU.max))
                        link(dve.tensor_scalar(sbias[:, 2 * c:2 * c + 2], smax[:, 2 * c:2 * c + 2],
                                               col[:, C_AB:C_AB + 1], -1.0, ALU.add, ALU.mult))
                        dve.tensor_scalar(sbias[:, 2 * c:2 * c + 2], sbias[:, 2 * c:2 * c + 2],
                                          col[:, C_AB:C_AB + 1], None, ALU.add).then_inc(s_sb, 1)
                        if c:
                            pool_tokens(c - 1)
                    pool_tokens(NCH - 1)
                    link(dve.reciprocal(esum[:, :], esum[:, :]))
                    dve.tensor_tensor(pooled[:, :], pooled[:, :], esum[:, :], ALU.mult).then_inc(s_pool, 1)
                    dve.wait_ge(s_lg, 1)
                    dve.wait_ge(s_gw, 32)
                    link(dve.tensor_tensor(lg[:, :], bank[0][0:B, 0:NE], gbias[:, :], ALU.add))
                    link(dve.tensor_reduce(lmax[:, :], lg[:, :], AX_X, ALU.max))
                    dve.tensor_scalar(lmax[:, :], lmax[:, :], -1.0, None, ALU.mult).then_inc(s_lm, 1)
                    dve.wait_ge(s_le, 1)
                    link(dve.reciprocal(lsum[:, :], lsum[:, :]))
                    link(dve.tensor_scalar(lp[:, :], le[:, :], lsum[:, 0:1], None, ALU.mult))
                    link(dve.max(top[:, :], lp[:, :]))
                    dve.max_index(topi[:, :], top[:, :], lp[:, :]).then_inc(s_idx, 1)
                    link(dve.tensor_reduce(gsum[:, :], top[:, 0:KSEL], AX_X, ALU.add))
                    link(dve.tensor_scalar(gsum[:, :], gsum[:, :], 1e-9, None, ALU.add))
                    link(dve.reciprocal(gsum[:, :], gsum[:, :]))
                    link(dve.tensor_scalar(g2[:, :], top[:, 0:KSEL], gsum[:, 0:1], None, ALU.mult))
                    for k in range(KSEL):
                        last = dve.tensor_scalar(diag[:, :, k], cst[0:B, 0:B], g2[:, k:k + 1], None, ALU.mult)
                    last.then_inc(s_dg, 1)
                    dve.wait_ge(s_gp, 1)
                    link(dve.tensor_copy(gates[:, :], bank[1][:, 0:B * KSEL]))

                @block.tensor
                def _(pe):
                    for c in range(NCH):
                        pe.wait_ge(s_res, c + 1)
                        pe.matmul(bank[c][:, 0:NLN], center, h_res[:, NLN * c:NLN * (c + 1)], start=True, stop=True)\
                          .then_inc(s_cen, 1)
                    for c in range(NCH):
                        pe.wait_ge(s_sq, c + 1)
                        pe.matmul(bank[4 + c][:, 0:NLN], average, sq[:, c, :], start=True, stop=True).then_inc(s_var, 1)
                    pe.wait_ge(s_aw, 1)
                    for c in range(NCH):
                        pe.wait_ge(s_xn, c + 1)
                        pe.matmul(bank[4 + c][:, 0:NLN], aw_bc[:, :], xn_b[:, NLN * c:NLN * (c + 1)],
                                  start=True, stop=True).then_inc(s_sc, 1)
                    pe.wait_ge(s_pool, 1)
                    pe.wait_ge(s_gw, 32)
                    pe.matmul(bank[0][0:B, 0:NE], pooled[:, :], gw[:, :], start=True, stop=True).then_inc(s_lg, 1)
                    pe.wait_ge(s_dg, 1)
                    pe.wait_ge(s_ones, 1)
                    pe.matmul(bank[1][:, 0:B * KSEL], ones8[:, :], diag[:, :, :].rearrange("p b k -> p (b k)"),
                              start=True, stop=True).then_inc(s_gp, 1)


        h_res2 = sb("h_res2", [P, N])
        h_res3 = sb("h_res3", [P, N])
        cw = sb("cw", [P, CW])
        sq_all = sb("sq_all", [P, NTT, P])
        ssum = sb("ssum", [P, NTT])
        xt = sb("xt", [P, NTT, XR])
        s_cwr, s_cw, s_cen4, s_sq4, s_tr, s_ht = (sem(n) for n in (
            "s_cwr", "s_cw", "s_cen4", "s_sq4", "s_tr", "s_ht"))

        def centered_ps(i):
            return bank[i // TPB][:, CW * (i % TPB):CW * (i % TPB) + CW]

        def pe_center(pe, first, last):
            for i in range(first, last):
                pe.matmul(centered_ps(i), h_res3[:, P * i:P * i + P], cw[:, :], start=True, stop=True)\
                  .then_inc(s_cen4, 1)

        def pe_turn(pe, first, last):
            for i in range(first, last):
                mm = pe.transpose(bank[4 + i // 4][:, P * (i % 4):P * (i % 4) + P], h_res3[:, P * i:P * i + P], ident)
                if i % 4 == 3:
                    mm.then_inc(s_tr, 1)

        def act_squares(act, first, last):
            for i in range(first, last):
                act.wait_ge(s_cen4, TPB * (i // TPB) + TPB)
                act.activation(sq_all[:, i, :], centered_ps(i)[:, 0:P], ACT.Square,
                               accum_out=ssum[:, i:i + 1]).then_inc(s_sq4, 1)

        def act_copy_turned(act, first, last):
            for g in range(first // 4, last // 4):
                act.wait_ge(s_tr, g + 1)
                act.activation(xt[:, 4 * g:4 * g + 4, P:2 * P], bank[4 + g][:, :].rearrange("p (i f) -> p i f", i=4),
                               ACT.Copy).then_inc(s_ht, 1)
        with ExitStack() as ast:
            def ab(name, shape, dt=F32):
                return ast.enter_context(nc.sbuf_tensor(name, shape, dt))

            def asem(name):
                return ctx.enter_context(nc.semaphore("a_" + name))

            NP = HEADS // 2
            NT = 3
            QR = T - P
            p_keep = asem("p_keep")
            ND = 2
            OPS = 24
            ew = ab("ew", [P, KSEL, XW])
            hid = ab("hid", [P, KSEL, NJ, T])
            eo = ab("eo", [P, KSEL, T])
            weo = ab("weo", [P, KSEL, T])
            gcur = ab("gcur", [P, KSEL])
            xc = ab("xc3", [P, T])
            sq = ab("sq3", [P, T])
            lnv = ab("lnv", [P, T])
            rstd = ab("rstd", [P, T])
            xn = ab("xn3", [P, T])
            qt = ab("qt", [P, 2, T])
            kt = ab("kt", [P, 2, T])
            vt = ab("vt", [KC, 2, HEADS * HPAD])
            ot = ab("ot", [P, 2, T])
            pr = ab("pr", [P, T])
            s_sb = ab("s_sb", [P, NP, NT, T])
            rest = ab("rest", [P, NP, NT, T])
            m8 = ab("m8", [P, NP, NT, TOPK // 8, 8])
            nbias = ab("nbias", [P, NP, NT])
            ex = ab("ex", [P, NP, NT, T])
            zsum = ab("zsum", [P, NP, NT])
            rz = ab("rz", [P, NP, NT])
            keep = ab("keep", [P, NP, NT, T])
            prob = ab("prob", [P, NP, NT, T])
            pt = ab("pt", [KC, NT, 2, P])
            hid_ps = [bank[0], bank[1]]
            v_ps, ln_ps, sa_ps, sb_ps, tp_ps, out_ps = bank[2:8]
            (s_ewd0, s_ewd1, s_head) = (asem(n) for n in ("ew0", "ew1", "scores0"))
            s_ewd = [s_ewd0, s_ewd1]
            s_ewo = [asem("ewo0"), asem("ewo1")]
            (s_h, s_eo, s_cen, s_var, s_q, s_k, s_v, s_sa, s_sbt, s_tpa, s_tpb, s_av, s_wo) = (asem(n) for n in (
                "hidden_ps", "eo_ps", "cen", "var", "q_ps", "k_ps", "v_ps", "scores01", "scores2", "turned01",
                "turned2", "av", "wo_ps"))
            (c_gelu, c_eo, c_sq, c_ln, c_rstd, c_q, c_k, c_v, c_sa, c_sb, c_e, c_tpa, c_tpb, c_o, c_pr) = (
                asem(n) for n in ("gelu", "eo", "square", "ln", "rstd", "q", "k", "v", "copied01", "copied2", "exp",
                                  "ptcopy01", "ptcopy2", "ocopy", "product"))
            (d_top, d_rz, d_keep) = (asem(n) for n in ("top", "rz", "keep"))
            (p_nb, p_prob, p_xn, p_h3, p_g, p_weo, p_h2) = (asem(n) for n in (
                "nbias", "prob", "xn", "h3", "gcol", "weighted", "h2"))

            def wait(eng, s, value):
                if not isinstance(value, int) or value > 0:
                    eng.wait_ge(s, value)

            def wait_alone(eng, s, value):
                if not isinstance(value, int) or value > 0:
                    eng.wait_ge(s, value)
                    eng.nop(nofuse=True)

            def cols(b):
                return slice(b * T, (b + 1) * T) if isinstance(b, int) else bass.ds(b * T, T)

            def iterations(eng, body):
                body(0, False, True)
                with eng.Fori(1, B - 1) as b:
                    body(b, True, True)
                body(B - 1, True, False)

            with nc.Block() as block:
                @block.sync
                def _(sp):
                    def expert_of(i):
                        return sp.value_load(chosen[0:1, i:i + 1] if isinstance(i, int) else chosen[0:1, bass.ds(i, 1)],
                                             min_val=0, max_val=NE - 1)

                    def load(b):
                        e = [expert_of(2 * b), expert_of(2 * b + 1)]
                        for k in range(KSEL):
                            wait(sp, c_eo, 2 * b + k - 1)
                            sp.dma_start(ew[:, k, 0:W1W],
                                         expert0[bass.ds(e[k], 1), :, 0:W1W].rearrange("e p w -> (e p) w"))\
                              .then_inc(s_ewd[k], 16)
                        for k in range(KSEL):
                            sp.dma_start(ew[:, k, W1W:XW],
                                         expert0[bass.ds(e[k], 1), :, W1W:XW].rearrange("e p w -> (e p) w"))\
                              .then_inc(s_ewo[k], 16)

                    load(0)
                    with sp.Fori(1, B) as b:
                        load(b)

                @block.tensor
                def _(pe):
                    pe.wait_ge(s_wat, 32)

                    def hidden(b, k):
                        pe.wait_ge(s_ewd[k], 16 * (b + 1))
                        if k == 0:
                            wait(pe, c_k, b)
                        for j in range(NJ):
                            if k:
                                pe.wait_ge(c_gelu, 8 * b + 2 * (j // 2) + 2)
                            pe.matmul(hid_ps[j // 2][:, T * (j % 2):T * (j % 2 + 1)], ew[:, k, j * P:(j + 1) * P],
                                      xn_b[:, cols(b)], start=True, stop=True).then_inc(s_h, 1)

                    def output(b, k):
                        pe.wait_ge(s_ewo[k], 16 * (b + 1))
                        pe.wait_ge(c_gelu, 8 * b + 4 * k + 4)
                        wait(pe, c_tpb, 4 * (b - 2) + 3 + k)
                        wait(pe, c_eo, 2 * b + k)
                        for j in range(NJ):
                            last = pe.matmul(ln_ps[:, 0:T], ew[:, k, W1W + j * P:W1W + (j + 1) * P],
                                             hid[:, k, j, :], start=(j == 0), stop=(j == NJ - 1))
                        last.then_inc(s_eo, 1)

                    def centered(b):
                        wait(pe, c_tpb, 4 * (b - 1))
                        pe.wait_ge(p_h2, 2 * b + 2)
                        pe.matmul(ln_ps[:, 0:T], center, h_res2[:, cols(b)], start=True, stop=True).then_inc(s_cen, 1)

                    def variance(b):
                        wait(pe, c_tpb, 4 * (b - 1) + 1)
                        pe.wait_ge(c_sq, b + 1)
                        pe.matmul(ln_ps[:, 0:T], average, sq[:, :], start=True, stop=True).then_inc(s_var, 1)

                    def queries(b):
                        pe.wait_ge(p_xn, b + 1)
                        for a, (bk, s) in enumerate(((hid_ps[0], s_q), (hid_ps[1], s_k))):
                            for half in range(2):
                                last = pe.matmul(bk[:, half * T:(half + 1) * T], wqkv[:, a, half * P:(half + 1) * P],
                                                 xn[:, :], start=True, stop=True)
                            last.then_inc(s, 1)

                    def values(b):
                        wait(pe, c_v, b)
                        for kc in range(2):
                            last = pe.matmul(v_ps[0:KC, kc * 256:kc * 256 + 256], xn[:, kc * KC:(kc + 1) * KC],
                                             wqkv[:, 2, :], start=True, stop=True)
                        last.then_inc(s_v, 1)

                    def pair_scores(b, p):
                        n, half, a = 4 * b + p, p // 2, HPAD * 2 * (p % 2)
                        if p == 0:
                            pe.wait_ge(c_k, b + 1)
                        wait(pe, c_sa, n)
                        wait(pe, c_sb, n)
                        for i in range(2):
                            r = slice(a + HPAD * i, a + HPAD * (i + 1))
                            if i:
                                pe.wait_ge(s_head, n + 1)
                            mm = pe.matmul(sa_ps[:, T * i:T * (i + 1)], qt[r, half, 0:P], kt[r, half, :],
                                           start=True, stop=True)
                            mm.then_inc(s_sa if i else s_head, 1)
                            mm = pe.matmul(sb_ps[QR * i:QR * (i + 1), 0:T], qt[r, half, P:T], kt[r, half, :],
                                           start=True, stop=True)
                        mm.then_inc(s_sbt, 1)

                    def turn(b, p, ln_free=None):
                        n = 4 * b + p
                        wait(pe, c_tpa, n)
                        for i in range(2):
                            pe.wait_ge(p_prob, 3 * n + i + 1)
                            for kc in range(2):
                                last = pe.transpose(tp_ps[0:KC, (2 * i + kc) * P:(2 * i + kc + 1) * P],
                                                    prob[:, p, i, kc * KC:(kc + 1) * KC], ident)
                        last.then_inc(s_tpa, 1)
                        wait(pe, c_tpb, n)
                        if ln_free:
                            wait(pe, *ln_free)
                        pe.wait_ge(p_prob, 3 * n + 3)
                        for kc in range(2):
                            last = pe.transpose(ln_ps[0:KC, kc * P:(kc + 1) * P],
                                                prob[:, p, 2, kc * KC:(kc + 1) * KC], ident)
                        last.then_inc(s_tpb, 1)

                    def weigh(b, p):
                        n, half, a = 4 * b + p, p // 2, HPAD * 2 * (p % 2)
                        if p == 0:
                            pe.wait_ge(c_v, b + 1)
                            wait(pe, c_pr, b)
                        pe.wait_ge(c_tpa, n + 1)
                        pe.wait_ge(c_tpb, n + 1)
                        for i in range(2):
                            h = 2 * p + i
                            o = out_ps[a + HPAD * i:a + HPAD * (i + 1), half * T:(half + 1) * T]
                            for lo, hi, rhs in ((0, P, pt[:, i, :, :]), (P, T, pt[:, 2, :, QR * i:QR * (i + 1)])):
                                for kc in range(2):
                                    last = pe.matmul(o[:, lo:hi], vt[:, kc, HPAD * h:HPAD * (h + 1)], rhs[:, kc, :],
                                                     start=(kc == 0), stop=(kc == 1))
                        last.then_inc(s_av, 1)

                    def project(b):
                        pe.wait_ge(c_o, b + 1)
                        for half in range(2):
                            last = pe.matmul(out_ps[:, 0:T], wo[:, half, :], ot[:, half, :],
                                             start=(half == 0), stop=(half == 1))
                        last.then_inc(s_wo, 1)

                    def body(b, prev, nxt):
                        pair_scores(b, 2)
                        if nxt:
                            hidden(b + 1, 0)
                        pair_scores(b, 3)
                        if prev:
                            turn(b - 1, 2)
                        if nxt:
                            hidden(b + 1, 1)
                            output(b + 1, 0)
                        if prev:
                            weigh(b - 1, 2)
                            turn(b - 1, 3, (c_eo, 2 * b + 3) if nxt else None)
                        if nxt:
                            output(b + 1, 1)
                        if prev:
                            weigh(b - 1, 3)
                        if nxt:
                            centered(b + 1)
                        if prev:
                            project(b - 1)
                        turn(b, 0, (c_sq, b + 2) if nxt else None)
                        if nxt:
                            variance(b + 1)
                        weigh(b, 0)
                        if nxt:
                            queries(b + 1)
                        turn(b, 1, (c_ln, b + 2) if nxt else None)
                        if nxt:
                            pair_scores(b + 1, 0)
                            values(b + 1)
                        weigh(b, 1)
                        if nxt:
                            pair_scores(b + 1, 1)

                    hidden(0, 0)
                    hidden(0, 1)
                    pe.wait_ge(s_wr, 32)
                    pe.matmul(out_ps[:, 0:NE], center, wr_sb[:, :], start=True, stop=True).then_inc(s_cwr, 1)
                    output(0, 0)
                    output(0, 1)
                    centered(0)
                    variance(0)
                    queries(0)
                    pair_scores(0, 0)
                    values(0)
                    pair_scores(0, 1)
                    pe.wait_ge(s_cw, 2)
                    iterations(pe, body)
                    pe.wait_ge(p_h3, B - 2)
                    pe.wait_ge(c_k, B)
                    pe.wait_ge(c_v, B)
                    pe_center(pe, 0, EARLY)
                    pe.wait_ge(c_sa, NP * B)
                    pe.wait_ge(c_sb, NP * B)
                    pe_turn(pe, 0, 8)
                    turn(B - 1, 2)
                    weigh(B - 1, 2)
                    turn(B - 1, 3)
                    weigh(B - 1, 3)
                    project(B - 1)
                    pe.wait_ge(p_h3, B)
                    pe.wait_ge(c_tpb, NP * B)
                    pe_center(pe, EARLY, NTT)
                    pe_turn(pe, 8, NTT)

                @block.scalar
                def _(act):
                    def hidden(b, k):
                        act.wait_ge(s_ewd[k], 16 * (b + 1))
                        wait(act, s_eo, 2 * b + k - 1)
                        for j in range(NJ):
                            act.wait_ge(s_h, 8 * b + 4 * k + 2 * (j // 2) + 2)
                            act.activation(hid[:, k, j, :], hid_ps[j // 2][:, T * (j % 2):T * (j % 2 + 1)],
                                           ACT.Gelu, bias=ew[:, k, HID + j:HID + j + 1]).then_inc(c_gelu, 1)

                    def output(b, k):
                        wait(act, p_h2, 2 * b + k - 1)
                        act.wait_ge(s_ewo[k], 16 * (b + 1))
                        act.wait_ge(s_eo, 2 * b + k + 1)
                        act.activation(eo[:, k, :], ln_ps[:, 0:T], ACT.Gelu,
                                       bias=ew[:, k, XW - 1:XW]).then_inc(c_eo, 1)
                        if k:
                            act.preload_act_table_set("natural_log_exp_and_others")

                    def squares(b):
                        wait(act, p_xn, b)
                        act.wait_ge(s_cen, b + 1)
                        act.activation(xc[:, :], ln_ps[:, 0:T], ACT.Copy)
                        act.activation(sq[:, :], ln_ps[:, 0:T], ACT.Square).then_inc(c_sq, 1)

                    def inverse_root(b):
                        act.wait_ge(s_var, b + 1)
                        act.activation(lnv[:, :], ln_ps[:, 0:T], ACT.Ln, bias=epsc[:, 0:1]).then_inc(c_ln, 1)
                        act.wait_ge(c_ln, b + 1)
                        act.activation(rstd[:, :], lnv[:, :], ACT.Exp, scale=-0.5).then_inc(c_rstd, 1)

                    def copy_qk(b):
                        wait(act, s_sbt, 4 * b)
                        act.wait_ge(s_q, b + 1)
                        act.activation(qt[:, :, :], hid_ps[0][:, 0:2 * T].rearrange("p (h t) -> p h t", h=2),
                                       ACT.Copy).then_inc(c_q, 1)
                        act.wait_ge(s_k, b + 1)
                        act.activation(kt[:, :, :], hid_ps[1][:, 0:2 * T].rearrange("p (h t) -> p h t", h=2),
                                       ACT.Copy).then_inc(c_k, 1)

                    def copy_scores(b, p):
                        n = 4 * b + p
                        wait(act, d_top, OPS * (n - NP) + 6)
                        wait(act, c_e, 3 * (n - NP) + 3)
                        act.wait_ge(s_sa, n + 1)
                        act.activation(s_sb[:, p, 0:2, :], sa_ps[:, 0:2 * T].rearrange("p (i t) -> p i t", i=2),
                                       ACT.Copy).then_inc(c_sa, 1)
                        act.wait_ge(s_sbt, n + 1)
                        act.activation(s_sb[:, p, 2, :], sb_ps[:, 0:T], ACT.Copy).then_inc(c_sb, 1)

                    def exps(b, p):
                        n = 4 * b + p
                        wait(act, p_prob, 3 * (n - NP) + 3)
                        wait(act, d_rz, n - NP + 1)
                        for i in range(NT):
                            act.wait_ge(p_nb, 3 * n + i + 1)
                            if i == 0:
                                act.wait_ge(c_sb, n + 1)
                            act.activation(ex[:, p, i, :], s_sb[:, p, i, :], ACT.Exp, scale=SCALE,
                                           bias=nbias[:, p, i:i + 1], accum_out=zsum[:, p, i:i + 1])\
                               .then_inc(c_e, 1)

                    def copy_turned(b, p):
                        n = 4 * b + p
                        wait(act, s_av, n)
                        act.wait_ge(s_tpa, n + 1)
                        act.activation(pt[:, 0:2, :, :], tp_ps[0:KC, :].rearrange("p (i c q) -> p i c q", i=2, c=2),
                                       ACT.Copy).then_inc(c_tpa, 1)
                        act.wait_ge(s_tpb, n + 1)
                        act.activation(pt[:, 2, :, :], ln_ps[0:KC, 0:2 * P].rearrange("p (c q) -> p c q", c=2),
                                       ACT.Copy).then_inc(c_tpb, 1)

                    def copy_sums(b):
                        act.wait_ge(s_av, 4 * b + 4)
                        act.activation(ot[:, :, :], out_ps[:, 0:2 * T].rearrange("p (h t) -> p h t", h=2),
                                       ACT.Copy).then_inc(c_o, 1)

                    def copy_product(b):
                        act.wait_ge(s_wo, b + 1)
                        act.activation(pr[:, :], out_ps[:, 0:T], ACT.Copy).then_inc(c_pr, 1)

                    def copy_values(b):
                        wait(act, s_av, 4 * b)
                        act.wait_ge(s_v, b + 1)
                        act.activation(vt[:, :, :], v_ps[0:KC, :].rearrange("p (c d) -> p c d", c=2), ACT.Copy)\
                           .then_inc(c_v, 1)

                    def body(b, prev, nxt):
                        copy_scores(b, 2)
                        exps(b, 0)
                        if nxt:
                            hidden(b + 1, 0)
                        copy_scores(b, 3)
                        if prev:
                            copy_turned(b - 1, 2)
                        if nxt:
                            hidden(b + 1, 1)
                            output(b + 1, 0)
                        if prev:
                            copy_turned(b - 1, 3)
                        if nxt:
                            output(b + 1, 1)
                        exps(b, 1)
                        if prev:
                            copy_sums(b - 1)
                        copy_values(b)
                        if nxt:
                            squares(b + 1)
                        if prev:
                            copy_product(b - 1)
                        copy_turned(b, 0)
                        if nxt:
                            inverse_root(b + 1)
                        exps(b, 2)
                        if nxt:
                            copy_qk(b + 1)
                        copy_turned(b, 1)
                        if nxt:
                            copy_scores(b + 1, 0)
                            copy_scores(b + 1, 1)
                        exps(b, 3)

                    act.preload_act_table_set("gelu_and_others")
                    hidden(0, 0)
                    hidden(0, 1)
                    output(0, 0)
                    output(0, 1)
                    squares(0)
                    inverse_root(0)
                    copy_qk(0)
                    copy_scores(0, 0)
                    copy_scores(0, 1)
                    iterations(act, body)
                    act_squares(act, 0, EARLY)
                    act_copy_turned(act, 0, 8)
                    copy_turned(B - 1, 2)
                    copy_turned(B - 1, 3)
                    copy_sums(B - 1)
                    copy_product(B - 1)
                    act_squares(act, EARLY, NTT)
                    act_copy_turned(act, 8, NTT)

                @block.vector
                def _(dve):
                    def top(b, p, between=None):
                        n, r = 4 * b + p, p
                        step = OPS * n
                        for rnd in range(TOPK // 8):
                            if rnd == 2 and between:
                                between()
                            for i in range(NT):
                                if rnd:
                                    wait_alone(dve, d_top, step + 6 * rnd - 3 + i + 1)
                                else:
                                    wait(dve, p_nb, 3 * (n - NP) + i + 1)
                                    wait_alone(dve, c_sa if i < 2 else c_sb, n + 1)
                                dve.max(m8[:, r, i, rnd, :], (rest if rnd else s_sb)[:, r, i, :]).then_inc(d_top, 1)
                            for i in range(NT):
                                if not rnd:
                                    wait(dve, p_prob, 3 * (n - NP) + i + 1)
                                wait_alone(dve, d_top, step + 6 * rnd + i + 1)
                                dve.match_replace(rest[:, r, i, :], m8[:, r, i, rnd, :],
                                                  (rest if rnd else s_sb)[:, r, i, :], NEG).then_inc(d_top, 1)

                    def mask(b, p, nd=ND):
                        n = 4 * b + p
                        dve.wait_ge(c_e, 3 * n + 3)
                        dve.reciprocal(rz[:, p, :], zsum[:, p, :]).then_inc(d_rz, 1)
                        for i in range(nd):
                            dve.wait_ge(d_rz, n + 1)
                            dve.wait_ge(d_top, OPS * n + 21 + i + 1)
                            dve.tensor_scalar(keep[:, p, i, :], rest[:, p, i, :], NEG, rz[:, p, i:i + 1],
                                              ALU.is_equal, ALU.mult).then_inc(d_keep, 1)

                    def body(b, prev, nxt):
                        top(b, 0, (lambda: mask(b - 1, 3)) if prev else None)
                        top(b, 1, lambda: mask(b, 0))
                        top(b, 2, lambda: mask(b, 1))
                        top(b, 3, lambda: mask(b, 2))

                    dve.wait_ge(s_cwr, 1)
                    dve.tensor_copy(cw[:, P:CW], out_ps[:, 0:NE]).then_inc(s_cw, 1)
                    iterations(dve, body)
                    mask(B - 1, 3, NT)

                @block.gpsimd
                def _(pool):
                    def bias(b, p):
                        n, r = 4 * b + p, p
                        for i in range(NT):
                            wait(pool, c_e, 3 * (n - NP) + i + 1)
                            wait_alone(pool, d_top, OPS * n + i + 1)
                            pool.tensor_scalar(nbias[:, r, i:i + 1], m8[:, r, i, 0, 0:1], -SCALE, None, ALU.mult)\
                                .then_inc(p_nb, 1)

                    def kept(b, p, parts=range(NT), nd=ND):
                        n, r = 4 * b + p, p
                        for i in parts:
                            if i >= nd:
                                wait_alone(pool, d_top, OPS * n + 21 + i + 1)
                                wait_alone(pool, d_rz, n + 1)
                                pool.tensor_scalar(keep[:, r, i, :], rest[:, r, i, :], NEG, rz[:, r, i:i + 1],
                                                   ALU.is_equal, ALU.mult).then_inc(p_keep, 1)
                            if p < NP - 1:
                                wait(pool, s_tpb, n - NP + 1)
                            if i < nd:
                                pool.wait_ge(d_keep, ND * n + i + 1)
                            else:
                                wait_alone(pool, p_keep, (NT - ND) * n + i - ND + 1)
                            pool.tensor_tensor(prob[:, r, i, :], keep[:, r, i, :], ex[:, r, i, :], ALU.mult)\
                                .then_inc(p_prob, 1)

                    def combine(b, k):
                        if k == 0:
                            wait(pool, p_weo, 2 * b)
                            pool.tensor_copy(gcur[:, :], gates[:, 2 * b:2 * b + 2] if isinstance(b, int)
                                             else gates[:, bass.ds(2 * b, 2)]).then_inc(p_g, 1)
                            wait_alone(pool, p_g, b + 1)
                        wait(pool, p_h2, 2 * b + k - 1)
                        wait_alone(pool, c_eo, 2 * b + k + 1)
                        pool.tensor_scalar(weo[:, k, :], eo[:, k, :], gcur[:, k:k + 1], None, ALU.mult)\
                            .then_inc(p_weo, 1)
                        if k:
                            wait(pool, p_h2, 2 * b + 1)
                        wait_alone(pool, p_weo, 2 * b + k + 1)
                        pool.tensor_tensor(h_res2[:, cols(b)], weo[:, k, :], (h_res2 if k else h_res)[:, cols(b)],
                                           ALU.add).then_inc(p_h2, 1)

                    def residual(b):
                        wait_alone(pool, c_pr, b + 1)
                        pool.tensor_tensor(h_res3[:, cols(b)], pr[:, :], h_res2[:, cols(b)], ALU.add).then_inc(p_h3, 1)

                    def norm(b):
                        wait(pool, s_v, b)
                        pool.wait_ge(c_rstd, b + 1)
                        pool.tensor_tensor(xn[:, :], xc[:, :], rstd[:, :], ALU.mult).then_inc(p_xn, 1)

                    def body(b, prev, nxt):
                        bias(b, 0)
                        if prev:
                            kept(b - 1, 3)
                        bias(b, 1)
                        if nxt:
                            combine(b + 1, 0)
                        kept(b, 0, (0, 1))
                        if nxt:
                            combine(b + 1, 1)
                        kept(b, 0, (2,))
                        bias(b, 2)
                        if nxt:
                            norm(b + 1)
                        kept(b, 1)
                        if prev:
                            residual(b - 1)
                        bias(b, 3)
                        kept(b, 2)

                    pool.tensor_copy(cw[:, 0:P], center).then_inc(s_cw, 1)
                    pool.tensor_copy(xt[:, :, 2 * P], cst[:, K_TOKEN:K_TOKEN + NTT])
                    combine(0, 0)
                    combine(0, 1)
                    norm(0)
                    iterations(pool, body)
                    kept(B - 1, 3, nd=NT)
                    residual(B - 1)

        slot = sb("slot", [P, NTT], U32)
        bexp = sb("bexp", [1, NBLK], U32)
        s_slot, s_bexp, s_xt, s_put = (sem(n) for n in ("s_slot", "s_bexp", "s_xt", "s_put"))
        with ExitStack() as rst:
            def rb(name, shape, dt=F32):
                return rst.enter_context(nc.sbuf_tensor(name, shape, dt))

            def rsem(name):
                return ctx.enter_context(nc.semaphore("r_" + name))

            every = [P, NTT, NE]
            lnv = rb("lnv4", [P, NTT])
            rstd = rb("rstd4", [P, NTT])
            lgt = rb("lgt", every)
            mx = rb("mx", [P, NTT])
            hit = rb("hit", every)
            hit16 = rb("hit16", [P, NTT + 1, NE], BF16)
            tri16 = rb("tri16", [P, 2, P], BF16)
            over = rb("over", [P, NE, NTT])
            nblk = rb("nblk", [P, NE])
            base = rb("base", [P, NE])
            upto = rb("upto", [P, NE])
            pairs = rb("pairs", [P, NE, NE])
            place = rb("place", every)
            placef = rb("placef", [P, NTT])
            past = rb("past", [P, NBLK, NE])
            bexpf = rb("bexpf", [P, NBLK])
            rank_ps = bank[7]
            s_ln, s_std, s_ch, s_hit, s_tri, s_rank = (rsem(n) for n in ("ln", "std", "chain", "hit", "tri", "rank"))

            with nc.Block() as block:
                @block.gpsimd
                def _(pool):
                    pool.memset(hit16[:, :, :], 0.0)
                    pool.tensor_copy(tri16[:, :, :], cst[:, K_TRI:K_TRI + 2 * P].rearrange("p (a q) -> p a q", a=2))\
                        .then_inc(s_tri, 1)
                    pool.wait_ge(s_slot, 1)
                    pool.wait_ge(s_empty, 16)
                    for i in range(NTT):
                        pool.wait_ge(s_xt, i // TPB + 1)
                        pool.wait_ge(s_ht, i // 4 + 1)
                        pool.indirect_dma_start(scr_x, bass.IndirectOffsetOnAxis(ap=slot[:, i:i + 1], axis=0),
                                                xt[:, i, :], None).then_inc(s_put, 16)

                @block.tensor
                def _(pe):
                    pe.wait_ge(s_hit, 1)
                    pe.wait_ge(s_tri, 1)
                    last = pe.matmul(rank_ps[:, 0:(NTT + 1) * NE], tri16[:, 0, :], hit16[:, :, :], start=True,
                                     stop=False, skip_group_check=True)
                    for i in range(NTT):
                        last = pe.matmul(rank_ps[:, NE * (i + 1):NE * (NTT + 1)].rearrange("p (i e) -> p i e", e=NE),
                                         tri16[:, 1, :],
                                         hit16[:, i, :].unsqueeze(1).to_broadcast([P, NTT - i, NE]),
                                         start=False, stop=(i == NTT - 1), skip_group_check=True)
                    last.then_inc(s_rank, 1)

                @block.scalar
                def _(act):
                    act.wait_ge(s_sq4, NTT)
                    act.activation(lnv[:, :], ssum[:, :], ACT.Ln, scale=1.0 / P, bias=epsc[:, 0:1]).then_inc(s_ln, 1)
                    act.wait_ge(s_ln, 1)
                    act.activation(rstd[:, :], lnv[:, :], ACT.Exp, scale=-0.5).then_inc(s_std, 1)

                @block.vector
                def _(dve):
                    n = 0

                    def link(ins):
                        nonlocal n
                        n += 1
                        ins.then_inc(s_ch, 1)
                        dve.wait_ge(s_ch, n)

                    def in_bank(g, lo, hi):
                        return bank[g][:, 0:TPB * CW].rearrange("p (i f) -> p i f", f=CW)[:, :, lo:hi]

                    def normed(g):
                        tiles = slice(TPB * g, TPB * g + TPB)
                        dve.tensor_tensor(xt[:, tiles, 0:P], in_bank(g, 0, P),
                                          rstd[:, tiles].unsqueeze(2).to_broadcast([P, TPB, P]), ALU.mult)\
                           .then_inc(s_xt, 1)

                    dve.wait_ge(s_wr, 32)
                    dve.wait_ge(s_std, 1)
                    for g in range(NTT // TPB):
                        tiles = slice(TPB * g, TPB * g + TPB)
                        last = dve.tensor_tensor(lgt[:, tiles, :], in_bank(g, P, CW),
                                                 rstd[:, tiles].unsqueeze(2).to_broadcast([P, TPB, NE]), ALU.mult)
                    link(last)
                    link(dve.tensor_tensor(lgt[:, :, :], lgt[:, :, :],
                                           br_sb[:, :].unsqueeze(1).to_broadcast(every), ALU.add))
                    link(dve.tensor_reduce(mx[:, :], lgt[:, :, :], AX_X, ALU.max))
                    link(dve.tensor_tensor(hit[:, :, :], lgt[:, :, :], mx[:, :].unsqueeze(2).to_broadcast(every),
                                           ALU.is_ge))
                    link(dve.tensor_tensor(hit[:, :, :], hit[:, :, :],
                                           cst[:, K_DESC:K_DESC + NE].unsqueeze(1).to_broadcast(every), ALU.mult))
                    link(dve.tensor_reduce(mx[:, :], hit[:, :, :], AX_X, ALU.max))
                    dve.wait_ge(s_tri, 1)
                    dve.tensor_tensor(hit16[:, 0:NTT, :], hit[:, :, :], mx[:, :].unsqueeze(2).to_broadcast(every),
                                      ALU.is_equal).then_inc(s_hit, 1)
                    dve.wait_ge(s_hit, 1)
                    normed(0)
                    dve.wait_ge(s_rank, 1)
                    link(dve.tensor_tensor(over[:, :, :], rank_ps[:, NTT * NE:(NTT + 1) * NE].unsqueeze(2)
                                           .to_broadcast([P, NE, NTT]),
                                           cst[:, K_MULT:K_MULT + NTT].unsqueeze(1).to_broadcast([P, NE, NTT]),
                                           ALU.is_gt))
                    link(dve.tensor_reduce(nblk[:, :], over[:, :, :], AX_X, ALU.add))
                    link(dve.tensor_tensor(pairs[:, :, :], nblk[:, :].unsqueeze(1).to_broadcast([P, NE, NE]),
                                           cst[:, K_BEFORE:K_BEFORE + NE * NE].rearrange("p (e f) -> p e f", e=NE),
                                           ALU.mult))
                    link(dve.tensor_reduce(base[:, :], pairs[:, :, :], AX_X, ALU.add))
                    link(dve.tensor_tensor(place[:, :, :], rank_ps[:, 0:NTT * NE].rearrange("p (i e) -> p i e", e=NE),
                                           base[:, :].unsqueeze(1).to_broadcast(every), ALU.add))
                    link(dve.tensor_tensor(place[:, :, :], place[:, :, :], hit16[:, 0:NTT, :], ALU.mult))
                    link(dve.tensor_reduce(placef[:, :], place[:, :, :], AX_X, ALU.add))
                    dve.tensor_copy(slot[:, :], placef[:, :]).then_inc(s_slot, 1)
                    for g in range(1, NTT // TPB):
                        normed(g)
                    link(dve.tensor_tensor(pairs[:, :, :], nblk[:, :].unsqueeze(1).to_broadcast([P, NE, NE]),
                                           cst[:, K_UPTO:K_UPTO + NE * NE].rearrange("p (e f) -> p e f", e=NE),
                                           ALU.mult))
                    link(dve.tensor_reduce(upto[:, :], pairs[:, :, :], AX_X, ALU.add))
                    link(dve.tensor_tensor(past[:, :, :],
                                           cst[:, K_BLOCK:K_BLOCK + NBLK].unsqueeze(2).to_broadcast([P, NBLK, NE]),
                                           upto[:, :].unsqueeze(1).to_broadcast([P, NBLK, NE]), ALU.is_ge))
                    link(dve.tensor_reduce(bexpf[:, :], past[:, :, :], AX_X, ALU.add))
                    dve.tensor_scalar(bexp[:, :], bexpf[0:1, :], float(NE - 1), None, ALU.min).then_inc(s_bexp, 1)

        with ExitStack() as fst:
            def fb(name, shape, dt=F32):
                return fst.enter_context(nc.sbuf_tensor(name, shape, dt))

            def fsem(name):
                return ctx.enter_context(nc.semaphore("f_" + name))

            R = 3
            xs = fb("xs", [P, R, XR])
            hs = fb("hs", [P, R, XR - P])
            xf = fb("xf", [P, R, P])
            w1c = fb("w1c", [P, R, W1W])
            hid = fb("hid4", [P, R, NJ, P])
            ys = fb("ys", [P, R, P])
            tok = fb("tok", [P, R], U32)
            h_ps, y_ps, x_ps = bank[0:3], bank[3:6], bank[6]
            s_ld = [fsem(f"loaded{r}") for r in range(R)]
            s_st = [fsem(f"stored{r}") for r in range(R)]
            c_hs = fsem("residual")
            s_turn, s_h, s_y, c_relu, d_w, d_x, d_y = (fsem(n) for n in (
                "turned", "hidden_ps", "y_ps", "relu", "weights", "x", "y"))

            def wait(eng, s, value):
                if not isinstance(value, int) or value > 0:
                    eng.wait_ge(s, value)

            def wait_alone(eng, s, value):
                if not isinstance(value, int) or value > 0:
                    eng.wait_ge(s, value)
                    eng.nop(nofuse=True)

            ROUNDS = (NBLK - 1) // R

            def number(g, j):
                return R * g + (1 + j) if not isinstance(g, int) else 1 + R * g + j

            def uses(g, j):
                return g + 1 if j == R - 1 else g

            def back(g, j, n):
                return (g, j - n) if j >= n else (g - 1, j - n + R)

            def after(g, j):
                return (g, j + 1) if j < R - 1 else (g + 1, 0)

            def blocks(eng, step):
                step(-1, R - 1)
                for j in range(R):
                    step(0, j)
                with eng.Fori(0, (ROUNDS - 2) // 2) as twice:
                    for i in range(2):
                        for j in range(R):
                            step(twice * 2 + (1 + i), j)
                for j in range(R):
                    step(ROUNDS - 1, j)

            def rows(k):
                return slice(k * P, (k + 1) * P) if isinstance(k, int) else bass.ds(k * P, P)

            def expert_of(eng, k):
                return eng.value_load(bexp[0:1, k:k + 1] if isinstance(k, int) else bexp[0:1, bass.ds(k, 1)],
                                      min_val=0, max_val=NE - 1)

            with nc.Block() as block:
                @block.gpsimd
                def _(pool):
                    def step(g, r):
                        wait_alone(pool, d_y, number(g, r) + 1)
                        pool.indirect_dma_start(out, bass.IndirectOffsetOnAxis(ap=tok[:, r:r + 1], axis=0),
                                                ys[:, r, :], None).then_inc(s_st[r], 16)

                    blocks(pool, step)
                    for r in range(R):
                        pool.wait_ge(s_st[r], 16 * (ROUNDS + int(r == R - 1)))

                @block.sync
                def _(sp):
                    sp.wait_ge(s_put, 16 * NTT)

                    def step(g, r):
                        k = number(g, r)
                        wait(sp, s_turn, k - R + 1)
                        wait(sp, c_hs, k - R + 1)
                        sp.dma_start(xs[:, r, :], scr_x[rows(k), :]).then_inc(s_ld[r], 16)

                    blocks(sp, step)

                @block.tensor
                def _(pe):
                    def turn(g, r):
                        wait_alone(pe, s_ld[r], 16 * (uses(g, r) + 1))
                        pe.transpose(x_ps[:, 0:P], xs[:, r, 0:P], ident).then_inc(s_turn, 1)

                    def hidden(g, r):
                        k = number(g, r)
                        wait_alone(pe, d_x, k + 1)
                        for j in range(NJ):
                            last = pe.matmul(h_ps[r][:, j * P:(j + 1) * P], w1c[:, r, j * P:(j + 1) * P], xf[:, r, :],
                                             start=True, stop=True)
                        last.then_inc(s_h, 1)

                    def output(g, r, e):
                        k = number(g, r)
                        wait_alone(pe, c_relu, k + 1)
                        for j in range(NJ):
                            pe.matmul(y_ps[r][:, 0:P], hid[:, r, j, :],
                                      xw[:, bass.ds(e, 1), W1W + j * P:W1W + (j + 1) * P].rearrange("p e f -> p (e f)"),
                                      start=(j == 0), stop=False)
                        pe.matmul(y_ps[r][:, 0:P], ones_p[:, :], b2_parts[:, bass.ds(e * P, P)],
                                  start=False, stop=True).then_inc(s_y, 1)

                    def step(g, r):
                        k = number(g, r)
                        if not isinstance(k, int) or k > 0:
                            e = expert_of(pe, k - 1)
                        hidden(g, r)
                        if not isinstance(k, int) or k < NBLK - 1:
                            turn(*after(g, r))
                        if not isinstance(k, int) or k > 0:
                            output(*back(g, r, 1), e)

                    pe.wait_ge(s_xw, 16)
                    pe.wait_ge(s_bexp, 1)
                    turn(-1, R - 1)
                    blocks(pe, step)
                    output(ROUNDS - 1, R - 1, expert_of(pe, NBLK - 1))

                @block.scalar
                def _(act):
                    def step(g, r):
                        k = number(g, r)
                        wait(act, d_y, k - R + 1)
                        act.wait_ge(s_ld[r], 16 * (uses(g, r) + 1))
                        act.activation(hs[:, r, :], xs[:, r, P:XR], ACT.Copy).then_inc(c_hs, 1)
                        wait(act, s_y, k - R + 1)
                        act.wait_ge(s_h, k + 1)
                        for j in range(NJ):
                            ins = act.activation(hid[:, r, j, :], h_ps[r][:, j * P:(j + 1) * P], ACT.Relu,
                                                 bias=w1c[:, r, HID + j:HID + j + 1])
                        ins.then_inc(c_relu, 1)

                    blocks(act, step)

                @block.vector
                def _(dve):
                    def weights(g, r):
                        k = number(g, r)
                        e = expert_of(dve, k)
                        wait_alone(dve, c_relu, k - R + 1)
                        dve.tensor_copy(w1c[:, r, :],
                                        xw[:, bass.ds(e, 1), 0:W1W].rearrange("p e f -> p (e f)")).then_inc(d_w, 1)

                    def turned(g, r):
                        k = number(g, r)
                        dve.wait_ge(s_turn, k + 1)
                        dve.tensor_copy(xf[:, r, :], x_ps[:, 0:P]).then_inc(d_x, 1)

                    def result(g, r):
                        k = number(g, r)
                        wait(dve, s_st[r], 16 * uses(g, r))
                        dve.wait_ge(c_hs, k + 1)
                        dve.tensor_copy(tok[:, r:r + 1], hs[:, r, P:P + 1])
                        dve.wait_ge(s_y, k + 1)
                        dve.tensor_tensor(ys[:, r, :], y_ps[r][:, 0:P], hs[:, r, 0:P], ALU.add).then_inc(d_y, 1)

                    def step(g, r):
                        k = number(g, r)
                        turned(g, r)
                        if not isinstance(k, int) or k < NBLK - 1:
                            weights(*after(g, r))
                        if not isinstance(k, int) or k > 1:
                            result(*back(g, r, 2))

                    dve.wait_ge(s_xw, 16)
                    dve.wait_ge(s_bexp, 1)
                    weights(-1, R - 1)
                    blocks(dve, step)
                    result(ROUNDS - 1, R - 2)
                    result(ROUNDS - 1, R - 1)


def layouts(a):
    f = {k: np.asarray(v) for k, v in a.items()}
    side = T_IMG_SIDE = P // PATCH
    d = {}
    d["xT"] = f["x"].reshape(B, side, PATCH, side, PATCH).transpose(2, 4, 1, 3, 0).reshape(PATCH * PATCH, NIMG)
    d["txtT"] = f["txt"].transpose(2, 1, 0).reshape(P, T_TXT * B)

    def halves(v):
        return v.reshape(KIN, P).T

    eo = [f[f"L0_tok_eps_out{w}"] for w in (1, 2)]
    d["noise"] = np.concatenate([np.broadcast_to(np.concatenate(eo), (P, 2 * P)),
                                 halves(f["L0_tok_eps_in1"]), halves(f["L0_tok_eps_in2"]),
                                 np.stack(eo, 1)], 1)
    d["cols"] = np.stack([f["L0_tok_W1_b"], f["L0_tok_W1_sb"], f["L0_tok_W2_b"], f["L0_tok_W2_sb"],
                          f["L0_tok_W3_b"], f["L0_ffn_attn_w"][:, 0], np.broadcast_to(f["L0_ffn_attn_b"], (P,))], 1)
    d["tokw"] = np.stack([f["L0_tok_" + n].T.reshape(KIN, P, P).transpose(1, 0, 2)
                          for n in ("W1_w", "W1_sw", "W2_w", "W2_sw")], 1)
    d["w3T"] = f["L0_tok_W3_w"].T
    d["wihT"] = f["L0_attn_W_ih"].T
    d["whhT"] = f["L0_attn_W_hh"].T
    d["bias3"] = np.broadcast_to(np.stack([f["L0_attn_b_ih"], f["L0_attn_b_hh"]]), (3, 2, 4 * P))
    pos = np.arange(T_IMG, dtype=np.float32)[:, None]
    div = np.exp(np.arange(0, P, 2, dtype=np.float32) * np.float32(-np.log(10000.0) / P))
    ang = (pos * div).astype(np.float32)
    pe = np.stack([np.sin(ang), np.cos(ang)], -1).reshape(T_IMG, P).astype(np.float32)
    eye = np.eye(P, dtype=np.float32)
    avg = np.full((P, P), 1.0 / P, np.float32)
    desc = np.broadcast_to(NE - np.arange(NE, dtype=np.float32), (P, NE))
    expert = np.arange(NE)
    before = P * (expert[None, :] < expert[:, None])
    upto = expert[None, :] <= expert[:, None]
    rows = [np.broadcast_to(v.reshape(-1).astype(np.float32), (P, v.size))
            for v in (P * np.arange(NTT), before, upto, np.arange(NBLK))]
    lane = np.arange(P)[:, None]
    rows += [(N + P * np.arange(NBLK) + lane).astype(np.float32), (P * np.arange(NTT) + lane).astype(np.float32)]
    earlier = np.triu(np.ones((P, P), np.float32), 1)
    d["consts"] = np.concatenate([eye, eye - avg, avg, pe.T, desc, earlier, np.ones((P, P), np.float32)] + rows, 1)
    d["gate_w"] = f["L0_ffn_gate_w"]
    d["gate_b"] = np.broadcast_to(f["L0_ffn_gate_b"], (B, NE))

    def expert_rows(w1, b1, w2, b2):
        return np.concatenate([w1, b1.reshape(NE, NJ, P).transpose(0, 2, 1),
                               w2.reshape(NE, NJ, P, P).transpose(0, 2, 1, 3).reshape(NE, P, HID), b2[:, :, None]], 2)

    d["expert0"] = expert_rows(f["L0_ffn_w1"], f["L0_ffn_b1"], f["L0_ffn_w2"], f["L0_ffn_b2"])
    w = f["L1_attn_W_qkv"].reshape(HEADS, 3, HD, P).transpose(3, 1, 0, 2)
    d["wqkvT"] = np.pad(w, ((0, 0), (0, 0), (0, 0), (0, HPAD - HD))).reshape(P, 3, HEADS * HPAD)
    wo = f["L1_attn_W_o"].T.reshape(HEADS, HD, P)
    d["woT"] = np.pad(wo, ((0, 0), (0, HPAD - HD), (0, 0))).reshape(2, P, P).transpose(1, 0, 2)
    d["wr"] = f["L1_ffn_Wr"]
    d["br"] = np.broadcast_to(f["L1_ffn_br"], (P, NE))
    d["expert1"] = expert_rows(f["L1_ffn_W1"], f["L1_ffn_b1"], f["L1_ffn_W2"], f["L1_ffn_b2"])[:, :, :XW - 1].transpose(1, 0, 2)
    d["b2rows"] = np.broadcast_to(f["L1_ffn_b2"].reshape(-1), (3, NE * P))
    return {k: np.ascontiguousarray(v) for k, v in d.items()}


def kernel(**inputs):
    import concourse.bacc as bacc
    from concourse.bass_utils import run_bass_kernel_spmd

    nc = bacc.Bacc("TRN2", target_bir_lowering=False, num_devices=1)
    arrays = layouts(inputs)
    aps = {n: nc.dram_tensor(n, v.shape, mybir.dt.from_np(v.dtype), kind="ExternalInput").ap()
           for n, v in arrays.items()}
    out = nc.dram_tensor("out", (N + NBLK * P, P), F32, kind="ExternalOutput").ap()
    build(nc, out=out, **aps)
    got = run_bass_kernel_spmd(nc, [arrays], core_ids=[0]).results[0]["out"]
    return got[:N].reshape(B, T, P)
```
